# Optimizing a Trainium2 kernel written in Bass

```python
import numpy as np
import jax
import jax.numpy as jnp

def _softmax(x, axis=-1):
    return jax.nn.softmax(x, axis=axis)

def _gelu(x):
    return jax.nn.gelu(x, approximate=True)

def _silu(x):
    return jax.nn.silu(x)

def _sigmoid(x):
    return jax.nn.sigmoid(x)

def _layernorm(x, axis=-1, eps=1e-05):
    m = jnp.mean(x, axis=axis, keepdims=True)
    v = jnp.var(x, axis=axis, keepdims=True)
    return (x - m) / jnp.sqrt(v + eps)

def _scatter_add(tgt, idx, src, axis=0):
    return tgt.at[idx].add(src)

def _segment_sum(src, seg, n):
    return jax.ops.segment_sum(src, seg, n)
kernel_name = 'mk_xattn_ffn_d4_seqx_r8_e87ed3'

def setup_inputs(seed: int=0):
    np.random.seed(seed)
    _w = jnp.asarray

    def _rec_inputs():
        import jax
        import jax.numpy as jnp
        _rk = jax.random.key(seed)
        x = -0.0002928 + 1 * jax.random.normal(jax.random.fold_in(_rk, 1), (8, 256, 128), jnp.float32)
        _lenS = 256 - jax.random.randint(jax.random.fold_in(_rk, 7), (8,), 0, max(1, 256 // 4) + 1, jnp.int32)
        _lenS2 = 256 - jax.random.randint(jax.random.fold_in(_rk, 8), (8,), 0, max(1, 256 // 4) + 1, jnp.int32)
        _ctx_1024P = jax.random.normal(jax.random.fold_in(_rk, 11), (8, 16, 128), jnp.float32)
        _ctx_1024c = jax.random.dirichlet(jax.random.fold_in(_rk, 511), 0.3 * jnp.ones((16,), jnp.float32), (8, 256))
        _ctx_1024t = jnp.einsum('bsk,bkd->bsd', _ctx_1024c, _ctx_1024P)
        _ctx_1024t = _ctx_1024t * jax.lax.rsqrt(jnp.mean(jnp.square(_ctx_1024t)) + 1e-12) * 0.953939
        ctx_1024 = -1.39393e-06 + 0.999914 * (_ctx_1024t + 0.3 * jax.random.normal(jax.random.fold_in(_rk, 611), (8, 256, 128), jnp.float32))
        _validS = jnp.arange(256)[None, :] < _lenS[:, None]
        _validS2 = jnp.arange(256)[None, :] < _lenS2[:, None]
        _causal = jnp.tril(jnp.ones((256, 256), dtype=bool))
        mask_BxS_bf1 = jnp.ones((8, 256), dtype=bool)
        mask_BxS_ik0 = jnp.where(jnp.broadcast_to(_validS[:, :], (8, 256)), 0, 1).astype(jnp.int32)
        mask_BxSxS2_ff0 = jnp.where(jnp.ones((8, 256, 256), dtype=bool), 0.0, -1000000000.0).astype(jnp.float32)
        return (x, ctx_1024, mask_BxS_bf1, mask_BxS_ik0, mask_BxSxS2_ff0)
    x, ctx_1024, mask_BxS_bf1, mask_BxS_ik0, mask_BxSxS2_ff0 = _rec_inputs()

    def _L0_xattn_setup():
        import jax, jax.numpy as jnp
        import numpy as np
        NUM_HEADS = 16
        TOKEN_DIM = 128
        D_HEAD = TOKEN_DIM // NUM_HEADS

        def masked_softmax(scores, mask):
            scores = jnp.clip(scores, -50.0, 50.0)
            exp_scores = jnp.exp(scores)
            if mask is not None:
                exp_scores = jnp.where(mask, exp_scores, 0.0)
            denom = jnp.sum(exp_scores, axis=-1, keepdims=True)
            denom = jnp.where(denom <= 0.0, 1.0, denom)
            return exp_scores / denom
        key = jax.random.key(seed)
        ks = jax.random.split(key, 8)
        B, Sq, Sk = (2, 256, 256)
        scale = 1.0 / np.sqrt(TOKEN_DIM)
        return {'Q': jax.random.normal(ks[0], (B, Sq, TOKEN_DIM), dtype=jnp.float32), 'K': jax.random.normal(ks[1], (B, Sk, TOKEN_DIM), dtype=jnp.float32), 'V': jax.random.normal(ks[2], (B, Sk, TOKEN_DIM), dtype=jnp.float32), 'mask': jnp.ones((B, Sq), dtype=bool), 'W_q': jax.random.normal(ks[3], (TOKEN_DIM, TOKEN_DIM), dtype=jnp.float32) * scale, 'W_k': jax.random.normal(ks[4], (TOKEN_DIM, TOKEN_DIM), dtype=jnp.float32) * scale, 'W_v': jax.random.normal(ks[5], (TOKEN_DIM, TOKEN_DIM), dtype=jnp.float32) * scale, 'W_o': jax.random.normal(ks[6], (TOKEN_DIM, TOKEN_DIM), dtype=jnp.float32) * scale}
    _L0_xattn_all = _L0_xattn_setup()
    _L0_xattn_in = {k: v for k, v in _L0_xattn_all.items() if k in ('W_q', 'W_k', 'W_v', 'W_o')}
    del _L0_xattn_all

    def _L0_ffn_setup():
        import jax, jax.numpy as jnp
        import numpy as np
        EPS = 1e-05

        def rmsnorm(x):
            var = jnp.mean(jnp.square(x), axis=-1, keepdims=True)
            return x * jax.lax.rsqrt(var + 1e-06)

        def activation_quant(x):
            scale = 127.0 / jnp.clip(jnp.max(jnp.abs(x), axis=-1, keepdims=True), EPS, None)
            return jnp.clip(jnp.round(x * scale), -128, 127) / scale

        def weight_quant(w):
            scale = 1.0 / jnp.clip(jnp.mean(jnp.abs(w)), EPS, None)
            return jnp.clip(jnp.round(w * scale), -1, 1) / scale

        def bitlinear(x, w, b):
            xn = rmsnorm(x)
            xq = xn + jax.lax.stop_gradient(activation_quant(xn) - xn)
            wq = w + jax.lax.stop_gradient(weight_quant(w) - w)
            return jnp.einsum('bsi,oi->bso', xq, wq) + b
        key = jax.random.key(seed)
        k1, k2, k3 = jax.random.split(key, 3)
        B, S, D, H = (4, 256, 128, 512)
        x = jax.random.normal(k1, (B, S, D), dtype=jnp.float32)
        w1 = jax.random.normal(k2, (H, D), dtype=jnp.float32) * D ** (-0.5)
        b1 = jnp.zeros((H,), dtype=jnp.float32)
        w2 = jax.random.normal(k3, (D, H), dtype=jnp.float32) * H ** (-0.5)
        b2 = jnp.zeros((D,), dtype=jnp.float32)
        return {'x': x, 'w1': w1, 'b1': b1, 'w2': w2, 'b2': b2}
    _L0_ffn_all = _L0_ffn_setup()
    _L0_ffn_in = {k: v for k, v in _L0_ffn_all.items() if k in ('w1', 'b1', 'w2', 'b2')}
    del _L0_ffn_all

    def _L1_xattn_setup():
        import jax, jax.numpy as jnp
        import numpy as np
        B, S, P, D, H = (2, 512, 128, 128, 16)
        key = jax.random.key(seed)
        ks = jax.random.split(key, 8)
        init = 0.02
        queries = jax.random.normal(ks[0], (B, S, D), dtype=jnp.float32)
        patch_representations = jax.random.normal(ks[1], (B, P, D), dtype=jnp.float32)
        patch_boundaries = jax.random.randint(ks[2], (B, S), 0, 2, dtype=jnp.int32)
        wq = jax.random.normal(ks[3], (D, D), dtype=jnp.float32) * init
        wk = jax.random.normal(ks[4], (D, D), dtype=jnp.float32) * init
        wv = jax.random.normal(ks[5], (D, D), dtype=jnp.float32) * init
        wo = jax.random.normal(ks[6], (D, D), dtype=jnp.float32) * init
        bq = jnp.zeros((D,), jnp.float32)
        bk = jnp.zeros((D,), jnp.float32)
        bv = jnp.zeros((D,), jnp.float32)
        bo = jnp.zeros((D,), jnp.float32)
        return {'queries': queries, 'patch_representations': patch_representations, 'patch_boundaries': patch_boundaries, 'wq': wq, 'wk': wk, 'wv': wv, 'wo': wo, 'bq': bq, 'bk': bk, 'bv': bv, 'bo': bo}
    _L1_xattn_all = _L1_xattn_setup()
    _L1_xattn_in = {k: v for k, v in _L1_xattn_all.items() if k in ('wq', 'wk', 'wv', 'wo', 'bq', 'bk', 'bv', 'bo')}
    del _L1_xattn_all

    def _L1_ffn_setup():
        import jax, jax.numpy as jnp
        import numpy as np
        D_MODEL = 128
        D_FF = 352
        N_EXPERTS = 8
        key = jax.random.key(seed)
        k_in, k1, k2, k3 = jax.random.split(key, 4)
        scale = 0.02
        inputs = jax.random.normal(k_in, (4, N_EXPERTS * 256, D_MODEL), dtype=jnp.float32)
        w1 = jax.random.normal(k1, (N_EXPERTS, D_MODEL, D_FF), dtype=jnp.float32) * scale
        w3 = jax.random.normal(k3, (N_EXPERTS, D_MODEL, D_FF), dtype=jnp.float32) * scale
        w2 = jax.random.normal(k2, (N_EXPERTS, D_FF, D_MODEL), dtype=jnp.float32) * scale
        return {'inputs': inputs, 'w1': w1, 'w3': w3, 'w2': w2}
    _L1_ffn_all = _L1_ffn_setup()
    _L1_ffn_in = {k: v for k, v in _L1_ffn_all.items() if k in ('w1', 'w3', 'w2')}
    del _L1_ffn_all

    def _L2_xattn_setup():
        import jax, jax.numpy as jnp
        import numpy as np
        DIM = 128
        CTX_DIM = 128
        HEADS = 16
        DIM_HEAD = 64
        INNER = HEADS * DIM_HEAD
        FF_INNER = 4 * DIM
        EPS = 1e-05

        def layer_norm(x, g, b):
            mu = jnp.mean(x, axis=-1, keepdims=True)
            var = jnp.var(x, axis=-1, keepdims=True)
            return (x - mu) * jax.lax.rsqrt(var + EPS) * g + b
        key = jax.random.key(seed)
        ks = jax.random.split(key, 10)
        b, n, j = (2, 256, 256)
        x = jax.random.normal(ks[0], (b, n, DIM), dtype=jnp.float32)
        context = jax.random.normal(ks[1], (b, j, CTX_DIM), dtype=jnp.float32)
        mask = jnp.zeros((b, n, j), dtype=jnp.float32)
        s = 0.02
        Wq = jax.random.normal(ks[2], (DIM, INNER), dtype=jnp.float32) * s
        Wkv = jax.random.normal(ks[3], (CTX_DIM, 2 * DIM_HEAD), dtype=jnp.float32) * s
        Wout = jax.random.normal(ks[4], (INNER, DIM), dtype=jnp.float32) * s
        W1 = jax.random.normal(ks[5], (DIM, 2 * FF_INNER), dtype=jnp.float32) * s
        W2 = jax.random.normal(ks[6], (FF_INNER, DIM), dtype=jnp.float32) * s
        ln_g = jnp.ones((DIM,), jnp.float32)
        ln_b = jnp.zeros((DIM,), jnp.float32)
        cln_g = jnp.ones((CTX_DIM,), jnp.float32)
        cln_b = jnp.zeros((CTX_DIM,), jnp.float32)
        return {'x': x, 'context': context, 'mask': mask, 'ln_g': ln_g, 'ln_b': ln_b, 'cln_g': cln_g, 'cln_b': cln_b, 'Wq': Wq, 'Wkv': Wkv, 'Wout': Wout, 'W1': W1, 'W2': W2}
    _L2_xattn_all = _L2_xattn_setup()
    _L2_xattn_in = {k: v for k, v in _L2_xattn_all.items() if k in ('ln_g', 'ln_b', 'cln_g', 'cln_b', 'Wq', 'Wkv', 'Wout', 'W1', 'W2')}
    del _L2_xattn_all

    def _L2_ffn_setup():
        import jax, jax.numpy as jnp
        import numpy as np
        B, S, D, F, E = (8, 128, 128, 512, 8)
        EPS = 1e-05
        key = jax.random.key(seed)
        ks = jax.random.split(key, 4)
        s = 0.02
        return {'input_features': jax.random.normal(ks[0], (B, S, D), jnp.float32), 'centroids': jax.random.normal(ks[1], (E, D), jnp.float32) * 0.1, 'ln_g': jnp.ones((E, D), jnp.float32), 'ln_b': jnp.zeros((E, D), jnp.float32), 'w1': jax.random.normal(ks[2], (E, D, F), jnp.float32) * s, 'b1': jnp.zeros((E, F), jnp.float32), 'w2': jax.random.normal(ks[3], (E, F, D), jnp.float32) * s, 'b2': jnp.zeros((E, D), jnp.float32)}
    _L2_ffn_all = _L2_ffn_setup()
    _L2_ffn_in = {k: v for k, v in _L2_ffn_all.items() if k in ('centroids', 'ln_g', 'ln_b', 'w1', 'b1', 'w2', 'b2')}
    del _L2_ffn_all

    def _L3_xattn_setup():
        import jax, jax.numpy as jnp
        import numpy as np
        DIM = 128
        HEAD_NUM = 8
        D_HEAD = DIM // HEAD_NUM
        B, S = (4, 256)
        key = jax.random.key(seed)
        ks = jax.random.split(key, 7)
        scale = 0.02
        return {'Q': jax.random.normal(ks[0], (B, S, DIM), dtype=jnp.float32), 'K': jax.random.normal(ks[1], (B, S, DIM), dtype=jnp.float32), 'V': jax.random.normal(ks[2], (B, S, DIM), dtype=jnp.float32), 'W_Q': jax.random.normal(ks[3], (DIM, DIM), dtype=jnp.float32) * scale, 'W_K': jax.random.normal(ks[4], (DIM, DIM), dtype=jnp.float32) * scale, 'W_V': jax.random.normal(ks[5], (DIM, DIM), dtype=jnp.float32) * scale, 'W_O': jax.random.normal(ks[6], (DIM, DIM), dtype=jnp.float32) * scale}
    _L3_xattn_all = _L3_xattn_setup()
    _L3_xattn_in = {k: v for k, v in _L3_xattn_all.items() if k in ('W_Q', 'W_K', 'W_V', 'W_O')}
    del _L3_xattn_all

    def _L3_ffn_setup():
        import jax, jax.numpy as jnp
        import numpy as np
        H = 128
        I = 512
        E = 4
        LN_EPS = 1e-12

        def _layer_norm(x, gamma, beta, eps=LN_EPS):
            mu = jnp.mean(x, axis=-1, keepdims=True)
            var = jnp.mean(jnp.square(x - mu), axis=-1, keepdims=True)
            return (x - mu) * jax.lax.rsqrt(var + eps) * gamma + beta
        key = jax.random.key(seed)
        ks = jax.random.split(key, 8)
        B, S = (4, 64)
        scale = 0.02
        return {'hidden_states': jax.random.normal(ks[0], (B, S, H), jnp.float32), 'W_router': jax.random.normal(ks[1], (H, E), jnp.float32) * scale, 'W1': jax.random.normal(ks[2], (E, H, I), jnp.float32) * scale, 'b1': jax.random.normal(ks[3], (E, I), jnp.float32) * scale, 'Wo': jax.random.normal(ks[4], (I, H), jnp.float32) * scale, 'bo': jax.random.normal(ks[5], (H,), jnp.float32) * scale, 'ln_gamma': jnp.ones((H,), jnp.float32), 'ln_beta': jnp.zeros((H,), jnp.float32)}
    _L3_ffn_all = _L3_ffn_setup()
    _L3_ffn_in = {k: v for k, v in _L3_ffn_all.items() if k in ('W_router', 'W1', 'b1', 'Wo', 'bo', 'ln_gamma', 'ln_beta')}
    del _L3_ffn_all
    return {'x': x, 'ctx_1024': ctx_1024, 'mask_BxS_bf1': mask_BxS_bf1, 'mask_BxS_ik0': mask_BxS_ik0, 'mask_BxSxS2_ff0': mask_BxSxS2_ff0, 'L0_xattn_W_q': _L0_xattn_in['W_q'], 'L0_xattn_W_k': _L0_xattn_in['W_k'], 'L0_xattn_W_v': _L0_xattn_in['W_v'], 'L0_xattn_W_o': _L0_xattn_in['W_o'], 'L0_ffn_w1': _L0_ffn_in['w1'], 'L0_ffn_b1': _L0_ffn_in['b1'], 'L0_ffn_w2': _L0_ffn_in['w2'], 'L0_ffn_b2': _L0_ffn_in['b2'], 'L1_xattn_wq': _L1_xattn_in['wq'], 'L1_xattn_wk': _L1_xattn_in['wk'], 'L1_xattn_wv': _L1_xattn_in['wv'], 'L1_xattn_wo': _L1_xattn_in['wo'], 'L1_xattn_bq': _L1_xattn_in['bq'], 'L1_xattn_bk': _L1_xattn_in['bk'], 'L1_xattn_bv': _L1_xattn_in['bv'], 'L1_xattn_bo': _L1_xattn_in['bo'], 'L1_ffn_w1': _L1_ffn_in['w1'], 'L1_ffn_w3': _L1_ffn_in['w3'], 'L1_ffn_w2': _L1_ffn_in['w2'], 'L2_xattn_ln_g': _L2_xattn_in['ln_g'], 'L2_xattn_ln_b': _L2_xattn_in['ln_b'], 'L2_xattn_cln_g': _L2_xattn_in['cln_g'], 'L2_xattn_cln_b': _L2_xattn_in['cln_b'], 'L2_xattn_Wq': _L2_xattn_in['Wq'], 'L2_xattn_Wkv': _L2_xattn_in['Wkv'], 'L2_xattn_Wout': _L2_xattn_in['Wout'], 'L2_xattn_W1': _L2_xattn_in['W1'], 'L2_xattn_W2': _L2_xattn_in['W2'], 'L2_ffn_centroids': _L2_ffn_in['centroids'], 'L2_ffn_ln_g': _L2_ffn_in['ln_g'], 'L2_ffn_ln_b': _L2_ffn_in['ln_b'], 'L2_ffn_w1': _L2_ffn_in['w1'], 'L2_ffn_b1': _L2_ffn_in['b1'], 'L2_ffn_w2': _L2_ffn_in['w2'], 'L2_ffn_b2': _L2_ffn_in['b2'], 'L3_xattn_W_Q': _L3_xattn_in['W_Q'], 'L3_xattn_W_K': _L3_xattn_in['W_K'], 'L3_xattn_W_V': _L3_xattn_in['W_V'], 'L3_xattn_W_O': _L3_xattn_in['W_O'], 'L3_ffn_W_router': _L3_ffn_in['W_router'], 'L3_ffn_W1': _L3_ffn_in['W1'], 'L3_ffn_b1': _L3_ffn_in['b1'], 'L3_ffn_Wo': _L3_ffn_in['Wo'], 'L3_ffn_bo': _L3_ffn_in['bo'], 'L3_ffn_ln_gamma': _L3_ffn_in['ln_gamma'], 'L3_ffn_ln_beta': _L3_ffn_in['ln_beta']}

def reference(x, ctx_1024, mask_BxS_bf1, mask_BxS_ik0, mask_BxSxS2_ff0, L0_xattn_W_q, L0_xattn_W_k, L0_xattn_W_v, L0_xattn_W_o, L0_ffn_w1, L0_ffn_b1, L0_ffn_w2, L0_ffn_b2, L1_xattn_wq, L1_xattn_wk, L1_xattn_wv, L1_xattn_wo, L1_xattn_bq, L1_xattn_bk, L1_xattn_bv, L1_xattn_bo, L1_ffn_w1, L1_ffn_w3, L1_ffn_w2, L2_xattn_ln_g, L2_xattn_ln_b, L2_xattn_cln_g, L2_xattn_cln_b, L2_xattn_Wq, L2_xattn_Wkv, L2_xattn_Wout, L2_xattn_W1, L2_xattn_W2, L2_ffn_centroids, L2_ffn_ln_g, L2_ffn_ln_b, L2_ffn_w1, L2_ffn_b1, L2_ffn_w2, L2_ffn_b2, L3_xattn_W_Q, L3_xattn_W_K, L3_xattn_W_V, L3_xattn_W_O, L3_ffn_W_router, L3_ffn_W1, L3_ffn_b1, L3_ffn_Wo, L3_ffn_bo, L3_ffn_ln_gamma, L3_ffn_ln_beta):
    import jax
    import jax.numpy as jnp

    def _L0_xattn_ref(Q, K, V, mask, W_q, W_k, W_v, W_o):
        import jax, jax.numpy as jnp
        import numpy as np
        NUM_HEADS = 16
        TOKEN_DIM = 128
        D_HEAD = TOKEN_DIM // NUM_HEADS

        def masked_softmax(scores, mask):
            scores = jnp.clip(scores, -50.0, 50.0)
            exp_scores = jnp.exp(scores)
            if mask is not None:
                exp_scores = jnp.where(mask, exp_scores, 0.0)
            denom = jnp.sum(exp_scores, axis=-1, keepdims=True)
            denom = jnp.where(denom <= 0.0, 1.0, denom)
            return exp_scores / denom
        B = Q.shape[0]
        q = (Q @ W_q.T).reshape(B, -1, NUM_HEADS, D_HEAD).transpose(0, 2, 1, 3)
        k = (K @ W_k.T).reshape(B, -1, NUM_HEADS, D_HEAD).transpose(0, 2, 1, 3)
        v = (V @ W_v.T).reshape(B, -1, NUM_HEADS, D_HEAD).transpose(0, 2, 1, 3)
        scores = jnp.einsum('bhqd,bhkd->bhqk', q, k) / np.sqrt(D_HEAD)
        m = mask[:, None, :, None] if mask is not None else None
        attn = masked_softmax(scores, m)
        out = jnp.einsum('bhqk,bhkd->bhqd', attn, v)
        out = out.transpose(0, 2, 1, 3).reshape(B, -1, NUM_HEADS * D_HEAD)
        return out @ W_o.T

    def _L0_ffn_ref(x, w1, b1, w2, b2):
        import jax, jax.numpy as jnp
        import numpy as np
        EPS = 1e-05

        def rmsnorm(x):
            var = jnp.mean(jnp.square(x), axis=-1, keepdims=True)
            return x * jax.lax.rsqrt(var + 1e-06)

        def activation_quant(x):
            scale = 127.0 / jnp.clip(jnp.max(jnp.abs(x), axis=-1, keepdims=True), EPS, None)
            return jnp.clip(jnp.round(x * scale), -128, 127) / scale

        def weight_quant(w):
            scale = 1.0 / jnp.clip(jnp.mean(jnp.abs(w)), EPS, None)
            return jnp.clip(jnp.round(w * scale), -1, 1) / scale

        def bitlinear(x, w, b):
            xn = rmsnorm(x)
            xq = xn + jax.lax.stop_gradient(activation_quant(xn) - xn)
            wq = w + jax.lax.stop_gradient(weight_quant(w) - w)
            return jnp.einsum('bsi,oi->bso', xq, wq) + b
        h = bitlinear(x, w1, b1)
        h = jax.nn.gelu(h, approximate=False)
        return bitlinear(h, w2, b2)

    def _L1_xattn_ref(queries, patch_representations, patch_boundaries, wq, wk, wv, wo, bq, bk, bv, bo):
        import jax, jax.numpy as jnp
        import numpy as np
        B, S, P, D, H = (2, 512, 128, 128, 16)
        b, s, d = queries.shape
        p = patch_representations.shape[1]
        h = H
        dh = d // h
        scale = 1.0 / jnp.sqrt(jnp.asarray(dh, queries.dtype))
        q = (queries @ wq.T + bq).reshape(b, s, h, dh)
        k = (patch_representations @ wk.T + bk).reshape(b, p, h, dh)
        v = (patch_representations @ wv.T + bv).reshape(b, p, h, dh)
        scores = jnp.einsum('bqhd,bkhd->bhqk', q, k) * scale
        patch_idx = jnp.cumsum(patch_boundaries, axis=1)
        mask = jnp.arange(p)[None, None, :] > patch_idx[:, :, None]
        scores = jnp.where(mask[:, None, :, :], jnp.finfo(scores.dtype).min, scores)
        attn = jax.nn.softmax(scores, axis=-1)
        out = jnp.einsum('bhqk,bkhd->bqhd', attn, v).reshape(b, s, d)
        return out @ wo.T + bo

    def _L1_ffn_ref(inputs, w1, w3, w2):
        import jax, jax.numpy as jnp
        import numpy as np
        D_MODEL = 128
        D_FF = 352
        N_EXPERTS = 8
        B, T, D = inputs.shape
        E = w1.shape[0]
        C = T // E
        x = inputs.reshape(B, E, C, D)
        gate = jnp.einsum('becd,edf->becf', x, w1)
        up = jnp.einsum('becd,edf->becf', x, w3)
        h = jax.nn.silu(gate) * up
        out = jnp.einsum('becf,efd->becd', h, w2)
        return out.reshape(B, T, D)

    def _L2_xattn_ref(x, context, mask, ln_g, ln_b, cln_g, cln_b, Wq, Wkv, Wout, W1, W2):
        import jax, jax.numpy as jnp
        import numpy as np
        DIM = 128
        CTX_DIM = 128
        HEADS = 16
        DIM_HEAD = 64
        INNER = HEADS * DIM_HEAD
        FF_INNER = 4 * DIM
        EPS = 1e-05

        def layer_norm(x, g, b):
            mu = jnp.mean(x, axis=-1, keepdims=True)
            var = jnp.var(x, axis=-1, keepdims=True)
            return (x - mu) * jax.lax.rsqrt(var + EPS) * g + b
        scale = DIM_HEAD ** (-0.5)
        xn = layer_norm(x, ln_g, ln_b)
        cn = layer_norm(context, cln_g, cln_b)
        b, n, _ = xn.shape
        q = (xn @ Wq).reshape(b, n, HEADS, DIM_HEAD).transpose(0, 2, 1, 3) * scale
        kv = cn @ Wkv
        k, v = jnp.split(kv, 2, axis=-1)
        sim = jnp.einsum('bhid,bjd->bhij', q, k) + mask[:, None, :, :]
        attn = jax.nn.softmax(sim, axis=-1)
        out = jnp.einsum('bhij,bjd->bhid', attn, v)
        out = out.transpose(0, 2, 1, 3).reshape(b, n, INNER) @ Wout
        h = xn @ W1
        val, gate = jnp.split(h, 2, axis=-1)
        out = out + jax.nn.silu(gate) * val @ W2
        return out

    def _L2_ffn_ref(input_features, centroids, ln_g, ln_b, w1, b1, w2, b2):
        import jax, jax.numpy as jnp
        import numpy as np
        B, S, D, F, E = (8, 128, 128, 512, 8)
        EPS = 1e-05
        x = input_features.reshape(-1, D)
        aff = jax.lax.stop_gradient(x @ centroids.T)
        eid = jnp.argmax(aff, axis=-1)
        alpha = jax.nn.sigmoid(jnp.sum(x * centroids[eid], axis=-1, keepdims=True))
        mu = jnp.mean(x, axis=-1, keepdims=True)
        var = jnp.mean((x - mu) ** 2, axis=-1, keepdims=True)
        xn = (x - mu) * jax.lax.rsqrt(var + EPS)
        xln = xn * ln_g[eid] + ln_b[eid]
        onehot = jax.nn.one_hot(eid, E, dtype=x.dtype)
        ffn = jnp.zeros_like(x)
        for e in range(E):
            h = jax.nn.relu(xln @ w1[e] + b1[e])
            ffn = ffn + onehot[:, e:e + 1] * (h @ w2[e] + b2[e])
        out = x + alpha * ffn
        return out.reshape(input_features.shape)

    def _L3_xattn_ref(Q, K, V, W_Q, W_K, W_V, W_O):
        import jax, jax.numpy as jnp
        import numpy as np
        DIM = 128
        HEAD_NUM = 8
        D_HEAD = DIM // HEAD_NUM
        B, S = (4, 256)
        b, s, d = Q.shape
        h, dh = (HEAD_NUM, d // HEAD_NUM)

        def proj_split(x, W):
            y = jnp.einsum('bsd,ed->bse', x, W)
            return y.reshape(b, s, h, dh).transpose(0, 2, 1, 3)
        q = proj_split(Q, W_Q)
        k = proj_split(K, W_K)
        v = proj_split(V, W_V)
        scores = jnp.einsum('bhqd,bhkd->bhqk', q, k) / jnp.sqrt(jnp.float32(dh))
        attn = jax.nn.softmax(scores, axis=1)
        ctx = jnp.einsum('bhqk,bhkd->bhqd', attn, v)
        ctx = ctx.transpose(0, 2, 1, 3).reshape(b, s, d)
        return jnp.einsum('bsd,ed->bse', ctx, W_O)

    def _L3_ffn_ref(hidden_states, W_router, W1, b1, Wo, bo, ln_gamma, ln_beta):
        import jax, jax.numpy as jnp
        import numpy as np
        H = 128
        I = 512
        E = 4
        LN_EPS = 1e-12

        def _layer_norm(x, gamma, beta, eps=LN_EPS):
            mu = jnp.mean(x, axis=-1, keepdims=True)
            var = jnp.mean(jnp.square(x - mu), axis=-1, keepdims=True)
            return (x - mu) * jax.lax.rsqrt(var + eps) * gamma + beta
        B, S, _ = hidden_states.shape
        x = hidden_states.reshape(-1, H)
        logits = x @ W_router
        expert_idx = jnp.argmax(logits, axis=-1)
        h = jnp.einsum('th,ehi->tei', x, W1) + b1
        h = jax.nn.gelu(h, approximate=False)
        onehot = jax.nn.one_hot(expert_idx, E, dtype=x.dtype)
        intermediate = jnp.einsum('te,tei->ti', onehot, h)
        y = intermediate @ Wo + bo + x
        y = _layer_norm(y, ln_gamma, ln_beta)
        return y.reshape(B, S, H)
    x = x + _L0_xattn_ref(_layernorm(x, axis=-1), ctx_1024, ctx_1024, mask_BxS_bf1, L0_xattn_W_q, L0_xattn_W_k, L0_xattn_W_v, L0_xattn_W_o)
    x = x + _L0_ffn_ref(_layernorm(x, axis=-1), L0_ffn_w1, L0_ffn_b1, L0_ffn_w2, L0_ffn_b2)
    x = x + _L1_xattn_ref(_layernorm(x, axis=-1), ctx_1024, mask_BxS_ik0, L1_xattn_wq, L1_xattn_wk, L1_xattn_wv, L1_xattn_wo, L1_xattn_bq, L1_xattn_bk, L1_xattn_bv, L1_xattn_bo)
    x = x + _L1_ffn_ref(_layernorm(x, axis=-1), L1_ffn_w1, L1_ffn_w3, L1_ffn_w2)
    x = x + _L2_xattn_ref(_layernorm(x, axis=-1), ctx_1024, mask_BxSxS2_ff0, L2_xattn_ln_g, L2_xattn_ln_b, L2_xattn_cln_g, L2_xattn_cln_b, L2_xattn_Wq, L2_xattn_Wkv, L2_xattn_Wout, L2_xattn_W1, L2_xattn_W2)
    x = x + _L2_ffn_ref(_layernorm(x, axis=-1), L2_ffn_centroids, L2_ffn_ln_g, L2_ffn_ln_b, L2_ffn_w1, L2_ffn_b1, L2_ffn_w2, L2_ffn_b2)
    x = x + _L3_xattn_ref(_layernorm(x, axis=-1), ctx_1024, ctx_1024, L3_xattn_W_Q, L3_xattn_W_K, L3_xattn_W_V, L3_xattn_W_O)
    x = x + _L3_ffn_ref(_layernorm(x, axis=-1), L3_ffn_W_router, L3_ffn_W1, L3_ffn_b1, L3_ffn_Wo, L3_ffn_bo, L3_ffn_ln_gamma, L3_ffn_ln_beta)
    return x

_drawn_inputs = setup_inputs


def setup_inputs(seed=0):
    import zlib

    import numpy as np

    out = dict(_drawn_inputs(seed))
    spreads = {'L0_ffn_b1': (0.0, 0.1),
     'L0_ffn_b2': (0.0, 0.1),
     'L1_xattn_bq': (0.0, 2.0),
     'L1_xattn_bk': (0.0, 2.0),
     'L1_xattn_bv': (0.0, 0.612),
     'L1_xattn_bo': (0.0, 0.1),
     'L2_xattn_ln_g': (1.0, 0.6),
     'L2_xattn_ln_b': (0.0, 0.8),
     'L2_xattn_cln_g': (1.0, 0.6),
     'L2_xattn_cln_b': (0.0, 2.0),
     'L2_ffn_ln_g': (1.0, 0.6),
     'L2_ffn_ln_b': (0.0, 2.0),
     'L2_ffn_b1': (0.0, 2.0),
     'L2_ffn_b2': (0.0, 0.8),
     'L3_ffn_ln_gamma': (1.0, 0.6),
     'L3_ffn_ln_beta': (0.0, 1.203)}
    factors = {'L1_xattn_wq': 28.501,
     'L1_xattn_wk': 26.5,
     'L1_ffn_w1': 8.0,
     'L1_ffn_w3': 8.0,
     'L1_ffn_w2': 8.0,
     'L2_xattn_Wq': 64.0,
     'L2_xattn_W1': 6.033,
     'L2_xattn_W2': 6.028,
     'L2_ffn_w1': 9.716,
     'L3_xattn_W_Q': 5.876,
     'L3_xattn_W_K': 5.948,
     'L3_ffn_W_router': 4.436,
     'L3_ffn_W1': 3.849,
     'L3_ffn_b1': 54.261,
     'L3_ffn_Wo': 3.824,
     'L3_ffn_bo': 50.986,
     'L2_xattn_Wkv': 4.641,
     'L2_xattn_Wout': 4.915}
    for name, (base, spread) in spreads.items():
        noise = np.random.default_rng([zlib.crc32(name.encode()), seed]).standard_normal(out[name].shape)
        drawn = base * np.exp(spread * noise) if base else spread * noise
        out[name] = jnp.asarray(drawn.astype(out[name].dtype))
    for name, factor in factors.items():
        out[name] = (out[name] * factor).astype(out[name].dtype)
    return out
```

```python
from contextlib import ExitStack

import concourse.bass as bass
from concourse import mybir

F32 = mybir.dt.float32
BF16 = mybir.dt.bfloat16
ALU = mybir.AluOpType
ACT = mybir.ActivationFunctionType
AX = mybir.AxisListType

P = 128
D = 128
NB = 8
S = 256
QT = S // P
NT = NB * QT
LN_EPS = 1e-5
RMS_EPS = 1e-6
QUANT_EPS = 1e-5
ROUND = 1.5 * 2.0 ** 23
MASKED = -1e30
EXP_LOW, EXP_HIGH = 1.9287498479639178e-22, 5.184705528587072e21


class Shared:

    def __init__(self, nc, ctx, dram):
        self.dram = dram
        self.retired_ctx, self.retired = ExitStack(), []
        self.x_all = ctx.enter_context(nc.sbuf_tensor("x_all", [P, NT, D], F32))
        self.ctxT = ctx.enter_context(nc.sbuf_tensor("ctxT", [P, NB * S], F32))
        self.ident = ctx.enter_context(nc.sbuf_tensor("ident", [P, P], F32))
        self.ident_bf = ctx.enter_context(nc.sbuf_tensor("ident_bf", [P, P], BF16))
        self.tri = ctx.enter_context(nc.sbuf_tensor("tri", [P, P], F32))
        self.ones = ctx.enter_context(nc.sbuf_tensor("ones", [P, P], F32))
        self.half = ctx.enter_context(nc.sbuf_tensor("half", [P, 4], F32))
        self.head8 = ctx.enter_context(nc.sbuf_tensor("head8", [P, 16], F32))
        self.head16 = ctx.enter_context(nc.sbuf_tensor("head16", [P, 8], F32))
        self.key_index = ctx.enter_context(nc.sbuf_tensor("key_index", [P, S], F32))
        self.expert_index = ctx.enter_context(nc.sbuf_tensor("expert_index", [P, 8], F32))
        self.query_mask = ctx.enter_context(nc.sbuf_tensor("query_mask", [P, NT], F32))
        self.last_patch = ctx.enter_context(nc.sbuf_tensor("last_patch", [P, NT], F32))
        self.xnT_all = ctx.enter_context(nc.sbuf_tensor("xnT_all", [P, NB * S], F32))
        self.cnT_all = ctx.enter_context(nc.sbuf_tensor("cnT_all", [P, NB * S], F32))
        self.y_all = ctx.enter_context(nc.sbuf_tensor("y_all", [P, NT, D], F32))


class Phase:

    def __init__(self, nc, ctx, name):
        self.nc, self.ctx, self.name = nc, ctx, name
        self.sem_ctx, self.sems = ExitStack(), []

    def sbuf(self, name, shape, dtype=F32):
        return self.ctx.enter_context(self.nc.sbuf_tensor(f"{self.name}_{name}", shape, dtype, align_bytes=64))

    def psum(self, name, shape, dtype=F32):
        return self.ctx.enter_context(self.nc.psum_tensor(f"{self.name}_{name}", shape, dtype))

    def sem(self, name):
        s = self.sem_ctx.enter_context(self.nc.semaphore(f"{self.name}_{name}"))
        self.sems.append(s)
        return s

    def retire(self, sh):
        sh.retired_ctx.close()
        sh.retired_ctx, sh.retired = self.sem_ctx, self.sems


def clear_retired(pool, sh):
    for s in sh.retired:
        pool.sem_clear(s)


class Counter:

    def __init__(self, per_batch):
        self.per_batch, self.n = per_batch, 0

    def up(self):
        self.n += 1
        return 1

    def all(self, b):
        return self.per_batch * b + self.n

    def close(self):
        assert self.n == self.per_batch, (self.n, self.per_batch)


def dve_choose(dve, sh, logits, top, first, onehot, step, n, b):
    E = logits.shape[2]
    index = sh.expert_index[:, 0:E].unsqueeze(1).to_broadcast([P, QT, E])
    dve.tensor_reduce(top[:, :], logits, AX.X, ALU.max).then_inc(step, n.up())
    dve.wait_ge(step, n.all(b))
    dve.tensor_tensor(onehot[:, :, :], logits, top[:, :].unsqueeze(2).to_broadcast([P, QT, E]), ALU.is_lt).then_inc(step, n.up())
    dve.wait_ge(step, n.all(b))
    dve.tensor_scalar(onehot[:, :, :], onehot[:, :, :], 16.0, None, ALU.mult).then_inc(step, n.up())
    dve.wait_ge(step, n.all(b))
    dve.tensor_tensor(onehot[:, :, :], onehot[:, :, :], index, ALU.add).then_inc(step, n.up())
    dve.wait_ge(step, n.all(b))
    dve.tensor_reduce(first[:, :], onehot[:, :, :], AX.X, ALU.min).then_inc(step, n.up())
    dve.wait_ge(step, n.all(b))
    dve.tensor_tensor(onehot[:, :, :], index, first[:, :].unsqueeze(2).to_broadcast([P, QT, E]), ALU.is_equal).then_inc(step, n.up())
    dve.wait_ge(step, n.all(b))


def phase_setup(nc, sh):
    with ExitStack() as ctx:
        ph = Phase(nc, ctx, "setup")
        ctx_rows = ph.sbuf("ctx_rows", [P, NT, D])
        mask_u8 = ph.sbuf("mask_u8", [P, NT], mybir.dt.uint8)
        mask_i32 = ph.sbuf("mask_i32", [P, NT], mybir.dt.int32)
        steps = ph.sbuf("steps", [P, NT])
        turned = [ph.psum(f"turned{i}", [P, 4, P]) for i in range(2)]
        sums = ph.psum("sums", [P, 512])
        loaded = ph.sem("loaded")
        masks_loaded = ph.sem("masks_loaded")
        blank = ph.sem("blank")
        consts = ph.sem("consts")
        steps_ready = ph.sem("steps_ready")
        sums_done = ph.sem("sums_done")
        turned_done = ph.sem("turned_done")
        turned_copied = ph.sem("turned_copied")
        block = ctx.enter_context(nc.Block())

        @block.sync
        def _(sp):
            sp.dma_start(ctx_rows[:, :, :], sh.dram["ctx_1024"].rearrange("b (q p) d -> p (b q) d", p=P)).then_inc(loaded, 16)
            sp.dma_start(sh.x_all[:, :, :], sh.dram["x"].rearrange("b (q p) d -> p (b q) d", p=P)).then_inc(loaded, 16)
            with nc.allow_non_contiguous_dma(reason="mask columns"):
                sp.dma_start(mask_u8[:, :], sh.dram["mask_BxS_bf1"].rearrange("b (q p) -> p (b q)", p=P)).then_inc(masks_loaded, 16)
                sp.dma_start(mask_i32[:, :], sh.dram["mask_BxS_ik0"].rearrange("b (q p) -> p (b q)", p=P)).then_inc(masks_loaded, 16)

        @block.gpsimd
        def _(pool):
            clear_retired(pool, sh)
            pool.memset(sh.ident[:, :], 0.0).then_inc(blank, 1)
            pool.memset(sh.ones[:, :], 1.0).then_inc(blank, 1)
            pool.memset(sh.tri[:, :], 1.0).then_inc(blank, 1)
            pool.memset(sh.head8[:, :], 1.0).then_inc(blank, 1)
            pool.memset(sh.head16[:, :], 1.0).then_inc(blank, 1)
            pool.memset(sh.half[:, :], -0.5).then_inc(blank, 1)
            pool.wait_ge(blank, 6)
            pool.affine_select(out=sh.ident[:, :], in_=sh.ident[:, :], compare_op=ALU.not_equal, fill=1.0,
                               base=0, pattern=[[-1, P]], channel_multiplier=1).then_inc(consts, 1)
            pool.affine_select(out=sh.tri[:, :], in_=sh.tri[:, :], compare_op=ALU.is_ge, fill=0.0,
                               base=0, pattern=[[1, P]], channel_multiplier=-1).then_inc(consts, 1)
            pool.affine_select(out=sh.head8[:, :], in_=sh.head8[:, :], compare_op=ALU.is_ge, fill=0.0,
                               base=0, pattern=[[-8, 16]], channel_multiplier=1).then_inc(consts, 1)
            pool.affine_select(out=sh.head16[:, :], in_=sh.head16[:, :], compare_op=ALU.is_ge, fill=0.0,
                               base=0, pattern=[[-16, 8]], channel_multiplier=1).then_inc(consts, 1)
            pool.iota(sh.key_index[:, :], [[1, S]], base=0, channel_multiplier=0,
                      allow_small_or_imprecise_dtypes=True).then_inc(consts, 1)
            pool.iota(sh.expert_index[:, :], [[1, 8]], base=0, channel_multiplier=0,
                      allow_small_or_imprecise_dtypes=True).then_inc(consts, 1)
            pool.wait_ge(consts, 6)
            pool.affine_select(out=sh.head8[:, :], in_=sh.head8[:, :], compare_op=ALU.is_ge, fill=0.0,
                               base=7, pattern=[[8, 16]], channel_multiplier=-1).then_inc(consts, 1)
            pool.affine_select(out=sh.head16[:, :], in_=sh.head16[:, :], compare_op=ALU.is_ge, fill=0.0,
                               base=15, pattern=[[16, 8]], channel_multiplier=-1).then_inc(consts, 1)
            pool.tensor_copy(sh.ident_bf[:, :], sh.ident[:, :]).then_inc(consts, 1)

        @block.tensor
        def _(pe):
            pe.wait_ge(consts, 6)
            pe.wait_ge(steps_ready, 2)
            pe.matmul(sums[:, 0:NT], sh.tri[:, :], steps[:, :], start=True, stop=True)
            pe.matmul(sums[:, NT:2 * NT], sh.ones[:, :], steps[:, :], start=True, stop=True).then_inc(sums_done, 1)
            pe.wait_ge(loaded, 32)
            for g in range(NT // 4):
                if g >= 2:
                    pe.wait_ge(turned_copied, g - 1)
                for j in range(4):
                    last = pe.transpose(turned[g % 2][:, j, :], ctx_rows[:, 4 * g + j, :], sh.ident[:, :])
                last.then_inc(turned_done, 1)

        @block.scalar
        def _(act):
            for g in range(NT // 4):
                act.wait_ge(turned_done, g + 1)
                act.activation(sh.ctxT[:, 512 * g:512 * (g + 1)].rearrange("p (a b) -> p a b", a=4),
                               turned[g % 2][:, :, :], ACT.Copy).then_inc(turned_copied, 1)

        @block.vector
        def _(dve):
            dve.wait_ge(masks_loaded, 32)
            dve.tensor_copy(sh.query_mask[:, :], mask_u8[:, :]).then_inc(steps_ready, 1)
            dve.tensor_copy(steps[:, :], mask_i32[:, :]).then_inc(steps_ready, 1)
            dve.wait_ge(sums_done, 1)
            dve.tensor_copy(sh.last_patch[:, :], sums[:, 0:NT]).then_inc(steps_ready, 1)
            dve.wait_ge(steps_ready, 3)
            odd = sh.last_patch[:, :].rearrange("p (b q) -> p b q", q=QT)[:, :, 1]
            even_total = sums[:, NT:2 * NT].rearrange("p (b q) -> p b q", q=QT)[:, :, 0]
            dve.tensor_tensor(odd, odd, even_total, ALU.add).then_inc(steps_ready, 1)

        ph.retire(sh)


def dve_layernorm(dve, src, out, stats, moments, stats_done, moments_done, rstd_done, normed, eps, b):
    for q in range(QT):
        dve.bn_stats(stats[:, q, :], src[q]).then_inc(stats_done, 1)
    dve.wait_ge(stats_done, (QT + 1) * b + QT)
    dve.sem_inc(stats_done, 1)
    for q in range(QT):
        dve.bn_aggr(moments[:, q, 0:2], stats[:, q, :]).then_inc(moments_done, 1)
    dve.wait_ge(moments_done, (QT + 1) * b + QT)
    dve.tensor_scalar(moments[:, :, 2:3], moments[:, :, 1:2], eps, None, ALU.add).then_inc(moments_done, 1)
    dve.wait_ge(rstd_done, b + 1)
    for q in range(QT):
        dve.tensor_scalar(out[q], src[q], moments[:, q, 0:1], moments[:, q, 3:4],
                          ALU.subtract, ALU.mult).then_inc(normed, 1)


def pool_rstd(pool, sh, moments, moments_done, rstd_done, b):
    pool.wait_ge(moments_done, (QT + 1) * (b + 1))
    pool.tensor_tensor(moments[:, :, 3:4], moments[:, :, 2:3], sh.half[:, 0:QT].rearrange("p (q o) -> p q o", o=1),
                       ALU.pow).then_inc(rstd_done, 1)


def phase_clipped_attention(nc, sh):
    H, DH, U = 16, 8, 8
    with ExitStack() as ctx:
        ph = Phase(nc, ctx, "l0a")
        w_rows = ph.sbuf("w_rows", [P, 4, D])
        wT = ph.sbuf("wT", [P, 4, D])
        stats = ph.sbuf("stats", [P, QT, 6])
        moments = ph.sbuf("moments", [P, QT, 4])
        xn = ph.sbuf("xn", [P, QT, D])
        xnT = ph.sbuf("xnT", [P, S])
        qT = ph.sbuf("qT", [P, S])
        ctx_now = ph.sbuf("ctx_now", [P, S])
        q_head = ph.sbuf("q_head", [P, 2, H, S])
        kT = ph.sbuf("kT", [P, 2, S])
        v_one = ph.sbuf("v_one", [P, 2, QT, H, DH + 1])
        probs = ph.sbuf("probs", [P, 2, QT, 2, S])
        inverse = ph.sbuf("inverse", [P, QT, H])
        mixed = ph.sbuf("mixed", [P, QT, H, DH])
        mixedT = ph.sbuf("mixedT", [P, S])
        scores = [ph.psum(f"scores{i}", [P, QT, 2, S]) for i in range(2)]
        out_sums = [ph.psum(f"out_sums{i}", [P, QT, H, 16]) for i in range(2)]
        front_bank = ph.psum("front_bank", [P, 512])
        tail_bank = ph.psum("tail_bank", [P, 512])
        names = ["w_loaded", "w_turned", "w_copied", "ones_set", "stats_done", "moments_done", "rstd_done",
                 "normed", "front_filled", "front_copied", "ctx_ready", "q_split", "scored", "exp_done",
                 "clipped", "summed", "inverted", "mixed_ready", "tail_filled", "tail_copied"]
        (w_loaded, w_turned, w_copied, ones_set, stats_done, moments_done, rstd_done, normed, front_filled,
         front_copied, ctx_ready, q_split, scored, exp_done, clipped, summed, inverted, mixed_ready,
         tail_filled, tail_copied) = [ph.sem(n) for n in names]
        block = ctx.enter_context(nc.Block())

        def batches(eng, front, unit, drain, tail):
            front(0, 0, True)

            def one(b, par, first, more):
                for u in range(U):
                    unit(b, par, u, first)
                    if u == 3 and more:
                        front(b + 1, 1 - par, False)
                drain(b, par, first)
                tail(b, par)

            one(0, 0, True, True)
            one(1, 1, True, True)
            with eng.Fori(2, NB - 2, 2) as b:
                one(b, 0, False, True)
                one(b + 1, 1, False, True)
            one(NB - 2, 0, False, True)
            one(NB - 1, 1, False, False)

        @block.sync
        def _(sp):
            for j, n in enumerate(("W_q", "W_k", "W_v", "W_o")):
                sp.dma_start(w_rows[:, j, :], sh.dram["L0_xattn_" + n]).then_inc(w_loaded, 16)

        @block.gpsimd
        def _(pool):
            clear_retired(pool, sh)
            pool.memset(v_one[:, :, :, :, DH:DH + 1], 1.0).then_inc(ones_set, 1)

            def front(b, par, first):
                if not first:
                    pool.wait_ge(front_filled, 3 * b)
                pool.tensor_copy(ctx_now[:, :], sh.ctxT[:, bass.ds(b * S, S)]).then_inc(ctx_ready, 1)
                pool_rstd(pool, sh, moments, moments_done, rstd_done, b)

            batches(pool, front, lambda *a: None, lambda *a: None, lambda *a: None)

        @block.tensor
        def _(pe):
            pe.wait_ge(w_loaded, 64)
            for j in range(4):
                last = pe.transpose(front_bank[:, P * j:P * (j + 1)], w_rows[:, j, :], sh.ident[:, :])
            last.then_inc(w_turned, 1)
            pe.wait_ge(w_copied, 1)

            def front(b, par, first):
                pe.wait_ge(normed, QT * (b + 1))
                if not first:
                    pe.wait_ge(front_copied, 3 * b)
                for q in range(QT):
                    last = pe.transpose(front_bank[:, P * q:P * (q + 1)], xn[:, q, :], sh.ident[:, :])
                last.then_inc(front_filled, 1)
                pe.wait_ge(front_copied, 3 * b + 1)
                pe.wait_ge(ctx_ready, b + 1)
                pe.matmul(front_bank[:, 0:S], wT[:, 0, :], xnT[:, :], start=True, stop=True)
                pe.matmul(front_bank[:, S:2 * S], wT[:, 1, :], ctx_now[:, :], start=True, stop=True).then_inc(front_filled, 1)
                pe.wait_ge(front_copied, 3 * b + 2)
                for t in range(QT):
                    last = pe.matmul(front_bank[:, D * t:D * (t + 1)], ctx_now[:, P * t:P * (t + 1)], wT[:, 2, :],
                                     start=True, stop=True)
                last.then_inc(front_filled, 1)

            def value_products(b, par, u, first):
                pe.wait_ge(clipped, U * b + u + 1)
                if u == 0:
                    pe.wait_ge(front_copied, 3 * b + 3)
                    if not first:
                        pe.wait_ge(mixed_ready, QT * (b - 1))
                for j in range(2):
                    for q in range(QT):
                        for t in range(QT):
                            last = pe.matmul(out_sums[par][:, q, 2 * u + j, 0:DH + 1],
                                             probs[:, u % 2, t, j, P * q:P * (q + 1)],
                                             v_one[:, par, t, 2 * u + j, :], start=(t == 0), stop=(t == QT - 1))
                last.then_inc(summed, 1)

            def unit(b, par, u, first):
                if u == 0:
                    pe.wait_ge(q_split, b + 1)
                if not (first and par == 0 and u < 2):
                    pe.wait_ge(exp_done, U * b + u - 1)
                for t in range(QT):
                    last = pe.matmul(scores[u % 2][:, t, :, :], kT[:, par, P * t:P * (t + 1)],
                                     q_head[:, par, 2 * u:2 * u + 2, :], start=True, stop=True)
                last.then_inc(scored, 1)
                if u:
                    value_products(b, par, u - 1, first)

            def tail(b, par):
                pe.wait_ge(mixed_ready, QT * (b + 1))
                for q in range(QT):
                    last = pe.transpose(tail_bank[:, P * q:P * (q + 1)],
                                        mixed[:, q, :, :].rearrange("p h d -> p (h d)"), sh.ident[:, :])
                last.then_inc(tail_filled, 1)
                pe.wait_ge(tail_copied, 2 * b + 1)
                for q in range(QT):
                    last = pe.matmul(tail_bank[:, D * q:D * (q + 1)], mixedT[:, P * q:P * (q + 1)], wT[:, 3, :],
                                     start=True, stop=True)
                last.then_inc(tail_filled, 1)

            batches(pe, front, unit, lambda b, par, first: value_products(b, par, U - 1, first), tail)

        @block.scalar
        def _(act):
            act.wait_ge(w_turned, 1)
            act.activation(wT[:, :, :], front_bank[:, :].rearrange("p (j d) -> p j d", j=4), ACT.Copy).then_inc(w_copied, 1)
            act.wait_ge(ones_set, 1)

            def front(b, par, first):
                act.wait_ge(front_filled, 3 * b + 1)
                act.activation(xnT[:, :], front_bank[:, 0:S], ACT.Copy).then_inc(front_copied, 1)
                act.wait_ge(front_filled, 3 * b + 2)
                act.activation(qT[:, :], front_bank[:, 0:S], ACT.Copy, scale=float(DH) ** -0.5)
                act.activation(kT[:, par, :], front_bank[:, S:2 * S], ACT.Copy).then_inc(front_copied, 1)
                act.wait_ge(front_filled, 3 * b + 3)
                act.activation(v_one[:, par, :, :, 0:DH],
                               front_bank[:, 0:S].rearrange("p (t h d) -> p t h d", t=QT, h=H), ACT.Copy).then_inc(front_copied, 1)

            def unit(b, par, u, first):
                act.wait_ge(scored, U * b + u + 1)
                if not (first and par == 0 and u < 2):
                    act.wait_ge(summed, U * b + u - 1)
                act.activation(probs[:, u % 2, :, :, :], scores[u % 2][:, :, :, :], ACT.Exp).then_inc(exp_done, 1)

            batches(act, front, unit, lambda *a: None, lambda *a: None)

        @block.vector
        def _(dve):
            def front(b, par, first):
                if not first:
                    dve.wait_ge(front_filled, 3 * b - 2)
                rows = [sh.x_all[:, bass.ds(b * QT + q, 1), :].rearrange("p o d -> p (o d)") for q in range(QT)]
                dve_layernorm(dve, rows, [xn[:, q, :] for q in range(QT)], stats, moments, stats_done,
                              moments_done, rstd_done, normed, LN_EPS, b)
                dve.wait_ge(front_copied, 3 * b + 2)
                for h in range(H):
                    last = dve.tensor_scalar(q_head[:, par, h, :], qT[:, :], sh.head8[:, h:h + 1], None, ALU.mult)
                last.then_inc(q_split, 1)

            def unit(b, par, u, first):
                dve.wait_ge(exp_done, U * b + u + 1)
                buf = probs[:, u % 2, :, :, :]
                dve.tensor_scalar(buf, buf, EXP_LOW, EXP_HIGH, ALU.max, ALU.min).then_inc(clipped, 1)

            def tail(b, par):
                dve.wait_ge(summed, U * (b + 1))
                dve.reciprocal(inverse[:, :, :], out_sums[par][:, :, :, DH]).then_inc(inverted, 1)
                dve.wait_ge(inverted, (1 + QT) * b + 1)
                for q in range(QT):
                    dve.tensor_scalar(inverse[:, q, :], inverse[:, q, :],
                                      sh.query_mask[:, bass.ds(b * QT + q, 1)], None, ALU.mult).then_inc(inverted, 1)
                dve.wait_ge(inverted, (1 + QT) * (b + 1))
                for q in range(QT):
                    dve.tensor_tensor(mixed[:, q, :, :], out_sums[par][:, q, :, 0:DH],
                                      inverse[:, q, :].unsqueeze(2).to_broadcast([P, H, DH]), ALU.mult).then_inc(mixed_ready, 1)
                dve.wait_ge(tail_filled, 2 * b + 1)
                dve.tensor_copy(mixedT[:, :], tail_bank[:, 0:S]).then_inc(tail_copied, 1)
                dve.wait_ge(tail_filled, 2 * b + 2)
                rows = sh.x_all[:, bass.ds(b * QT, QT), :]
                dve.tensor_tensor(rows, rows, tail_bank[:, 0:S].rearrange("p (q d) -> p q d", q=QT),
                                  ALU.add).then_inc(tail_copied, 1)

            batches(dve, front, unit, lambda *a: None, tail)
        ph.retire(sh)


def dve_quantise(dve, rows, width, rms, rounded, quant, deq, w_mean, step, n, row_sum, root, quantised, b):
    dve.tensor_reduce(rms[:, :, 3], rows[:, :, :], AX.X, ALU.max, apply_absolute_value=True).then_inc(step, n.up())
    dve.wait_ge(step, n.all(b))
    dve.tensor_scalar(rms[:, :, 0], rms[:, :, 2], 1.0 / width, RMS_EPS, ALU.mult, ALU.add).then_inc(row_sum, 1)
    dve.wait_ge(root, b + 1)
    dve.tensor_tensor(rms[:, :, 2], rms[:, :, 3], rms[:, :, 1], ALU.mult).then_inc(step, n.up())
    for q in range(QT):
        dve.tensor_scalar(rounded[:, q, :], rows[:, q, :], rms[:, q, 1:2], None, ALU.mult).then_inc(step, n.up())
    dve.wait_ge(step, n.all(b))
    dve.tensor_scalar(rms[:, :, 2], rms[:, :, 2], QUANT_EPS, None, ALU.max).then_inc(step, n.up())
    dve.wait_ge(step, n.all(b))
    dve.reciprocal(rms[:, :, 3], rms[:, :, 2]).then_inc(step, n.up())
    dve.tensor_scalar(deq[:, :], rms[:, :, 2], w_mean, 1.0 / 127.0, ALU.mult, ALU.mult).then_inc(step, n.up())
    dve.wait_ge(step, n.all(b))
    dve.tensor_scalar(rms[:, :, 3], rms[:, :, 3], 127.0, None, ALU.mult).then_inc(step, n.up())
    dve.wait_ge(step, n.all(b))
    for q in range(QT):
        dve.tensor_scalar(rounded[:, q, :], rounded[:, q, :], rms[:, q, 3:4], ROUND, ALU.mult, ALU.add).then_inc(step, n.up())
    dve.wait_ge(step, n.all(b))
    dve.tensor_scalar(rounded[:, :, :], rounded[:, :, :], ROUND, -128.0, ALU.subtract, ALU.max).then_inc(step, n.up())
    dve.wait_ge(step, n.all(b))
    dve.tensor_scalar(quant[:, :, :], rounded[:, :, :], 127.0, None, ALU.min).then_inc(quantised, 1)


def phase_ternary_ffn(nc, sh):
    F = 512
    C = F // P
    STEPS = 2 + 2 * 11
    with ExitStack() as ctx:
        ph = Phase(nc, ctx, "l0f")
        step = ph.sem("step")
        w1_rows = ph.sbuf("w1_rows", [P, C, D])
        w2_rows = ph.sbuf("w2_rows", [P, F])
        magnitude = ph.sbuf("magnitude", [P, 2])
        w_scale = ph.sbuf("w_scale", [P, 2, 2])
        w_round = ph.sbuf("w_round", [P, 2, F])
        w_tern = ph.sbuf("w_tern", [P, 2, F], BF16)
        w1q = ph.sbuf("w1q", [P, F], BF16)
        w2q = ph.sbuf("w2q", [P, C, D], BF16)
        bias1 = ph.sbuf("bias1", [P, F])
        bias2 = ph.sbuf("bias2", [P, D])
        stats = ph.sbuf("stats", [P, QT, 6])
        moments = ph.sbuf("moments", [P, QT, 4])
        xn = ph.sbuf("xn", [P, QT, D])
        squares = ph.sbuf("squares", [P, QT, F])
        rms1 = ph.sbuf("rms1", [P, QT, 4])
        rms2 = ph.sbuf("rms2", [P, QT, 4])
        deq1 = ph.sbuf("deq1", [P, QT])
        deq2 = ph.sbuf("deq2", [P, QT])
        rounded1 = ph.sbuf("rounded1", [P, QT, D])
        quant1 = ph.sbuf("quant1", [P, QT, D], BF16)
        quant1T = ph.sbuf("quant1T", [P, QT, P], BF16)
        hidden = ph.sbuf("hidden", [P, QT, F])
        gelu = ph.sbuf("gelu", [P, QT, F])
        rounded2 = ph.sbuf("rounded2", [P, QT, F])
        quant2 = ph.sbuf("quant2", [P, QT, F], BF16)
        quant2T = ph.sbuf("quant2T", [P, QT, C, P], BF16)
        turned1 = ph.psum("turned1", [P, QT, 512], BF16)
        turned2 = ph.psum("turned2", [P, QT, 1024], BF16)
        up = ph.psum("up", [P, QT, F])
        down = ph.psum("down", [P, 512])
        (loaded, summed, totals, scaled, wrounded, ternary, w_turned, w_copied, stats_done, moments_done, rstd_done,
         normed, row1, root1, scale1, quantised1, turned1_done, copied1, up_done, hidden_done, gelu_done, squared2,
         row2, root2, scale2, quantised2, turned2_done, copied2, down_done, added) = [ph.sem(n) for n in (
             "loaded", "summed", "totals", "scaled", "wrounded", "ternary", "w_turned", "w_copied", "stats_done",
             "moments_done", "rstd_done", "normed", "row1", "root1", "scale1", "quantised1", "turned1_done",
             "copied1", "up_done", "hidden_done", "gelu_done", "squared2", "row2", "root2", "scale2",
             "quantised2", "turned2_done", "copied2", "down_done", "added")]
        block = ctx.enter_context(nc.Block())

        @block.sync
        def _(sp):
            sp.dma_start(w1_rows[:, :, :], sh.dram["L0_ffn_w1"].rearrange("(c p) i -> p c i", p=P)).then_inc(loaded, 16)
            sp.dma_start(w2_rows[:, :], sh.dram["L0_ffn_w2"]).then_inc(loaded, 16)
            sp.dma_start(bias1[:, :], sh.dram["L0_ffn_b1"].rearrange("(o f) -> o f", o=1).to_broadcast([P, F])).then_inc(loaded, 16)
            sp.dma_start(bias2[:, :], sh.dram["L0_ffn_b2"].rearrange("(o f) -> o f", o=1).to_broadcast([P, D])).then_inc(loaded, 16)

        @block.gpsimd
        def _(pool):
            clear_retired(pool, sh)
            with pool.Fori(0, NB) as b:
                pool_rstd(pool, sh, moments, moments_done, rstd_done, b)
                pool.wait_ge(row1, b + 1)
                pool.tensor_tensor(rms1[:, :, 1:2], rms1[:, :, 0:1], sh.half[:, 0:QT].unsqueeze(2), ALU.pow).then_inc(root1, 1)
                pool.wait_ge(row2, b + 1)
                pool.tensor_tensor(rms2[:, :, 1:2], rms2[:, :, 0:1], sh.half[:, 0:QT].unsqueeze(2), ALU.pow).then_inc(root2, 1)

        @block.tensor
        def _(pe):
            pe.wait_ge(summed, 2)
            pe.matmul(down[:, 0:2], sh.ones[:, :], magnitude[:, :], start=True, stop=True).then_inc(totals, 1)
            pe.wait_ge(ternary, 2)
            for j in range(2):
                for c in range(C):
                    last = pe.transpose(turned2[:, j, P * c:P * (c + 1)], w_tern[:, j, P * c:P * (c + 1)], sh.ident_bf[:, :])
            last.then_inc(w_turned, 1)
            pe.wait_ge(w_copied, 2)
            with pe.Fori(0, NB) as b:
                pe.wait_ge(quantised1, b + 1)
                for q in range(QT):
                    last = pe.transpose(turned1[:, q, 0:P], quant1[:, q, :], sh.ident_bf[:, :])
                last.then_inc(turned1_done, 1)
                pe.wait_ge(copied1, b + 1)
                for q in range(QT):
                    pe.matmul(up[:, q, :], quant1T[:, q, :], w1q[:, :], start=True, stop=True).then_inc(up_done, 1)
                pe.wait_ge(quantised2, b + 1)
                for q in range(QT):
                    for c in range(C):
                        last = pe.transpose(turned2[:, q, P * c:P * (c + 1)], quant2[:, q, P * c:P * (c + 1)], sh.ident_bf[:, :])
                    last.then_inc(turned2_done, 1)
                for q in range(QT):
                    pe.wait_ge(copied2, QT * b + q + 1)
                    for c in range(C):
                        last = pe.matmul(down[:, D * q:D * (q + 1)], quant2T[:, q, c, :], w2q[:, c, :],
                                         start=(c == 0), stop=(c == C - 1))
                last.then_inc(down_done, 1)

        @block.scalar
        def _(act):
            act.wait_ge(w_turned, 1)
            act.activation(w1q[:, :], turned2[:, 0, 0:F], ACT.Copy).then_inc(w_copied, 1)
            act.activation(w2q[:, :, :], turned2[:, 1, 0:F].rearrange("p (c o) -> p c o", c=C), ACT.Copy).then_inc(w_copied, 1)
            with act.Fori(0, NB) as b:
                act.wait_ge(turned1_done, b + 1)
                act.activation(quant1T[:, :, :], turned1[:, :, 0:P], ACT.Copy).then_inc(copied1, 1)
                for q in range(QT):
                    act.wait_ge(hidden_done, QT * b + q + 1)
                    act.activation(gelu[:, q, :], hidden[:, q, :], ACT.Gelu).then_inc(gelu_done, 1)
                for q in range(QT):
                    act.wait_ge(gelu_done, QT * b + q + 1)
                    act.activation(squares[:, q, :], gelu[:, q, :], ACT.Square, accum_out=rms2[:, q, 2:3]).then_inc(squared2, 1)
                for q in range(QT):
                    act.wait_ge(turned2_done, QT * b + q + 1)
                    act.activation(quant2T[:, q, :, :], turned2[:, q, 0:F].rearrange("p (c t) -> p c t", c=C), ACT.Copy).then_inc(copied2, 1)

        @block.vector
        def _(dve):
            dve.wait_ge(loaded, 64)
            dve.tensor_reduce(magnitude[:, 0:1], w1_rows[:, :, :].rearrange("p c i -> p (c i)"), AX.X, ALU.add, apply_absolute_value=True).then_inc(summed, 1)
            dve.tensor_reduce(magnitude[:, 1:2], w2_rows[:, :], AX.X, ALU.add, apply_absolute_value=True).then_inc(summed, 1)
            dve.wait_ge(totals, 1)
            dve.tensor_scalar(w_scale[:, :, 0], down[:, 0:2], 1.0 / (F * D), QUANT_EPS, ALU.mult, ALU.max).then_inc(scaled, 1)
            dve.wait_ge(scaled, 1)
            dve.reciprocal(w_scale[:, :, 1], w_scale[:, :, 0]).then_inc(scaled, 1)
            dve.wait_ge(scaled, 2)
            for j, w in enumerate((w1_rows[:, :, :].rearrange("p c i -> p (c i)"), w2_rows[:, :])):
                dve.tensor_scalar(w_round[:, j, :], w, w_scale[:, j, 1:2], ROUND, ALU.mult, ALU.add).then_inc(wrounded, 1)
            for j in range(2):
                dve.wait_ge(wrounded, 2 + j)
                dve.tensor_scalar(w_round[:, j, :], w_round[:, j, :], ROUND, 1.0, ALU.subtract, ALU.min).then_inc(wrounded, 1)
            dve.wait_ge(wrounded, 4)
            for j in range(2):
                dve.tensor_scalar(w_tern[:, j, :], w_round[:, j, :], -1.0, None, ALU.max).then_inc(ternary, 1)

            with dve.Fori(0, NB) as b:
                rows = [sh.x_all[:, bass.ds(b * QT + q, 1), :].rearrange("p o d -> p (o d)") for q in range(QT)]
                dve_layernorm(dve, rows, [xn[:, q, :] for q in range(QT)], stats, moments, stats_done,
                              moments_done, rstd_done, normed, LN_EPS, b)
                dve.wait_ge(normed, QT * (b + 1))
                n = Counter(STEPS)
                dve.tensor_tensor(squares[:, :, 0:D], xn[:, :, :], xn[:, :, :], ALU.mult).then_inc(step, n.up())
                dve.wait_ge(step, n.all(b))
                dve.tensor_reduce(rms1[:, :, 2], squares[:, :, 0:D], AX.X, ALU.add).then_inc(step, n.up())
                dve_quantise(dve, xn, D, rms1, rounded1, quant1, deq1, w_scale[:, 0, 0:1], step, n, row1, root1, quantised1, b)
                for q in range(QT):
                    dve.wait_ge(up_done, QT * b + q + 1)
                    dve.scalar_tensor_tensor(out=hidden[:, q, :], in0=up[:, q, :], scalar=deq1[:, q:q + 1],
                                             in1=bias1[:, :], op0=ALU.mult, op1=ALU.add).then_inc(hidden_done, 1)
                dve.wait_ge(squared2, QT * (b + 1))
                dve_quantise(dve, gelu, F, rms2, rounded2, quant2, deq2, w_scale[:, 1, 0:1], step, n, row2, root2, quantised2, b)
                n.close()
                dve.wait_ge(down_done, b + 1)
                for q in range(QT):
                    dve.scalar_tensor_tensor(out=xn[:, q, :], in0=down[:, D * q:D * (q + 1)], scalar=deq2[:, q:q + 1],
                                             in1=bias2[:, :], op0=ALU.mult, op1=ALU.add).then_inc(added, 1)
                dve.wait_ge(added, (QT + 1) * b + QT)
                out_rows = sh.x_all[:, bass.ds(b * QT, QT), :]
                dve.tensor_tensor(out_rows, out_rows, xn[:, :, :], ALU.add).then_inc(added, 1)
                dve.wait_ge(added, (QT + 1) * (b + 1))
        ph.retire(sh)


def phase_softmax_attention(nc, sh, multi_query):
    H, G, U = 16, 4, 8
    DH = 64 if multi_query else 8
    C = H * DH // P
    FC = 5 if multi_query else 3
    TC = 2 * QT + 1 if multi_query else 2
    with ExitStack() as ctx:
        ph = Phase(nc, ctx, "l2a" if multi_query else "l1a")
        if multi_query:
            wq = ph.sbuf("wq", [P, H * DH])
            wkv = ph.sbuf("wkv", [P, 3 * DH])
            wo = ph.sbuf("wo", [P, C, D])
        else:
            w_rows = ph.sbuf("w_rows", [P, 4, D])
            wT = ph.sbuf("wT", [P, 4, D])
            bias_cols = ph.sbuf("bias_cols", [P, 2])
            bias_q = ph.sbuf("bias_q", [P, 1])
            bias_rows = ph.sbuf("bias_rows", [1, 2, D])
            stats = ph.sbuf("stats", [P, QT, 6])
            moments = ph.sbuf("moments", [P, QT, 4])
            xn = ph.sbuf("xn", [P, QT, D])
            xnT = ph.sbuf("xnT", [P, S])
            k_head = ph.sbuf("k_head", [P, 2, H, S])
        ctx_now = ph.sbuf("ctx_now", [P, S])
        qT = ph.sbuf("qT", [P, 2, C, S])
        kT = ph.sbuf("kT", [P, 2, S])
        values = ph.sbuf("values", [P, 2, QT, 64 if multi_query else D])
        mask = ph.sbuf("mask", [P, 2, QT, S])
        masked = ph.sbuf("masked", [P, 2, G, S])
        minus_max = ph.sbuf("minus_max", [P, 2, G])
        probs = ph.sbuf("probs", [P, 2, G, S])
        sums = ph.sbuf("sums", [P, 4, G])
        inverse = ph.sbuf("inverse", [P, 4, G])
        probsT = ph.sbuf("probsT", [P, 2, G, QT, P])
        mixed = ph.sbuf("mixed", [P, QT, H, DH])
        mixedT = ph.sbuf("mixedT", [P, QT, C, P])
        scores = [ph.psum(f"scores{i}", [P, G, S]) for i in range(2)]
        turned = ph.psum("turned", [P, G, QT, P])
        out_sums = ph.psum("out_sums", [P, 512])
        side = ph.psum("side", [P, 512])
        out_view = out_sums[:, 0:G * DH].rearrange("p (g d) -> p g d", g=G)
        (w_loaded, w_turned, w_copied, bias_scaled, stats_done, moments_done, rstd_done, normed, side_filled,
         side_copied, ctx_ready, heads_split, mask_ready, mask_used, scored, mask_added, max_ready, exp_done,
         turned_done, turned_copied, summed, inverted, mixed_ready, added) = [ph.sem(n) for n in (
             "w_loaded", "w_turned", "w_copied", "bias_scaled", "stats_done", "moments_done", "rstd_done",
             "normed", "side_filled", "side_copied", "ctx_ready", "heads_split", "mask_ready", "mask_used",
             "scored", "mask_added", "max_ready", "exp_done", "turned_done", "turned_copied", "summed",
             "inverted", "mixed_ready", "added")]
        block = ctx.enter_context(nc.Block())

        def head_of(j):
            return 2 * (j % 2) + j // 2 if multi_query else j

        def front_base(b, first):
            return 0 if first else b * (FC + TC) - TC

        def tail_base(b, last):
            return b * (FC + TC) + (FC if last else 2 * FC)

        def batches(eng, front, unit, drain, tail):
            front(0, 0, True)

            def one(b, par, first, more):
                for u in range(U):
                    unit(b, par, u, first)
                    if u == 3 and more:
                        front(b + 1, 1 - par, False)
                drain(b, par, first)
                tail(b, par, not more)

            one(0, 0, True, True)
            one(1, 1, False, True)
            with eng.Fori(2, NB - 2, 2) as b:
                one(b, 0, False, True)
                one(b + 1, 1, False, True)
            one(NB - 2, 0, False, True)
            one(NB - 1, 1, False, False)

        @block.sync
        def _(sp):
            if multi_query:
                sp.dma_start(wq[:, :], sh.dram["L2_xattn_Wq"]).then_inc(w_loaded, 16)
                for j in range(2):
                    sp.dma_start(wkv[:, DH * j:DH * (j + 1)], sh.dram["L2_xattn_Wkv"][:, 0:DH]).then_inc(w_loaded, 16)
                sp.dma_start(wkv[:, 2 * DH:3 * DH], sh.dram["L2_xattn_Wkv"][:, DH:2 * DH]).then_inc(w_loaded, 16)
                sp.dma_start(wo[:, :, :], sh.dram["L2_xattn_Wout"].rearrange("(c p) d -> p c d", p=P)).then_inc(w_loaded, 16)

                def front(b, par, first):
                    if not first:
                        sp.wait_ge(mask_ready, 16 * b)
                    if not (isinstance(b, int) and b < 2):
                        sp.wait_ge(mask_used, b - 1)
                    sp.dma_start(mask[:, par, :, :], sh.dram["mask_BxSxS2_ff0"][bass.ds(b, 1), :, :]
                                 .rearrange("o (q p) k -> p (o q) k", p=P)).then_inc(mask_ready, 16)

                batches(sp, front, lambda *a: None, lambda *a: None, lambda *a: None)
            else:
                for j, n in enumerate(("wq", "wk", "wv", "wo")):
                    sp.dma_start(w_rows[:, j, :], sh.dram["L1_xattn_" + n]).then_inc(w_loaded, 16)
                with nc.allow_non_contiguous_dma(reason="bias columns"):
                    for j, n in enumerate(("bq", "bk")):
                        sp.dma_start(bias_cols[:, j:j + 1], sh.dram["L1_xattn_" + n].rearrange("(d o) -> d o", o=1)).then_inc(w_loaded, 16)
                for j, n in enumerate(("bv", "bo")):
                    sp.dma_start(bias_rows[:, j, :], sh.dram["L1_xattn_" + n].rearrange("(o d) -> o d", o=1)).then_inc(w_loaded, 16)

        @block.gpsimd
        def _(pool):
            clear_retired(pool, sh)
            def front(b, par, first):
                if not first:
                    pool.wait_ge(side_filled, front_base(b - 1, isinstance(b, int) and b == 1) + FC)
                source = sh.cnT_all if multi_query else sh.ctxT
                pool.tensor_copy(ctx_now[:, :], source[:, bass.ds(b * S, S)]).then_inc(ctx_ready, 1)
                if not multi_query:
                    pool_rstd(pool, sh, moments, moments_done, rstd_done, b)

            batches(pool, front, lambda *a: None, lambda *a: None, lambda *a: None)

        @block.tensor
        def _(pe):
            if not multi_query:
                pe.wait_ge(w_loaded, 128)
                for j in range(4):
                    last = pe.transpose(side[:, P * j:P * (j + 1)], w_rows[:, j, :], sh.ident[:, :])
                last.then_inc(w_turned, 1)
                pe.wait_ge(w_copied, 1)
            else:
                pe.wait_ge(w_loaded, 80)

            def front(b, par, first):
                base = front_base(b, first)
                if multi_query:
                    for r in range(4):
                        if not (first and r == 0):
                            pe.wait_ge(side_copied, base + r)
                        for j in range(2):
                            last = pe.matmul(side[:, S * j:S * (j + 1)], wq[:, P * (2 * r + j):P * (2 * r + j + 1)],
                                             sh.xnT_all[:, bass.ds(b * S, S)], start=True, stop=True)
                        last.then_inc(side_filled, 1)
                    pe.wait_ge(side_copied, base + 4)
                    pe.wait_ge(ctx_ready, b + 1)
                    pe.matmul(side[:, 0:S], wkv[:, 0:2 * DH], ctx_now[:, :], start=True, stop=True)
                    for t in range(QT):
                        last = pe.matmul(side[:, S + DH * t:S + DH * (t + 1)], ctx_now[:, P * t:P * (t + 1)],
                                         wkv[:, 2 * DH:3 * DH], start=True, stop=True)
                    last.then_inc(side_filled, 1)
                    return
                pe.wait_ge(normed, QT * (b + 1))
                if not first:
                    pe.wait_ge(side_copied, base)
                for q in range(QT):
                    last = pe.transpose(side[:, P * q:P * (q + 1)], xn[:, q, :], sh.ident[:, :])
                last.then_inc(side_filled, 1)
                pe.wait_ge(side_copied, base + 1)
                pe.wait_ge(ctx_ready, b + 1)
                pe.matmul(side[:, 0:S], wT[:, 0, :], xnT[:, :], start=True, stop=True)
                pe.matmul(side[:, S:2 * S], wT[:, 1, :], ctx_now[:, :], start=True, stop=True).then_inc(side_filled, 1)
                pe.wait_ge(side_copied, base + 2)
                for t in range(QT):
                    pe.matmul(side[:, D * t:D * (t + 1)], ctx_now[:, P * t:P * (t + 1)], wT[:, 2, :], start=True, stop=False)
                    last = pe.matmul(side[:, D * t:D * (t + 1)], sh.ones[0:1, :], bias_rows[:, 0, :], start=False, stop=True)
                last.then_inc(side_filled, 1)

            def turn(b, par, u):
                pe.wait_ge(exp_done, U * b + u + 1)
                if not (isinstance(b, int) and b == 0 and u == 0):
                    pe.wait_ge(turned_copied, U * b + u)
                for j in range(G):
                    for t in range(QT):
                        last = pe.transpose(turned[:, j, t, :], probs[:, u % 2, j, P * t:P * (t + 1)], sh.ident[:, :])
                last.then_inc(turned_done, 1)

            def value_products(b, par, u):
                pe.wait_ge(turned_copied, U * b + u + 1)
                if not (isinstance(b, int) and b == 0 and u == 0):
                    pe.wait_ge(mixed_ready, U * b + u)
                for j in range(G):
                    h = G * (u % 4) + head_of(j)
                    for t in range(QT):
                        v = values[:, par, t, :] if multi_query else values[:, par, t, DH * h:DH * (h + 1)]
                        last = pe.matmul(out_view[:, head_of(j), :], probsT[:, u % 2, j, t, :], v, start=(t == 0), stop=(t == QT - 1))
                last.then_inc(summed, 1)

            def unit(b, par, u, first):
                q, g = u // 4, u % 4
                if u == 0:
                    if multi_query:
                        pe.wait_ge(side_copied, front_base(b, first) + FC)
                    else:
                        pe.wait_ge(heads_split, b + 1)
                if not (first and u < 2):
                    pe.wait_ge(mask_added, U * b + u - 1)
                if multi_query:
                    for j in range(G):
                        h = G * g + head_of(j)
                        rows = slice(DH * (h % 2), DH * (h % 2 + 1))
                        last = pe.matmul(scores[u % 2][:, j, :], qT[rows, par, h // 2, P * q:P * (q + 1)],
                                         kT[rows, par, :], start=True, stop=True)
                else:
                    for j in range(0, G, 2):
                        last = pe.matmul(scores[u % 2][:, j:j + 2, :], qT[:, par, 0, P * q:P * (q + 1)],
                                         k_head[:, par, G * g + j:G * g + j + 2, :], start=True, stop=True)
                last.then_inc(scored, 1)
                if u == 0:
                    pe.wait_ge(side_copied, front_base(b, first) + FC)
                if u >= 1:
                    turn(b, par, u - 1)
                if u >= 2:
                    value_products(b, par, u - 2)

            def drain(b, par, first):
                turn(b, par, U - 1)
                value_products(b, par, U - 2)
                value_products(b, par, U - 1)

            def tail(b, par, last_batch):
                base = tail_base(b, last_batch)
                pe.wait_ge(mixed_ready, U * (b + 1))
                pe.wait_ge(side_copied, base)
                if multi_query:
                    for r in range(2 * QT):
                        if r:
                            pe.wait_ge(side_copied, base + r)
                        for j in range(4):
                            c = 4 * (r % 2) + j
                            last = pe.transpose(side[:, P * j:P * (j + 1)],
                                                mixed[:, r // 2, 2 * c:2 * c + 2, :].rearrange("p h d -> p (h d)"), sh.ident[:, :])
                        last.then_inc(side_filled, 1)
                else:
                    for q in range(QT):
                        last = pe.transpose(side[:, P * q:P * (q + 1)],
                                            mixed[:, q, :, :].rearrange("p h d -> p (h d)"), sh.ident[:, :])
                    last.then_inc(side_filled, 1)
                pe.wait_ge(side_copied, base + TC - 1)
                for q in range(QT):
                    for c in range(C):
                        last = pe.matmul(side[:, D * q:D * (q + 1)], mixedT[:, q, c, :],
                                         wo[:, c, :] if multi_query else wT[:, 3, :],
                                         start=(c == 0), stop=(multi_query and c == C - 1))
                    if not multi_query:
                        last = pe.matmul(side[:, D * q:D * (q + 1)], sh.ones[0:1, :], bias_rows[:, 1, :], start=False, stop=True)
                last.then_inc(side_filled, 1)

            batches(pe, front, unit, drain, tail)

        @block.scalar
        def _(act):
            if not multi_query:
                act.wait_ge(w_turned, 1)
                act.activation(wT[:, :, :], side[:, :].rearrange("p (j d) -> p j d", j=4), ACT.Copy).then_inc(w_copied, 1)
                act.activation(bias_q[:, :], bias_cols[:, 0:1], ACT.Copy, scale=float(DH) ** -0.5).then_inc(bias_scaled, 1)
                act.wait_ge(bias_scaled, 1)

            def front(b, par, first):
                base = front_base(b, first)
                if multi_query:
                    for r in range(4):
                        act.wait_ge(side_filled, base + r + 1)
                        act.activation(qT[:, par, 2 * r:2 * r + 2, :], side[:, :].rearrange("p (c s) -> p c s", c=2),
                                       ACT.Copy, scale=float(DH) ** -0.5).then_inc(side_copied, 1)
                    act.wait_ge(side_filled, base + 5)
                    act.activation(kT[:, par, :], side[:, 0:S], ACT.Copy)
                    act.activation(values[:, par, :, :], side[:, S:S + QT * DH].rearrange("p (t d) -> p t d", t=QT),
                                   ACT.Copy).then_inc(side_copied, 1)
                    return
                act.wait_ge(side_filled, base + 1)
                act.activation(xnT[:, :], side[:, 0:S], ACT.Copy).then_inc(side_copied, 1)
                act.wait_ge(side_filled, base + 2)
                act.activation(qT[:, par, 0, :], side[:, 0:S], ACT.Identity, scale=float(DH) ** -0.5, bias=bias_q[:, :])
                act.activation(kT[:, par, :], side[:, S:2 * S], ACT.Identity, bias=bias_cols[:, 1:2]).then_inc(side_copied, 1)
                act.wait_ge(side_filled, base + 3)
                act.activation(values[:, par, :, :], side[:, 0:QT * D].rearrange("p (t d) -> p t d", t=QT), ACT.Copy).then_inc(side_copied, 1)

            def copy_turned(b, par, u):
                act.wait_ge(turned_done, U * b + u + 1)
                act.activation(probsT[:, u % 2, :, :, :], turned[:, :, :, :], ACT.Copy).then_inc(turned_copied, 1)

            def unit(b, par, u, first):
                act.wait_ge(max_ready, U * b + u + 1)
                if not (first and u < 2):
                    act.wait_ge(turned_done, U * b + u - 1)
                for j in range(G):
                    last = act.activation(probs[:, u % 2, j, :], masked[:, u % 2, j, :], ACT.Exp,
                                          bias=minus_max[:, u % 2, j:j + 1], accum_out=sums[:, u % 4, head_of(j):head_of(j) + 1])
                last.then_inc(exp_done, 1)
                if u >= 1:
                    copy_turned(b, par, u - 1)

            def tail(b, par, last_batch):
                base = tail_base(b, last_batch)
                if multi_query:
                    for r in range(2 * QT):
                        act.wait_ge(side_filled, base + r + 1)
                        act.activation(mixedT[:, r // 2, 4 * (r % 2):4 * (r % 2) + 4, :],
                                       side[:, :].rearrange("p (c t) -> p c t", c=4), ACT.Copy).then_inc(side_copied, 1)
                else:
                    act.wait_ge(side_filled, base + 1)
                    act.activation(mixedT[:, :, 0, :], side[:, 0:S].rearrange("p (q t) -> p q t", q=QT), ACT.Copy).then_inc(side_copied, 1)

            batches(act, front, unit, lambda b, par, first: copy_turned(b, par, U - 1), tail)

        @block.vector
        def _(dve):
            def front(b, par, first):
                if multi_query:
                    return
                base = front_base(b, first)
                if not first:
                    dve.wait_ge(side_filled, front_base(b - 1, isinstance(b, int) and b == 1) + 1)
                rows = [sh.x_all[:, bass.ds(b * QT + q, 1), :].rearrange("p o d -> p (o d)") for q in range(QT)]
                dve_layernorm(dve, rows, [xn[:, q, :] for q in range(QT)], stats, moments, stats_done,
                              moments_done, rstd_done, normed, LN_EPS, b)
                for q in range(QT):
                    dve.tensor_scalar(mask[:, par, q, :], sh.key_index[:, :], sh.last_patch[:, bass.ds(b * QT + q, 1)],
                                      MASKED, ALU.is_gt, ALU.mult).then_inc(mask_ready, 8)
                dve.wait_ge(side_copied, base + 2)
                for h in range(H):
                    last = dve.tensor_scalar(k_head[:, par, h, :], kT[:, par, :], sh.head8[:, h:h + 1], None, ALU.mult)
                last.then_inc(heads_split, 1)

            def mix(b, par, u):
                dve.wait_ge(exp_done, U * b + u + 1)
                dve.reciprocal(inverse[:, u % 4, :], sums[:, u % 4, :]).then_inc(inverted, 1)
                dve.wait_ge(inverted, U * b + u + 1)
                dve.wait_ge(summed, U * b + u + 1)
                dve.tensor_tensor(mixed[:, u // 4, G * (u % 4):G * (u % 4 + 1), :], out_view,
                                  inverse[:, u % 4, :].unsqueeze(2).to_broadcast([P, G, DH]), ALU.mult).then_inc(mixed_ready, 1)

            def unit(b, par, u, first):
                if u == 0:
                    dve.wait_ge(mask_ready, 16 * (b + 1))
                dve.wait_ge(scored, U * b + u + 1)
                if not (first and u < 2):
                    dve.wait_ge(exp_done, U * b + u - 1)
                dve.tensor_tensor(masked[:, u % 2, :, :], scores[u % 2][:, :, :],
                                  mask[:, par, u // 4, :].unsqueeze(1).to_broadcast([P, G, S]), ALU.add).then_inc(mask_added, 1)
                dve.wait_ge(mask_added, U * b + u + 1)
                dve.tensor_reduce(minus_max[:, u % 2, :], masked[:, u % 2, :, :], AX.X, ALU.max, negate=True).then_inc(max_ready, 1)
                if u == U - 1:
                    dve.sem_inc(mask_used, 1)
                if u >= 2:
                    mix(b, par, u - 2)

            def drain(b, par, first):
                mix(b, par, U - 2)
                mix(b, par, U - 1)

            def tail(b, par, last_batch):
                base = tail_base(b, last_batch)
                dve.wait_ge(side_filled, base + TC)
                rows = sh.x_all[:, bass.ds(b * QT, QT), :]
                if multi_query:
                    dve.tensor_tensor(rows, rows, sh.y_all[:, bass.ds(b * QT, QT), :], ALU.add).then_inc(added, 1)
                    dve.wait_ge(added, b + 1)
                dve.tensor_tensor(rows, rows, side[:, 0:QT * D].rearrange("p (q d) -> p q d", q=QT), ALU.add).then_inc(side_copied, 1)

            batches(dve, front, unit, drain, tail)
        ph.retire(sh)


def phase_expert_ffn(nc, sh):
    E, F, T = 8, 352, 32
    CH = [(0, P), (P, P), (2 * P, F - 2 * P)]
    HALF = 4
    with ExitStack() as ctx:
        ph = Phase(nc, ctx, "l1f")
        w_gate = ph.sbuf("w_gate", [P, E, F])
        w_up = ph.sbuf("w_up", [P, E, F])
        w_down = ph.sbuf("w_down", [P, E, 3, D])
        stats = ph.sbuf("stats", [P, QT, 6])
        moments = ph.sbuf("moments", [P, QT, 4])
        xn = ph.sbuf("xn", [P, QT, D])
        x_expert = ph.sbuf("x_expert", [P, E, NB, T])
        silu = ph.sbuf("silu", [P, 2, F])
        hidden = ph.sbuf("hidden", [P, 2, F])
        hiddenT = ph.sbuf("hiddenT", [P, 2, 3, P])
        xT = ph.psum("xT", [P, 512])
        gate = ph.psum("gate", [P, 2, 512])
        up = ph.psum("up", [P, 2, 512])
        turned = ph.psum("turned", [P, 512])
        down = ph.psum("down", [P, 2, 512])
        (w_loaded, stats_done, moments_done, rstd_done, normed, xT_done, xT_copied, up_done, silu_done,
         hidden_done, turned_done, turned_copied, down_done, added) = [ph.sem(n) for n in (
             "w_loaded", "stats_done", "moments_done", "rstd_done", "normed", "xT_done", "xT_copied", "up_done",
             "silu_done", "hidden_done", "turned_done", "turned_copied", "down_done", "added")]
        block = ctx.enter_context(nc.Block())

        @block.sync
        def _(sp):
            sp.dma_start(w_gate[:, :, :], sh.dram["L1_ffn_w1"].rearrange("e d f -> d e f")).then_inc(w_loaded, 16)
            sp.dma_start(w_up[:, :, :], sh.dram["L1_ffn_w3"].rearrange("e d f -> d e f")).then_inc(w_loaded, 16)
            w2 = sh.dram["L1_ffn_w2"]
            for c, (at, n) in enumerate(CH):
                sp.dma_start(w_down[0:n, :, c, :], w2[:, at:at + n, :].rearrange("e f d -> f e d")).then_inc(w_loaded, 16)

        @block.gpsimd
        def _(pool):
            clear_retired(pool, sh)
            with pool.Fori(0, NB) as b:
                pool_rstd(pool, sh, moments, moments_done, rstd_done, b)

        units = [(e, half) for e in range(E) for half in range(2)]

        @block.tensor
        def _(pe):
            with pe.Fori(0, NB) as b:
                pe.wait_ge(normed, QT * (b + 1))
                for q in range(QT):
                    last = pe.transpose(xT[:, P * q:P * (q + 1)], xn[:, q, :], sh.ident[:, :])
                last.then_inc(xT_done, 1)
                pe.wait_ge(xT_copied, b + 1)
            pe.wait_ge(w_loaded, 80)

            def down_products(u):
                e, half = units[u]
                pe.wait_ge(hidden_done, u + 1)
                if u >= 1:
                    pe.wait_ge(turned_copied, u)
                for c, (at, n) in enumerate(CH):
                    last = pe.transpose(turned[0:n, P * c:P * (c + 1)], hidden[:, u % 2, at:at + n], sh.ident[:, :])
                last.then_inc(turned_done, 1)
                pe.wait_ge(turned_copied, u + 1)
                if u >= 2:
                    pe.wait_ge(added, 4 * (u - 1))
                for c, (at, n) in enumerate(CH):
                    last = pe.matmul(down[:, u % 2, 0:D], hiddenT[0:n, u % 2, c, :], w_down[0:n, e, c, :],
                                     start=(c == 0), stop=(c == 2))
                last.then_inc(down_done, 1)

            for u, (e, half) in enumerate(units):
                rows = x_expert[:, e, HALF * half:HALF * (half + 1), :].rearrange("p b t -> p (b t)")
                if u >= 2:
                    pe.wait_ge(hidden_done, u - 1)
                pe.matmul(gate[:, u % 2, 0:F], rows, w_gate[:, e, :], start=True, stop=True)
                pe.matmul(up[:, u % 2, 0:F], rows, w_up[:, e, :], start=True, stop=True).then_inc(up_done, 1)
                if u:
                    down_products(u - 1)
            down_products(len(units) - 1)

        @block.scalar
        def _(act):
            with act.Fori(0, NB) as b:
                act.wait_ge(xT_done, b + 1)
                act.activation(x_expert[:, :, bass.ds(b, 1), :].rearrange("p e o t -> p e (o t)"),
                               xT[:, 0:S].rearrange("p (e t) -> p e t", e=E), ACT.Copy).then_inc(xT_copied, 1)

            def copy_turned(u):
                act.wait_ge(turned_done, u + 1)
                for c, (at, n) in enumerate(CH):
                    last = act.activation(hiddenT[0:n, u % 2, c, :], turned[0:n, P * c:P * (c + 1)], ACT.Copy)
                last.then_inc(turned_copied, 1)

            for u in range(len(units)):
                act.wait_ge(up_done, u + 1)
                if u >= 2:
                    act.wait_ge(hidden_done, u - 1)
                act.activation(silu[:, u % 2, :], gate[:, u % 2, 0:F], ACT.Silu).then_inc(silu_done, 1)
                if u:
                    copy_turned(u - 1)
            copy_turned(len(units) - 1)

        @block.vector
        def _(dve):
            with dve.Fori(0, NB) as b:
                rows = [sh.x_all[:, bass.ds(b * QT + q, 1), :].rearrange("p o d -> p (o d)") for q in range(QT)]
                dve_layernorm(dve, rows, [xn[:, q, :] for q in range(QT)], stats, moments, stats_done,
                              moments_done, rstd_done, normed, LN_EPS, b)
                dve.wait_ge(xT_done, b + 1)

            def add_down(u):
                e, half = units[u]
                dve.wait_ge(down_done, u + 1)
                at = T * (e % 4)
                for j in range(HALF):
                    b = HALF * half + j
                    rows = sh.x_all[at:at + T, QT * b + e // 4, :]
                    dve.tensor_tensor(rows, rows, down[T * j:T * (j + 1), u % 2, 0:D], ALU.add).then_inc(added, 1)

            for u in range(len(units)):
                dve.wait_ge(silu_done, u + 1)
                if u >= 2:
                    dve.wait_ge(turned_done, u - 1)
                dve.tensor_tensor(hidden[:, u % 2, :], silu[:, u % 2, :], up[:, u % 2, 0:F], ALU.mult).then_inc(hidden_done, 1)
                if u:
                    add_down(u - 1)
            add_down(len(units) - 1)
        ph.retire(sh)


def phase_multi_query_inputs(nc, sh):
    F = 512
    C = F // P
    with ExitStack() as ctx:
        ph = Phase(nc, ctx, "l2f")
        ctx_rows = ph.sbuf("ctx_rows", [P, NT, D])
        w1 = ph.sbuf("w1", [P, 2 * F])
        w2 = ph.sbuf("w2", [P, C, D])
        affine = ph.sbuf("affine", [P, 4, D])
        stats = [ph.sbuf(f"stats{i}", [P, QT, 6]) for i in range(3)]
        moments = [ph.sbuf(f"moments{i}", [P, QT, 4]) for i in range(3)]
        x_mid = ph.sbuf("x_mid", [P, QT, D])
        normed_rows = ph.sbuf("normed_rows", [P, 2, QT, D])
        scaled_rows = ph.sbuf("scaled_rows", [P, 2, QT, D])
        affine_rows = ph.sbuf("affine_rows", [P, 2, QT, D])
        rowsT = ph.sbuf("rowsT", [P, S])
        silu = ph.sbuf("silu", [P, QT, F])
        hidden = ph.sbuf("hidden", [P, QT, F])
        hiddenT = ph.sbuf("hiddenT", [P, QT, C, P])
        turned_rows = ph.psum("turned_rows", [P, 2, S])
        up = ph.psum("up", [P, QT, 2, F])
        turned = ph.psum("turned", [P, QT, C, P])
        down = ph.psum("down", [P, 512])
        stats_done = [ph.sem(f"stats_done{i}") for i in range(3)]
        moments_done = [ph.sem(f"moments_done{i}") for i in range(3)]
        rstd_done = [ph.sem(f"rstd_done{i}") for i in range(3)]
        normed = [ph.sem(f"normed{i}") for i in range(3)]
        (w_loaded, scaled, affine_done, rows_turned, rows_copied, up_done, silu_done, hidden_done, hidden_turned,
         hidden_copied, down_done, y_done) = [ph.sem(n) for n in (
             "w_loaded", "scaled", "affine_done", "rows_turned", "rows_copied", "up_done", "silu_done",
             "hidden_done", "hidden_turned", "hidden_copied", "down_done", "y_done")]
        block = ctx.enter_context(nc.Block())

        @block.sync
        def _(sp):
            sp.dma_start(ctx_rows[:, :, :], sh.dram["ctx_1024"].rearrange("b (q p) d -> p (b q) d", p=P)).then_inc(w_loaded, 16)
            sp.dma_start(w1[:, :], sh.dram["L2_xattn_W1"]).then_inc(w_loaded, 16)
            sp.dma_start(w2[:, :, :], sh.dram["L2_xattn_W2"].rearrange("(c p) d -> p c d", p=P)).then_inc(w_loaded, 16)
            for j, n in enumerate(("ln_g", "ln_b", "cln_g", "cln_b")):
                sp.dma_start(affine[:, j, :], sh.dram["L2_xattn_" + n].rearrange("(o d) -> o d", o=1).to_broadcast([P, D])).then_inc(w_loaded, 16)

        @block.gpsimd
        def _(pool):
            clear_retired(pool, sh)
            with pool.Fori(0, NB) as b:
                for i in (0, 2, 1):
                    pool_rstd(pool, sh, moments[i], moments_done[i], rstd_done[i], b)

        @block.tensor
        def _(pe):
            pe.wait_ge(w_loaded, 112)
            with pe.Fori(0, NB) as b:
                pe.wait_ge(affine_done, b + 1)
                for j in range(2):
                    for q in range(QT):
                        last = pe.transpose(turned_rows[:, j, P * q:P * (q + 1)], affine_rows[:, j, q, :], sh.ident[:, :])
                last.then_inc(rows_turned, 1)
                pe.wait_ge(rows_copied, b + 1)
                for q in range(QT):
                    for j in range(2):
                        last = pe.matmul(up[:, q, j, :], rowsT[:, P * q:P * (q + 1)], w1[:, F * j:F * (j + 1)], start=True, stop=True)
                    last.then_inc(up_done, 1)
                for q in range(QT):
                    pe.wait_ge(hidden_done, QT * b + q + 1)
                    for c in range(C):
                        last = pe.transpose(turned[:, q, c, :], hidden[:, q, P * c:P * (c + 1)], sh.ident[:, :])
                    last.then_inc(hidden_turned, 1)
                for q in range(QT):
                    pe.wait_ge(hidden_copied, QT * b + q + 1)
                    for c in range(C):
                        last = pe.matmul(down[:, D * q:D * (q + 1)], hiddenT[:, q, c, :], w2[:, c, :], start=(c == 0), stop=(c == C - 1))
                last.then_inc(down_done, 1)

        @block.scalar
        def _(act):
            with act.Fori(0, NB) as b:
                act.wait_ge(rows_turned, b + 1)
                act.activation(sh.xnT_all[:, bass.ds(b * S, S)], turned_rows[:, 0, :], ACT.Copy)
                act.activation(sh.cnT_all[:, bass.ds(b * S, S)], turned_rows[:, 1, :], ACT.Copy)
                act.activation(rowsT[:, :], turned_rows[:, 0, :], ACT.Copy).then_inc(rows_copied, 1)
                for q in range(QT):
                    act.wait_ge(up_done, QT * b + q + 1)
                    act.activation(silu[:, q, :], up[:, q, 1, :], ACT.Silu).then_inc(silu_done, 1)
                for q in range(QT):
                    act.wait_ge(hidden_turned, QT * b + q + 1)
                    act.activation(hiddenT[:, q, :, :], turned[:, q, :, :], ACT.Copy).then_inc(hidden_copied, 1)

        @block.vector
        def _(dve):
            dve.wait_ge(w_loaded, 112)
            with dve.Fori(0, NB) as b:
                x_rows = [sh.x_all[:, bass.ds(b * QT + q, 1), :].rearrange("p o d -> p (o d)") for q in range(QT)]
                c_rows = [ctx_rows[:, bass.ds(b * QT + q, 1), :].rearrange("p o d -> p (o d)") for q in range(QT)]
                mid = [x_mid[:, q, :] for q in range(QT)]
                dve_layernorm(dve, x_rows, mid, stats[0], moments[0], stats_done[0], moments_done[0], rstd_done[0], normed[0], LN_EPS, b)
                dve_layernorm(dve, c_rows, [normed_rows[:, 1, q, :] for q in range(QT)], stats[2], moments[2],
                              stats_done[2], moments_done[2], rstd_done[2], normed[2], LN_EPS, b)
                dve.wait_ge(normed[0], QT * (b + 1))
                dve_layernorm(dve, mid, [normed_rows[:, 0, q, :] for q in range(QT)], stats[1], moments[1],
                              stats_done[1], moments_done[1], rstd_done[1], normed[1], LN_EPS, b)
                dve.wait_ge(normed[1], QT * (b + 1))
                dve.wait_ge(normed[2], QT * (b + 1))
                for j in range(2):
                    dve.tensor_tensor(scaled_rows[:, j, :, :], normed_rows[:, j, :, :],
                                      affine[:, 2 * j, :].unsqueeze(1).to_broadcast([P, QT, D]), ALU.mult).then_inc(scaled, 1)
                dve.wait_ge(scaled, 2 * (b + 1))
                for j in range(2):
                    last = dve.tensor_tensor(affine_rows[:, j, :, :], scaled_rows[:, j, :, :],
                                             affine[:, 2 * j + 1, :].unsqueeze(1).to_broadcast([P, QT, D]), ALU.add)
                last.then_inc(affine_done, 1)
                for q in range(QT):
                    dve.wait_ge(silu_done, QT * b + q + 1)
                    dve.tensor_tensor(hidden[:, q, :], silu[:, q, :], up[:, q, 0, :], ALU.mult).then_inc(hidden_done, 1)
                dve.wait_ge(down_done, b + 1)
                dve.tensor_copy(sh.y_all[:, bass.ds(b * QT, QT), :], down[:, 0:QT * D].rearrange("p (q d) -> p q d", q=QT)).then_inc(y_done, 1)
        ph.retire(sh)


def phase_routed_ffn(nc, sh):
    E, F = 8, 512
    C = F // P
    STEPS = 10
    with ExitStack() as ctx:
        ph = Phase(nc, ctx, "l2r")
        cent_rows = ph.sbuf("cent_rows", [E, D])
        centT = ph.sbuf("centT", [P, E])
        affine = ph.sbuf("affine", [E, 2, D])
        w1 = ph.sbuf("w1", [P, E, F])
        w2 = ph.sbuf("w2", [P, C, E, D])
        bias1 = ph.sbuf("bias1", [E, F])
        bias2 = ph.sbuf("bias2", [E, D])
        stats = [ph.sbuf(f"stats{i}", [P, QT, 6]) for i in range(2)]
        moments = [ph.sbuf(f"moments{i}", [P, QT, 4]) for i in range(2)]
        x_in = ph.sbuf("x_in", [P, QT, D])
        x_inT = ph.sbuf("x_inT", [P, QT, P])
        xn = ph.sbuf("xn", [P, QT, D])
        logits = ph.sbuf("logits", [P, QT, E])
        top = ph.sbuf("top", [P, QT])
        first = ph.sbuf("first", [P, QT])
        onehot = ph.sbuf("onehot", [P, QT, E])
        onehotT = ph.sbuf("onehotT", [E, QT, P])
        alpha = ph.sbuf("alpha", [P, QT, 3])
        expert_rows = ph.sbuf("expert_rows", [P, QT, E, D])
        expert_rowsT = ph.sbuf("expert_rowsT", [P, QT, E, P])
        relu = ph.sbuf("relu", [P, QT, F])
        reluT = ph.sbuf("reluT", [P, QT, C, P])
        y = ph.sbuf("y", [P, QT, D])
        small = ph.psum("small", [P, 512])
        gathered = ph.psum("gathered", [P, QT, 2, D])
        turned = ph.psum("turned", [P, QT, 4, P])
        up = ph.psum("up", [P, 512])
        down = ph.psum("down", [P, E, D])
        bias_out = ph.psum("bias_out", [P, 512])
        stats_done = [ph.sem(f"stats_done{i}") for i in range(2)]
        moments_done = [ph.sem(f"moments_done{i}") for i in range(2)]
        rstd_done = [ph.sem(f"rstd_done{i}") for i in range(2)]
        normed = [ph.sem(f"normed{i}") for i in range(2)]
        (w_loaded, cent_turned, cent_copied, step, x_turned, x_copied, logits_done, logits_copied, chosen,
         choice_turned, choice_copied, gather_done, exp_done, rows_ready, rows_turned, rows_copied, up_done,
         relu_done, relu_turned, relu_copied, down_done, selected, selected_step, y_done) = [ph.sem(n) for n in (
             "w_loaded", "cent_turned", "cent_copied", "step", "x_turned", "x_copied", "logits_done",
             "logits_copied", "chosen", "choice_turned", "choice_copied", "gather_done", "exp_done",
             "rows_ready", "rows_turned", "rows_copied", "up_done", "relu_done", "relu_turned", "relu_copied",
             "down_done", "selected", "selected_step", "y_done")]
        block = ctx.enter_context(nc.Block())

        @block.sync
        def _(sp):
            sp.dma_start(cent_rows[:, :], sh.dram["L2_ffn_centroids"]).then_inc(w_loaded, 16)
            sp.dma_start(affine[:, 0, :], sh.dram["L2_ffn_ln_g"]).then_inc(w_loaded, 16)
            sp.dma_start(affine[:, 1, :], sh.dram["L2_ffn_ln_b"]).then_inc(w_loaded, 16)
            sp.dma_start(bias1[:, :], sh.dram["L2_ffn_b1"]).then_inc(w_loaded, 16)
            sp.dma_start(bias2[:, :], sh.dram["L2_ffn_b2"]).then_inc(w_loaded, 16)
            sp.dma_start(w1[:, :, :], sh.dram["L2_ffn_w1"].rearrange("e d f -> d e f")).then_inc(w_loaded, 16)
            for c in range(C):
                sp.dma_start(w2[:, c, :, :], sh.dram["L2_ffn_w2"][:, P * c:P * (c + 1), :].rearrange("e f d -> f e d")).then_inc(w_loaded, 16)

        @block.gpsimd
        def _(pool):
            clear_retired(pool, sh)
            with pool.Fori(0, NB) as b:
                for i in range(2):
                    pool_rstd(pool, sh, moments[i], moments_done[i], rstd_done[i], b)

        @block.tensor
        def _(pe):
            pe.wait_ge(w_loaded, 160)
            pe.transpose(small[:, 0:E], cent_rows[:, :], sh.ident[0:E, 0:E]).then_inc(cent_turned, 1)
            pe.wait_ge(cent_copied, 1)
            with pe.Fori(0, NB) as b:
                pe.wait_ge(normed[0], QT * (b + 1))
                for q in range(QT):
                    last = pe.transpose(small[:, P * q:P * (q + 1)], x_in[:, q, :], sh.ident[:, :])
                last.then_inc(x_turned, 1)
                pe.wait_ge(x_copied, b + 1)
                for q in range(QT):
                    last = pe.matmul(small[:, 2 * P + E * q:2 * P + E * (q + 1)], x_inT[:, q, :], centT[:, :], start=True, stop=True)
                last.then_inc(logits_done, 1)
                pe.wait_ge(logits_copied, b + 1)
                pe.wait_ge(chosen, b + 1)
                for q in range(QT):
                    last = pe.transpose(small[0:E, P * q:P * (q + 1)], onehot[:, q, :], sh.ident[:, :])
                last.then_inc(choice_turned, 1)
                pe.wait_ge(choice_copied, b + 1)
                for q in range(QT):
                    pe.matmul(gathered[:, q, :, :], onehotT[:, q, :], affine[:, :, :], start=True, stop=True)
                    last = pe.matmul(bias_out[:, D * q:D * (q + 1)], onehotT[:, q, :], bias2[:, :], start=True, stop=True)
                last.then_inc(gather_done, 1)
                for q in range(QT):
                    pe.wait_ge(rows_ready, QT * b + q + 1)
                    for g in range(2):
                        if (q, g) != (0, 0):
                            pe.wait_ge(rows_copied, 2 * QT * b + 2 * q + g)
                        for j in range(4):
                            last = pe.transpose(turned[:, g, j, :], expert_rows[:, q, 4 * g + j, :], sh.ident[:, :])
                        last.then_inc(rows_turned, 1)
                    pe.wait_ge(rows_copied, 2 * QT * b + 2 * q + 2)
                    if q:
                        pe.wait_ge(relu_done, QT * b + q)
                    for e in range(E):
                        pe.matmul(up[:, :], expert_rowsT[:, q, e, :], w1[:, e, :], start=(e == 0), stop=False)
                    pe.matmul(up[:, :], onehotT[:, q, :], bias1[:, :], start=False, stop=True).then_inc(up_done, 1)
                    pe.wait_ge(relu_done, QT * b + q + 1)
                    for c in range(C):
                        last = pe.transpose(turned[:, 0, c, :], relu[:, q, P * c:P * (c + 1)], sh.ident[:, :])
                    last.then_inc(relu_turned, 1)
                    pe.wait_ge(relu_copied, QT * b + q + 1)
                    if q:
                        pe.wait_ge(selected, QT * b + q)
                    for g in range(2):
                        for c in range(C):
                            last = pe.matmul(down[:, 4 * g:4 * g + 4, :], reluT[:, q, c, :], w2[:, c, 4 * g:4 * g + 4, :],
                                             start=(c == 0), stop=(c == C - 1))
                    last.then_inc(down_done, 1)

        @block.scalar
        def _(act):
            act.wait_ge(cent_turned, 1)
            act.activation(centT[:, :], small[:, 0:E], ACT.Copy).then_inc(cent_copied, 1)
            with act.Fori(0, NB) as b:
                act.wait_ge(x_turned, b + 1)
                act.activation(x_inT[:, :, :], small[:, 0:S].rearrange("p (q t) -> p q t", q=QT), ACT.Copy).then_inc(x_copied, 1)
                act.wait_ge(logits_done, b + 1)
                act.activation(logits[:, :, :], small[:, 2 * P:2 * P + QT * E].rearrange("p (q e) -> p q e", q=QT), ACT.Copy).then_inc(logits_copied, 1)
                act.wait_ge(choice_turned, b + 1)
                act.activation(onehotT[:, :, :], small[0:E, 0:S].rearrange("p (q t) -> p q t", q=QT), ACT.Copy).then_inc(choice_copied, 1)
                act.activation(alpha[:, :, 0], top[:, :], ACT.Exp, scale=-1.0).then_inc(exp_done, 1)
                for q in range(QT):
                    for g in range(2):
                        act.wait_ge(rows_turned, 2 * QT * b + 2 * q + g + 1)
                        act.activation(expert_rowsT[:, q, 4 * g:4 * g + 4, :], turned[:, g, :, :], ACT.Copy).then_inc(rows_copied, 1)
                    act.wait_ge(up_done, QT * b + q + 1)
                    act.activation(relu[:, q, :], up[:, :], ACT.Relu).then_inc(relu_done, 1)
                    act.wait_ge(relu_turned, QT * b + q + 1)
                    act.activation(reluT[:, q, :, :], turned[:, 0, :, :], ACT.Copy).then_inc(relu_copied, 1)

        @block.vector
        def _(dve):
            with dve.Fori(0, NB) as b:
                n = Counter(STEPS)
                rows = [sh.x_all[:, bass.ds(b * QT + q, 1), :].rearrange("p o d -> p (o d)") for q in range(QT)]
                inner = [x_in[:, q, :] for q in range(QT)]
                dve_layernorm(dve, rows, inner, stats[0], moments[0], stats_done[0], moments_done[0], rstd_done[0], normed[0], LN_EPS, b)
                dve.wait_ge(normed[0], QT * (b + 1))
                dve_layernorm(dve, inner, [xn[:, q, :] for q in range(QT)], stats[1], moments[1], stats_done[1],
                              moments_done[1], rstd_done[1], normed[1], LN_EPS, b)
                dve.wait_ge(logits_copied, b + 1)
                dve_choose(dve, sh, logits[:, :, :], top, first, onehot, step, n, b)
                dve.sem_inc(chosen, 1)
                dve.wait_ge(exp_done, b + 1)
                dve.tensor_scalar(alpha[:, :, 1], alpha[:, :, 0], 1.0, None, ALU.add).then_inc(step, n.up())
                dve.wait_ge(step, n.all(b))
                dve.reciprocal(alpha[:, :, 2], alpha[:, :, 1]).then_inc(step, n.up())
                dve.wait_ge(gather_done, b + 1)
                dve.wait_ge(normed[1], QT * (b + 1))
                dve.tensor_tensor(xn[:, :, :], xn[:, :, :], gathered[:, :, 0, :], ALU.mult).then_inc(step, n.up())
                dve.wait_ge(step, n.all(b))
                dve.tensor_tensor(xn[:, :, :], xn[:, :, :], gathered[:, :, 1, :], ALU.add).then_inc(step, n.up())
                dve.wait_ge(step, n.all(b))
                for q in range(QT):
                    for e in range(E):
                        last = dve.tensor_scalar(expert_rows[:, q, e, :], xn[:, q, :], onehot[:, q, e:e + 1], None, ALU.mult)
                    last.then_inc(rows_ready, 1)
                for q in range(QT):
                    dve.wait_ge(down_done, QT * b + q + 1)
                    for e in range(E):
                        before = bias_out[:, D * q:D * (q + 1)] if e == 0 else y[:, q, :]
                        if e == 0:
                            dve.tensor_copy(y[:, q, :], before).then_inc(selected_step, 1)
                            dve.wait_ge(selected_step, (E + 1) * (QT * b + q) + 1)
                        dve.scalar_tensor_tensor(out=y[:, q, :], in0=down[:, e, :], scalar=onehot[:, q, e:e + 1],
                                                 in1=y[:, q, :], op0=ALU.mult, op1=ALU.add).then_inc(selected_step, 1)
                        dve.wait_ge(selected_step, (E + 1) * (QT * b + q) + e + 2)
                    dve.sem_inc(selected, 1)
                for q in range(QT):
                    dve.scalar_tensor_tensor(out=y[:, q, :], in0=y[:, q, :], scalar=alpha[:, q, 2:3],
                                             in1=x_in[:, q, :], op0=ALU.mult, op1=ALU.add).then_inc(y_done, 1)
                dve.wait_ge(y_done, (QT + 1) * b + QT)
                out_rows = sh.x_all[:, bass.ds(b * QT, QT), :]
                dve.tensor_tensor(out_rows, out_rows, y[:, :, :], ALU.add).then_inc(y_done, 1)
                dve.wait_ge(y_done, (QT + 1) * (b + 1))
                n.close()
        ph.retire(sh)


def phase_head_softmax_attention(nc, sh):
    H, DH, U = 8, 16, 4
    with ExitStack() as ctx:
        ph = Phase(nc, ctx, "l3a")
        w_rows = ph.sbuf("w_rows", [P, 4, D])
        wT = ph.sbuf("wT", [P, 4, D])
        stats = ph.sbuf("stats", [P, QT, 6])
        moments = ph.sbuf("moments", [P, QT, 4])
        xn = ph.sbuf("xn", [P, QT, D])
        xnT = ph.sbuf("xnT", [P, S])
        qT = ph.sbuf("qT", [P, S])
        ctx_now = ph.sbuf("ctx_now", [P, S])
        q_head = ph.sbuf("q_head", [P, 2, H, S])
        kT = ph.sbuf("kT", [P, 2, S])
        values = ph.sbuf("values", [P, 2, QT, H, DH])
        largest = ph.sbuf("largest", [P, 2, P])
        lowered = ph.sbuf("lowered", [P, 2, H, P])
        probs = ph.sbuf("probs", [P, 2, H, P])
        total = ph.sbuf("total", [P, 2, P])
        inverse = ph.sbuf("inverse", [P, 2, P])
        shares = ph.sbuf("shares", [P, 2, H, P])
        mixed = ph.sbuf("mixed", [P, QT, D])
        mixedT = ph.sbuf("mixedT", [P, S])
        scores = [ph.psum(f"scores{i}", [P, H, P]) for i in range(2)]
        out_sums = [ph.psum(f"out_sums{i}", [P, 512]) for i in range(QT)]
        front_bank = ph.psum("front_bank", [P, 512])
        tail_bank = ph.psum("tail_bank", [P, 512])
        names = ["w_loaded", "w_turned", "w_copied", "stats_done", "moments_done", "rstd_done",
                 "normed", "front_filled", "front_copied", "ctx_ready", "q_split", "scored", "exp_done",
                 "max_ready", "lowered_ready", "totalled", "inverted", "shared", "summed", "mixed_ready", "tail_filled", "tail_copied"]
        (w_loaded, w_turned, w_copied, stats_done, moments_done, rstd_done, normed, front_filled,
         front_copied, ctx_ready, q_split, scored, exp_done, max_ready, lowered_ready, totalled, inverted, shared, summed, mixed_ready,
         tail_filled, tail_copied) = [ph.sem(n) for n in names]
        block = ctx.enter_context(nc.Block())

        def batches(eng, front, unit, drain, tail):
            front(0, 0, True)

            def one(b, par, first, more):
                for u in range(U):
                    unit(b, par, u, first)
                    if u == 1 and more:
                        front(b + 1, 1 - par, False)
                drain(b, par, first)
                tail(b, par)

            one(0, 0, True, True)
            one(1, 1, True, True)
            with eng.Fori(2, NB - 2, 2) as b:
                one(b, 0, False, True)
                one(b + 1, 1, False, True)
            one(NB - 2, 0, False, True)
            one(NB - 1, 1, False, False)

        @block.sync
        def _(sp):
            for j, n in enumerate(("W_Q", "W_K", "W_V", "W_O")):
                sp.dma_start(w_rows[:, j, :], sh.dram["L3_xattn_" + n]).then_inc(w_loaded, 16)

        @block.gpsimd
        def _(pool):
            clear_retired(pool, sh)
            def front(b, par, first):
                if not first:
                    pool.wait_ge(front_filled, 3 * b)
                pool.tensor_copy(ctx_now[:, :], sh.ctxT[:, bass.ds(b * S, S)]).then_inc(ctx_ready, 1)
                pool_rstd(pool, sh, moments, moments_done, rstd_done, b)

            def share(b, u):
                pool.wait_ge(inverted, U * b + u + 1)
                if not (isinstance(b, int) and b == 0 and u < 2):
                    pool.wait_ge(summed, U * b + u - 1)
                pool.tensor_tensor(shares[:, u % 2, :, :], probs[:, u % 2, :, :],
                                   inverse[:, u % 2, :].unsqueeze(1).to_broadcast([P, H, P]), ALU.mult).then_inc(shared, 1)

            batches(pool, front, lambda b, par, u, first: share(b, u - 1) if u else None,
                    lambda b, par, first: share(b, U - 1), lambda *a: None)

        @block.tensor
        def _(pe):
            pe.wait_ge(w_loaded, 64)
            for j in range(4):
                last = pe.transpose(front_bank[:, P * j:P * (j + 1)], w_rows[:, j, :], sh.ident[:, :])
            last.then_inc(w_turned, 1)
            pe.wait_ge(w_copied, 1)

            def front(b, par, first):
                pe.wait_ge(normed, QT * (b + 1))
                if not first:
                    pe.wait_ge(front_copied, 3 * b)
                for q in range(QT):
                    last = pe.transpose(front_bank[:, P * q:P * (q + 1)], xn[:, q, :], sh.ident[:, :])
                last.then_inc(front_filled, 1)
                pe.wait_ge(front_copied, 3 * b + 1)
                pe.wait_ge(ctx_ready, b + 1)
                pe.matmul(front_bank[:, 0:S], wT[:, 0, :], xnT[:, :], start=True, stop=True)
                pe.matmul(front_bank[:, S:2 * S], wT[:, 1, :], ctx_now[:, :], start=True, stop=True).then_inc(front_filled, 1)
                pe.wait_ge(front_copied, 3 * b + 2)
                for t in range(QT):
                    last = pe.matmul(front_bank[:, D * t:D * (t + 1)], ctx_now[:, P * t:P * (t + 1)], wT[:, 2, :],
                                     start=True, stop=True)
                last.then_inc(front_filled, 1)

            def value_products(b, par, u, first):
                q, t = u // 2, u % 2
                pe.wait_ge(shared, U * b + u + 1)
                if u == 0:
                    pe.wait_ge(front_copied, 3 * b + 3)
                    if not (isinstance(b, int) and b == 0):
                        pe.wait_ge(mixed_ready, QT * b)
                for h in range(H):
                    last = pe.matmul(out_sums[q][:, DH * h:DH * (h + 1)], shares[:, u % 2, h, :], values[:, par, t, h, :],
                                     start=(t == 0 and h == 0), stop=(t == QT - 1), skip_group_check=True)
                last.then_inc(summed, 1)

            def unit(b, par, u, first):
                q, t = u // 2, u % 2
                if u == 0:
                    pe.wait_ge(q_split, b + 1)
                if not (first and par == 0 and u < 2):
                    pe.wait_ge(lowered_ready, U * b + u - 1)
                for g in range(2):
                    last = pe.matmul(scores[u % 2][:, 4 * g:4 * g + 4, :], kT[:, par, P * t:P * (t + 1)],
                                     q_head[:, par, 4 * g:4 * g + 4, P * q:P * (q + 1)], start=True, stop=True)
                last.then_inc(scored, 1)
                if u:
                    value_products(b, par, u - 1, first)

            def tail(b, par):
                pe.wait_ge(mixed_ready, QT * (b + 1))
                for q in range(QT):
                    last = pe.transpose(tail_bank[:, P * q:P * (q + 1)],
                                        mixed[:, q, :], sh.ident[:, :])
                last.then_inc(tail_filled, 1)
                pe.wait_ge(tail_copied, 2 * b + 1)
                for q in range(QT):
                    last = pe.matmul(tail_bank[:, D * q:D * (q + 1)], mixedT[:, P * q:P * (q + 1)], wT[:, 3, :],
                                     start=True, stop=True)
                last.then_inc(tail_filled, 1)

            batches(pe, front, unit, lambda b, par, first: value_products(b, par, U - 1, first), tail)

        @block.scalar
        def _(act):
            act.wait_ge(w_turned, 1)
            act.activation(wT[:, :, :], front_bank[:, :].rearrange("p (j d) -> p j d", j=4), ACT.Copy).then_inc(w_copied, 1)

            def front(b, par, first):
                act.wait_ge(front_filled, 3 * b + 1)
                act.activation(xnT[:, :], front_bank[:, 0:S], ACT.Copy).then_inc(front_copied, 1)
                act.wait_ge(front_filled, 3 * b + 2)
                act.activation(qT[:, :], front_bank[:, 0:S], ACT.Copy, scale=float(DH) ** -0.5)
                act.activation(kT[:, par, :], front_bank[:, S:2 * S], ACT.Copy).then_inc(front_copied, 1)
                act.wait_ge(front_filled, 3 * b + 3)
                act.activation(values[:, par, :, :, :],
                               front_bank[:, 0:S].rearrange("p (t h d) -> p t h d", t=QT, h=H), ACT.Copy).then_inc(front_copied, 1)

            def unit(b, par, u, first):
                act.wait_ge(lowered_ready, U * b + u + 1)
                if not (first and par == 0 and u < 2):
                    act.wait_ge(shared, U * b + u - 1)
                act.activation(probs[:, u % 2, :, :], lowered[:, u % 2, :, :], ACT.Exp).then_inc(exp_done, 1)

            batches(act, front, unit, lambda *a: None, lambda *a: None)

        @block.vector
        def _(dve):
            def front(b, par, first):
                if not first:
                    dve.wait_ge(front_filled, 3 * b - 2)
                rows = [sh.x_all[:, bass.ds(b * QT + q, 1), :].rearrange("p o d -> p (o d)") for q in range(QT)]
                dve_layernorm(dve, rows, [xn[:, q, :] for q in range(QT)], stats, moments, stats_done,
                              moments_done, rstd_done, normed, LN_EPS, b)
                dve.wait_ge(front_copied, 3 * b + 2)
                for h in range(H):
                    last = dve.tensor_scalar(q_head[:, par, h, :], qT[:, :], sh.head16[:, h:h + 1], None, ALU.mult)
                last.then_inc(q_split, 1)

            def sum_heads(b, u):
                dve.wait_ge(exp_done, U * b + u + 1)
                dve.tensor_reduce(total[:, u % 2, :], probs[:, u % 2, :, :].rearrange("p h q -> p q h"), AX.X, ALU.add).then_inc(totalled, 1)
                dve.wait_ge(totalled, U * b + u + 1)
                dve.reciprocal(inverse[:, u % 2, :], total[:, u % 2, :]).then_inc(inverted, 1)

            def unit(b, par, u, first):
                dve.wait_ge(scored, U * b + u + 1)
                dve.tensor_reduce(largest[:, u % 2, :], scores[u % 2][:, :, :].rearrange("p h q -> p q h"), AX.X, ALU.max).then_inc(max_ready, 1)
                dve.wait_ge(max_ready, U * b + u + 1)
                if not (first and par == 0 and u < 2):
                    dve.wait_ge(exp_done, U * b + u - 1)
                dve.tensor_tensor(lowered[:, u % 2, :, :], scores[u % 2][:, :, :],
                                  largest[:, u % 2, :].unsqueeze(1).to_broadcast([P, H, P]), ALU.subtract).then_inc(lowered_ready, 1)
                if u:
                    sum_heads(b, u - 1)

            def tail(b, par):
                dve.wait_ge(summed, U * (b + 1))
                for q in range(QT):
                    dve.tensor_copy(mixed[:, q, :], out_sums[q][:, 0:D]).then_inc(mixed_ready, 1)
                dve.wait_ge(tail_filled, 2 * b + 1)
                dve.tensor_copy(mixedT[:, :], tail_bank[:, 0:S]).then_inc(tail_copied, 1)
                dve.wait_ge(tail_filled, 2 * b + 2)
                rows = sh.x_all[:, bass.ds(b * QT, QT), :]
                dve.tensor_tensor(rows, rows, tail_bank[:, 0:S].rearrange("p (q d) -> p q d", q=QT),
                                  ALU.add).then_inc(tail_copied, 1)

            batches(dve, front, unit, lambda b, par, first: sum_heads(b, U - 1), tail)
        ph.retire(sh)


def phase_hard_expert_ffn(nc, sh):
    E, F = 4, 512
    C = F // P
    LN3_EPS = 1e-12
    STEPS = 6 + 2
    with ExitStack() as ctx:
        ph = Phase(nc, ctx, "l3f")
        router = ph.sbuf("router", [P, E])
        w1 = ph.sbuf("w1", [P, E, F])
        wo = ph.sbuf("wo", [P, C, D])
        bias1 = ph.sbuf("bias1", [E, F])
        bias_out = ph.sbuf("bias_out", [P, 3, D])
        stats = [ph.sbuf(f"stats{i}", [P, QT, 6]) for i in range(2)]
        moments = [ph.sbuf(f"moments{i}", [P, QT, 4]) for i in range(2)]
        x_in = ph.sbuf("x_in", [P, QT, D])
        x_inT = ph.sbuf("x_inT", [P, QT, P])
        logits = ph.sbuf("logits", [P, QT, E])
        top = ph.sbuf("top", [P, QT])
        first = ph.sbuf("first", [P, QT])
        onehot = ph.sbuf("onehot", [P, QT, E])
        onehotT = ph.sbuf("onehotT", [E, QT, P])
        expert_rows = ph.sbuf("expert_rows", [P, QT, E, D])
        expert_rowsT = ph.sbuf("expert_rowsT", [P, QT, E, P])
        gelu = ph.sbuf("gelu", [P, QT, F])
        geluT = ph.sbuf("geluT", [P, QT, C, P])
        y = ph.sbuf("y", [P, QT, D])
        yn = ph.sbuf("yn", [P, QT, D])
        small = ph.psum("small", [P, 512])
        turned = ph.psum("turned", [P, QT, 4, P])
        up = ph.psum("up", [P, QT, 512])
        down = ph.psum("down", [P, 512])
        stats_done = [ph.sem(f"stats_done{i}") for i in range(2)]
        moments_done = [ph.sem(f"moments_done{i}") for i in range(2)]
        rstd_done = [ph.sem(f"rstd_done{i}") for i in range(2)]
        normed = [ph.sem(f"normed{i}") for i in range(2)]
        (w_loaded, step, x_turned, x_copied, logits_done, logits_copied, chosen, choice_turned, choice_copied,
         rows_ready, rows_turned, rows_copied, up_done, gelu_done, gelu_turned, gelu_copied, down_done,
         y_ready, stored) = [ph.sem(n) for n in (
             "w_loaded", "step", "x_turned", "x_copied", "logits_done", "logits_copied", "chosen", "choice_turned",
             "choice_copied", "rows_ready", "rows_turned", "rows_copied", "up_done", "gelu_done", "gelu_turned",
             "gelu_copied", "down_done", "y_ready", "stored")]
        block = ctx.enter_context(nc.Block())

        @block.sync
        def _(sp):
            sp.dma_start(router[:, :], sh.dram["L3_ffn_W_router"]).then_inc(w_loaded, 16)
            sp.dma_start(bias1[:, :], sh.dram["L3_ffn_b1"]).then_inc(w_loaded, 16)
            for j, n in enumerate(("bo", "ln_gamma", "ln_beta")):
                sp.dma_start(bias_out[:, j, :], sh.dram["L3_ffn_" + n].rearrange("(o d) -> o d", o=1).to_broadcast([P, D])).then_inc(w_loaded, 16)
            sp.dma_start(w1[:, :, :], sh.dram["L3_ffn_W1"].rearrange("e d f -> d e f")).then_inc(w_loaded, 16)
            sp.dma_start(wo[:, :, :], sh.dram["L3_ffn_Wo"].rearrange("(c p) d -> p c d", p=P)).then_inc(w_loaded, 16)

        @block.gpsimd
        def _(pool):
            clear_retired(pool, sh)
            with pool.Fori(0, NB) as b:
                for i in range(2):
                    pool_rstd(pool, sh, moments[i], moments_done[i], rstd_done[i], b)

        @block.tensor
        def _(pe):
            pe.wait_ge(w_loaded, 112)
            with pe.Fori(0, NB) as b:
                pe.wait_ge(normed[0], QT * (b + 1))
                for q in range(QT):
                    last = pe.transpose(small[:, P * q:P * (q + 1)], x_in[:, q, :], sh.ident[:, :])
                last.then_inc(x_turned, 1)
                pe.wait_ge(x_copied, b + 1)
                for q in range(QT):
                    last = pe.matmul(small[:, 2 * P + E * q:2 * P + E * (q + 1)], x_inT[:, q, :], router[:, :], start=True, stop=True)
                last.then_inc(logits_done, 1)
                pe.wait_ge(logits_copied, b + 1)
                pe.wait_ge(chosen, b + 1)
                for q in range(QT):
                    last = pe.transpose(small[0:E, P * q:P * (q + 1)], onehot[:, q, :], sh.ident[:, :])
                last.then_inc(choice_turned, 1)
                pe.wait_ge(rows_ready, b + 1)
                for q in range(QT):
                    for e in range(E):
                        last = pe.transpose(turned[:, q, e, :], expert_rows[:, q, e, :], sh.ident[:, :])
                    last.then_inc(rows_turned, 1)
                pe.wait_ge(choice_copied, b + 1)
                for q in range(QT):
                    pe.wait_ge(rows_copied, QT * b + q + 1)
                    for e in range(E):
                        pe.matmul(up[:, q, :], expert_rowsT[:, q, e, :], w1[:, e, :], start=(e == 0), stop=False)
                    pe.matmul(up[:, q, :], onehotT[:, q, :], bias1[:, :], start=False, stop=True).then_inc(up_done, 1)
                for q in range(QT):
                    pe.wait_ge(gelu_done, QT * b + q + 1)
                    for c in range(C):
                        last = pe.transpose(turned[:, q, c, :], gelu[:, q, P * c:P * (c + 1)], sh.ident[:, :])
                    last.then_inc(gelu_turned, 1)
                for q in range(QT):
                    pe.wait_ge(gelu_copied, QT * b + q + 1)
                    for c in range(C):
                        last = pe.matmul(down[:, D * q:D * (q + 1)], geluT[:, q, c, :], wo[:, c, :], start=(c == 0), stop=(c == C - 1))
                last.then_inc(down_done, 1)

        @block.scalar
        def _(act):
            with act.Fori(0, NB) as b:
                act.wait_ge(x_turned, b + 1)
                act.activation(x_inT[:, :, :], small[:, 0:S].rearrange("p (q t) -> p q t", q=QT), ACT.Copy).then_inc(x_copied, 1)
                act.wait_ge(logits_done, b + 1)
                act.activation(logits[:, :, :], small[:, 2 * P:2 * P + QT * E].rearrange("p (q e) -> p q e", q=QT), ACT.Copy).then_inc(logits_copied, 1)
                act.wait_ge(choice_turned, b + 1)
                act.activation(onehotT[:, :, :], small[0:E, 0:S].rearrange("p (q t) -> p q t", q=QT), ACT.Copy).then_inc(choice_copied, 1)
                for q in range(QT):
                    act.wait_ge(rows_turned, QT * b + q + 1)
                    act.activation(expert_rowsT[:, q, :, :], turned[:, q, :, :], ACT.Copy).then_inc(rows_copied, 1)
                for q in range(QT):
                    act.wait_ge(up_done, QT * b + q + 1)
                    act.activation(gelu[:, q, :], up[:, q, :], ACT.Gelu).then_inc(gelu_done, 1)
                for q in range(QT):
                    act.wait_ge(gelu_turned, QT * b + q + 1)
                    act.activation(geluT[:, q, :, :], turned[:, q, :, :], ACT.Copy).then_inc(gelu_copied, 1)

        @block.vector
        def _(dve):
            dve.wait_ge(w_loaded, 112)
            with dve.Fori(0, NB) as b:
                n = Counter(STEPS)
                rows = [sh.x_all[:, bass.ds(b * QT + q, 1), :].rearrange("p o d -> p (o d)") for q in range(QT)]
                inner = [x_in[:, q, :] for q in range(QT)]
                dve_layernorm(dve, rows, inner, stats[0], moments[0], stats_done[0], moments_done[0], rstd_done[0], normed[0], LN_EPS, b)
                dve.wait_ge(logits_copied, b + 1)
                dve_choose(dve, sh, logits[:, :, :], top, first, onehot, step, n, b)
                dve.sem_inc(chosen, 1)
                for q in range(QT):
                    for e in range(E):
                        last = dve.tensor_scalar(expert_rows[:, q, e, :], x_in[:, q, :], onehot[:, q, e:e + 1], None, ALU.mult)
                last.then_inc(rows_ready, 1)
                dve.tensor_tensor(y[:, :, :], x_in[:, :, :], bias_out[:, 0, :].unsqueeze(1).to_broadcast([P, QT, D]), ALU.add).then_inc(y_ready, 1)
                dve.wait_ge(down_done, b + 1)
                dve.wait_ge(y_ready, 3 * b + 1)
                dve.tensor_tensor(y[:, :, :], y[:, :, :], down[:, 0:QT * D].rearrange("p (q d) -> p q d", q=QT), ALU.add).then_inc(y_ready, 1)
                dve.wait_ge(y_ready, 3 * b + 2)
                dve_layernorm(dve, [y[:, q, :] for q in range(QT)], [yn[:, q, :] for q in range(QT)], stats[1], moments[1],
                              stats_done[1], moments_done[1], rstd_done[1], normed[1], LN3_EPS, b)
                dve.wait_ge(normed[1], QT * (b + 1))
                dve.tensor_tensor(yn[:, :, :], yn[:, :, :], bias_out[:, 1, :].unsqueeze(1).to_broadcast([P, QT, D]), ALU.mult).then_inc(step, n.up())
                dve.wait_ge(step, n.all(b))
                dve.tensor_tensor(yn[:, :, :], yn[:, :, :], bias_out[:, 2, :].unsqueeze(1).to_broadcast([P, QT, D]), ALU.add).then_inc(step, n.up())
                dve.wait_ge(step, n.all(b))
                out_rows = sh.x_all[:, bass.ds(b * QT, QT), :]
                dve.tensor_tensor(out_rows, out_rows, yn[:, :, :], ALU.add).then_inc(y_ready, 1)
                dve.wait_ge(y_ready, 3 * (b + 1))
                n.close()
        ph.retire(sh)


INPUTS = [
    "x",
    "ctx_1024",
    "mask_BxS_bf1",
    "mask_BxS_ik0",
    "mask_BxSxS2_ff0",
    "L0_xattn_W_q",
    "L0_xattn_W_k",
    "L0_xattn_W_v",
    "L0_xattn_W_o",
    "L0_ffn_w1",
    "L0_ffn_b1",
    "L0_ffn_w2",
    "L0_ffn_b2",
    "L1_xattn_wq",
    "L1_xattn_wk",
    "L1_xattn_wv",
    "L1_xattn_wo",
    "L1_xattn_bq",
    "L1_xattn_bk",
    "L1_xattn_bv",
    "L1_xattn_bo",
    "L1_ffn_w1",
    "L1_ffn_w3",
    "L1_ffn_w2",
    "L2_xattn_ln_g",
    "L2_xattn_ln_b",
    "L2_xattn_cln_g",
    "L2_xattn_cln_b",
    "L2_xattn_Wq",
    "L2_xattn_Wkv",
    "L2_xattn_Wout",
    "L2_xattn_W1",
    "L2_xattn_W2",
    "L2_ffn_centroids",
    "L2_ffn_ln_g",
    "L2_ffn_ln_b",
    "L2_ffn_w1",
    "L2_ffn_b1",
    "L2_ffn_w2",
    "L2_ffn_b2",
    "L3_xattn_W_Q",
    "L3_xattn_W_K",
    "L3_xattn_W_V",
    "L3_xattn_W_O",
    "L3_ffn_W_router",
    "L3_ffn_W1",
    "L3_ffn_b1",
    "L3_ffn_Wo",
    "L3_ffn_bo",
    "L3_ffn_ln_gamma",
    "L3_ffn_ln_beta",
]


def build(nc, dram, out):
    with ExitStack() as ctx:
        sh = Shared(nc, ctx, dram)
        phase_setup(nc, sh)
        phase_clipped_attention(nc, sh)
        phase_ternary_ffn(nc, sh)
        phase_softmax_attention(nc, sh, False)
        phase_expert_ffn(nc, sh)
        phase_multi_query_inputs(nc, sh)
        phase_softmax_attention(nc, sh, True)
        phase_routed_ffn(nc, sh)
        phase_head_softmax_attention(nc, sh)
        phase_hard_expert_ffn(nc, sh)
        with ExitStack() as end:
            stored = end.enter_context(nc.semaphore("stored"))
            block = end.enter_context(nc.Block())

            @block.sync
            def _(sp):
                sp.dma_start(out.rearrange("b (q p) d -> p (b q) d", p=P), sh.x_all[:, :, :]).then_inc(stored, 16)
                sp.wait_ge(stored, 16)


def kernel(**inputs):
    import numpy as np
    import concourse.bacc as bacc
    from concourse.bass_utils import run_bass_kernel_spmd

    nc = bacc.Bacc("TRN2", target_bir_lowering=False, num_devices=1)
    arrays, dram = {}, {}
    for name in INPUTS:
        a = np.ascontiguousarray(inputs[name])
        if a.dtype == np.bool_:
            a = a.view(np.uint8)
        arrays["in_" + name] = a
        dram[name] = nc.dram_tensor("in_" + name, a.shape, mybir.dt.from_np(a.dtype), kind="ExternalInput").ap()
    shape = (NB, S, D)
    out = nc.dram_tensor("out", shape, F32, kind="ExternalOutput").ap()
    build(nc, dram, out)
    return run_bass_kernel_spmd(nc, [arrays], core_ids=[0]).results[0]["out"]
```

```python
from contextlib import ExitStack

import concourse.bass as bass
from concourse import mybir

F32 = mybir.dt.float32
BF16 = mybir.dt.bfloat16
ALU = mybir.AluOpType
ACT = mybir.ActivationFunctionType
AX = mybir.AxisListType

P = 128
D = 128
NB = 8
S = 256
QT = S // P
NT = NB * QT
LN_EPS = 1e-5
RMS_EPS = 1e-6
QUANT_EPS = 1e-5
ROUND = 1.5 * 2.0 ** 23
MASKED = -1e30
EXP_LOW, EXP_HIGH = 1.9287498479639178e-22, 5.184705528587072e21


class Shared:

    def __init__(self, nc, ctx, dram):
        self.dram = dram
        self.retired_ctx, self.retired = ExitStack(), []
        self.x_all = ctx.enter_context(nc.sbuf_tensor("x_all", [P, NT, D], F32))
        self.ctxT = ctx.enter_context(nc.sbuf_tensor("ctxT", [P, NB * S], F32))
        self.ident = ctx.enter_context(nc.sbuf_tensor("ident", [P, P], F32))
        self.ident_bf = ctx.enter_context(nc.sbuf_tensor("ident_bf", [P, P], BF16))
        self.tri = ctx.enter_context(nc.sbuf_tensor("tri", [P, P], F32))
        self.ones = ctx.enter_context(nc.sbuf_tensor("ones", [P, P], F32))
        self.half = ctx.enter_context(nc.sbuf_tensor("half", [P, 4], F32))
        self.head8 = ctx.enter_context(nc.sbuf_tensor("head8", [P, 16], F32))
        self.head16 = ctx.enter_context(nc.sbuf_tensor("head16", [P, 8], F32))
        self.key_index = ctx.enter_context(nc.sbuf_tensor("key_index", [P, S], F32))
        self.expert_index = ctx.enter_context(nc.sbuf_tensor("expert_index", [P, 8], F32))
        self.query_mask = ctx.enter_context(nc.sbuf_tensor("query_mask", [P, NT], F32))
        self.last_patch = ctx.enter_context(nc.sbuf_tensor("last_patch", [P, NT], F32))
        self.xnT_all = ctx.enter_context(nc.sbuf_tensor("xnT_all", [P, NB * S], F32))
        self.cnT_all = ctx.enter_context(nc.sbuf_tensor("cnT_all", [P, NB * S], F32))
        self.y_all = ctx.enter_context(nc.sbuf_tensor("y_all", [P, NT, D], F32))


class Phase:

    def __init__(self, nc, ctx, name):
        self.nc, self.ctx, self.name = nc, ctx, name
        self.sem_ctx, self.sems = ExitStack(), []

    def sbuf(self, name, shape, dtype=F32):
        return self.ctx.enter_context(self.nc.sbuf_tensor(f"{self.name}_{name}", shape, dtype, align_bytes=64))

    def psum(self, name, shape, dtype=F32):
        return self.ctx.enter_context(self.nc.psum_tensor(f"{self.name}_{name}", shape, dtype))

    def sem(self, name):
        s = self.sem_ctx.enter_context(self.nc.semaphore(f"{self.name}_{name}"))
        self.sems.append(s)
        return s

    def retire(self, sh):
        sh.retired_ctx.close()
        sh.retired_ctx, sh.retired = self.sem_ctx, self.sems


def clear_retired(pool, sh):
    for s in sh.retired:
        pool.sem_clear(s)


class Counter:

    def __init__(self, per_batch):
        self.per_batch, self.n = per_batch, 0

    def up(self):
        self.n += 1
        return 1

    def all(self, b):
        return self.per_batch * b + self.n

    def close(self):
        assert self.n == self.per_batch, (self.n, self.per_batch)


def dve_choose(dve, sh, logits, top, first, onehot, step, n, b):
    E = logits.shape[2]
    index = sh.expert_index[:, 0:E].unsqueeze(1).to_broadcast([P, QT, E])
    dve.tensor_reduce(top[:, :], logits, AX.X, ALU.max).then_inc(step, n.up())
    dve.wait_ge(step, n.all(b))
    dve.tensor_tensor(onehot[:, :, :], logits, top[:, :].unsqueeze(2).to_broadcast([P, QT, E]), ALU.is_lt).then_inc(step, n.up())
    dve.wait_ge(step, n.all(b))
    dve.tensor_scalar(onehot[:, :, :], onehot[:, :, :], 16.0, None, ALU.mult).then_inc(step, n.up())
    dve.wait_ge(step, n.all(b))
    dve.tensor_tensor(onehot[:, :, :], onehot[:, :, :], index, ALU.add).then_inc(step, n.up())
    dve.wait_ge(step, n.all(b))
    dve.tensor_reduce(first[:, :], onehot[:, :, :], AX.X, ALU.min).then_inc(step, n.up())
    dve.wait_ge(step, n.all(b))
    dve.tensor_tensor(onehot[:, :, :], index, first[:, :].unsqueeze(2).to_broadcast([P, QT, E]), ALU.is_equal).then_inc(step, n.up())
    dve.wait_ge(step, n.all(b))


def phase_setup(nc, sh):
    with ExitStack() as ctx:
        ph = Phase(nc, ctx, "setup")
        ctx_rows = ph.sbuf("ctx_rows", [P, NT, D])
        mask_u8 = ph.sbuf("mask_u8", [P, NT], mybir.dt.uint8)
        mask_i32 = ph.sbuf("mask_i32", [P, NT], mybir.dt.int32)
        steps = ph.sbuf("steps", [P, NT])
        turned = [ph.psum(f"turned{i}", [P, 4, P]) for i in range(2)]
        sums = ph.psum("sums", [P, 512])
        loaded = ph.sem("loaded")
        masks_loaded = ph.sem("masks_loaded")
        blank = ph.sem("blank")
        consts = ph.sem("consts")
        steps_ready = ph.sem("steps_ready")
        sums_done = ph.sem("sums_done")
        turned_done = ph.sem("turned_done")
        turned_copied = ph.sem("turned_copied")
        block = ctx.enter_context(nc.Block())

        @block.sync
        def _(sp):
            sp.dma_start(ctx_rows[:, :, :], sh.dram["ctx_1024"].rearrange("b (q p) d -> p (b q) d", p=P)).then_inc(loaded, 16)
            sp.dma_start(sh.x_all[:, :, :], sh.dram["x"].rearrange("b (q p) d -> p (b q) d", p=P)).then_inc(loaded, 16)
            with nc.allow_non_contiguous_dma(reason="mask columns"):
                sp.dma_start(mask_u8[:, :], sh.dram["mask_BxS_bf1"].rearrange("b (q p) -> p (b q)", p=P)).then_inc(masks_loaded, 16)
                sp.dma_start(mask_i32[:, :], sh.dram["mask_BxS_ik0"].rearrange("b (q p) -> p (b q)", p=P)).then_inc(masks_loaded, 16)

        @block.gpsimd
        def _(pool):
            clear_retired(pool, sh)
            pool.memset(sh.ident[:, :], 0.0).then_inc(blank, 1)
            pool.memset(sh.ones[:, :], 1.0).then_inc(blank, 1)
            pool.memset(sh.tri[:, :], 1.0).then_inc(blank, 1)
            pool.memset(sh.head8[:, :], 1.0).then_inc(blank, 1)
            pool.memset(sh.head16[:, :], 1.0).then_inc(blank, 1)
            pool.memset(sh.half[:, :], -0.5).then_inc(blank, 1)
            pool.wait_ge(blank, 6)
            pool.affine_select(out=sh.ident[:, :], in_=sh.ident[:, :], compare_op=ALU.not_equal, fill=1.0,
                               base=0, pattern=[[-1, P]], channel_multiplier=1).then_inc(consts, 1)
            pool.affine_select(out=sh.tri[:, :], in_=sh.tri[:, :], compare_op=ALU.is_ge, fill=0.0,
                               base=0, pattern=[[1, P]], channel_multiplier=-1).then_inc(consts, 1)
            pool.affine_select(out=sh.head8[:, :], in_=sh.head8[:, :], compare_op=ALU.is_ge, fill=0.0,
                               base=0, pattern=[[-8, 16]], channel_multiplier=1).then_inc(consts, 1)
            pool.affine_select(out=sh.head16[:, :], in_=sh.head16[:, :], compare_op=ALU.is_ge, fill=0.0,
                               base=0, pattern=[[-16, 8]], channel_multiplier=1).then_inc(consts, 1)
            pool.iota(sh.key_index[:, :], [[1, S]], base=0, channel_multiplier=0,
                      allow_small_or_imprecise_dtypes=True).then_inc(consts, 1)
            pool.iota(sh.expert_index[:, :], [[1, 8]], base=0, channel_multiplier=0,
                      allow_small_or_imprecise_dtypes=True).then_inc(consts, 1)
            pool.wait_ge(consts, 6)
            pool.affine_select(out=sh.head8[:, :], in_=sh.head8[:, :], compare_op=ALU.is_ge, fill=0.0,
                               base=7, pattern=[[8, 16]], channel_multiplier=-1).then_inc(consts, 1)
            pool.affine_select(out=sh.head16[:, :], in_=sh.head16[:, :], compare_op=ALU.is_ge, fill=0.0,
                               base=15, pattern=[[16, 8]], channel_multiplier=-1).then_inc(consts, 1)
            pool.tensor_copy(sh.ident_bf[:, :], sh.ident[:, :]).then_inc(consts, 1)

        @block.tensor
        def _(pe):
            pe.wait_ge(consts, 6)
            pe.wait_ge(steps_ready, 2)
            pe.matmul(sums[:, 0:NT], sh.tri[:, :], steps[:, :], start=True, stop=True)
            pe.matmul(sums[:, NT:2 * NT], sh.ones[:, :], steps[:, :], start=True, stop=True).then_inc(sums_done, 1)
            pe.wait_ge(loaded, 32)
            for g in range(NT // 4):
                if g >= 2:
                    pe.wait_ge(turned_copied, g - 1)
                for j in range(4):
                    last = pe.transpose(turned[g % 2][:, j, :], ctx_rows[:, 4 * g + j, :], sh.ident[:, :])
                last.then_inc(turned_done, 1)

        @block.scalar
        def _(act):
            for g in range(NT // 4):
                act.wait_ge(turned_done, g + 1)
                act.activation(sh.ctxT[:, 512 * g:512 * (g + 1)].rearrange("p (a b) -> p a b", a=4),
                               turned[g % 2][:, :, :], ACT.Copy).then_inc(turned_copied, 1)

        @block.vector
        def _(dve):
            dve.wait_ge(masks_loaded, 32)
            dve.tensor_copy(sh.query_mask[:, :], mask_u8[:, :]).then_inc(steps_ready, 1)
            dve.tensor_copy(steps[:, :], mask_i32[:, :]).then_inc(steps_ready, 1)
            dve.wait_ge(sums_done, 1)
            dve.tensor_copy(sh.last_patch[:, :], sums[:, 0:NT]).then_inc(steps_ready, 1)
            dve.wait_ge(steps_ready, 3)
            odd = sh.last_patch[:, :].rearrange("p (b q) -> p b q", q=QT)[:, :, 1]
            even_total = sums[:, NT:2 * NT].rearrange("p (b q) -> p b q", q=QT)[:, :, 0]
            dve.tensor_tensor(odd, odd, even_total, ALU.add).then_inc(steps_ready, 1)

        ph.retire(sh)


def dve_moments(dve, src, stats, moments, stats_done, moments_done, eps, b):
    for q in range(QT):
        dve.bn_stats(stats[:, q, :], src[q]).then_inc(stats_done, 1)
    dve.wait_ge(stats_done, (QT + 1) * b + QT)
    dve.sem_inc(stats_done, 1)
    for q in range(QT):
        dve.bn_aggr(moments[:, q, 0:2], stats[:, q, :]).then_inc(moments_done, 1)
    dve.wait_ge(moments_done, (QT + 1) * b + QT)
    dve.tensor_scalar(moments[:, :, 2:3], moments[:, :, 1:2], eps, None, ALU.add).then_inc(moments_done, 1)


def dve_normalise(dve, src, out, moments, rstd_done, normed, b):
    dve.wait_ge(rstd_done, b + 1)
    for q in range(QT):
        dve.tensor_scalar(out[q], src[q], moments[:, q, 0:1], moments[:, q, 3:4],
                          ALU.subtract, ALU.mult).then_inc(normed, 1)


def dve_layernorm(dve, src, out, stats, moments, stats_done, moments_done, rstd_done, normed, eps, b):
    dve_moments(dve, src, stats, moments, stats_done, moments_done, eps, b)
    dve_normalise(dve, src, out, moments, rstd_done, normed, b)


def pool_rstd(pool, sh, moments, moments_done, rstd_done, b):
    pool.wait_ge(moments_done, (QT + 1) * (b + 1))
    pool.tensor_tensor(moments[:, :, 3:4], moments[:, :, 2:3], sh.half[:, 0:QT].rearrange("p (q o) -> p q o", o=1),
                       ALU.pow).then_inc(rstd_done, 1)


class Stacks:

    def __init__(self, ph, heads, width):
        self.heads, self.width = heads, width
        pairs = [(i, j) for i in range(3) for j in range(3)]
        if len(pairs) * width > P:
            pairs = [(i, j) for i, j in pairs if i + j <= 2]
        self.counts = [sum(1 for first, _ in pairs if first == i) for i in range(3)]
        self.LOADS = len(pairs) + 3
        self.rows = len(pairs) * width
        self.exact = ph.sbuf("exact", [P, 2, S])
        self.rest = ph.sbuf("rest", [P, 2, S])
        self.parts = ph.sbuf("parts", [P, 2, 3, S], BF16)
        self.stacked = ph.sbuf("stacked", [self.rows, 2, 2, heads, S], BF16)
        self.bounce = ph.nc.dram_tensor(f"{ph.name}_bounce", [2, 3, P, S], BF16, kind="Internal").ap()
        self.split = ph.sem("split")
        self.stored = ph.sem("stored")
        self.stacked_ready = ph.sem("stacked_ready")
        self.free = ph.sem("free")

    def split_parts(self, dve, b):
        parts, rest = self.parts, self.rest
        dve.tensor_copy(parts[:, :, 0, :], self.exact[:, :, :]).then_inc(self.split, 1)
        dve.wait_ge(self.split, 4 * b + 1)
        dve.tensor_tensor(rest[:, :, :], self.exact[:, :, :], parts[:, :, 0, :], ALU.subtract).then_inc(self.split, 1)
        dve.wait_ge(self.split, 4 * b + 2)
        dve.tensor_copy(parts[:, :, 1, :], rest[:, :, :]).then_inc(self.split, 1)
        dve.wait_ge(self.split, 4 * b + 3)
        dve.tensor_tensor(parts[:, :, 2, :], rest[:, :, :], parts[:, :, 1, :], ALU.subtract).then_inc(self.split, 1)

    def load(self, sp, b, par):
        sp.wait_ge(self.split, 4 * (b + 1))
        sp.dma_start(self.bounce.rearrange("s a p t -> p (s a) t"),
                     self.parts[:, :, :, :].rearrange("p s a t -> p (s a) t")).then_inc(self.stored, 16)
        sp.wait_ge(self.stored, 16 * (b + 1))
        row, width = 0, self.width
        for i, count in enumerate(self.counts):
            query_part = self.bounce[0, i, :, :].rearrange("(d h) t -> d h t", h=self.heads)
            key_parts = self.bounce[1, 0:count, :, :].rearrange("a (d h) t -> (a d) h t", h=self.heads)
            sp.dma_start(self.stacked[row:row + width * count, par, 1, :, :], key_parts).then_inc(self.stacked_ready, 16)
            for _ in range(count):
                sp.dma_start(self.stacked[row:row + width, par, 0, :, :], query_part).then_inc(self.stacked_ready, 16)
                row += width


def phase_clipped_attention(nc, sh):
    H, DH, G, U = 16, 8, 4, 8
    STEPS = 4
    W = P // G
    with ExitStack() as ctx:
        ph = Phase(nc, ctx, "l0a")
        w_rows = ph.sbuf("w_rows", [P, 4, D])
        wT = ph.sbuf("wT", [P, 4, D])
        stats = ph.sbuf("stats", [P, QT, 6])
        moments = ph.sbuf("moments", [P, QT, 4])
        xn = ph.sbuf("xn", [P, QT, D])
        xnT = ph.sbuf("xnT", [P, S])
        ctx_now = ph.sbuf("ctx_now", [P, S])
        stacks = Stacks(ph, H, DH)
        v_one = ph.sbuf("v_one", [P, 2, QT, H, W])
        probs = ph.sbuf("probs", [P, 2, G, S])
        outT = ph.sbuf("outT", [P, G, S])
        inverse = ph.sbuf("inverse", [P, QT, H])
        mixed = ph.sbuf("mixed", [P, QT, H, DH])
        mixedT = ph.sbuf("mixedT", [P, S])
        scores = [ph.psum(f"scores{i}", [P, G, S]) for i in range(2)]
        out_sums = ph.psum("out_sums", [P, G, S])
        front_bank = ph.psum("front_bank", [P, 512])
        tail_bank = ph.psum("tail_bank", [P, 512])
        (w_loaded, w_turned, w_copied, ones_set, stats_done, moments_done, rstd_done, normed, front_filled,
         front_copied, ctx_ready, scored, exp_done, clipped, summed, out_copied, inverted, mixed_ready,
         tail_filled, tail_copied) = [ph.sem(n) for n in (
             "w_loaded", "w_turned", "w_copied", "ones_set", "stats_done", "moments_done", "rstd_done", "normed",
             "front_filled", "front_copied", "ctx_ready", "scored", "exp_done", "clipped", "summed", "out_copied",
             "inverted", "mixed_ready", "tail_filled", "tail_copied")]
        block = ctx.enter_context(nc.Block())

        def run(eng, front, unit, finish, tail):
            def one(b, par, first, more):
                for u in range(U):
                    unit(b, par, u, first)
                    if u < STEPS and more:
                        front(b + 1, 1 - par, False, u)
                    if 2 <= u < 2 + STEPS and not first:
                        tail(b - 1, 1 - par, u - 2)

            for step in range(STEPS):
                front(0, 0, True, step)
            one(0, 0, True, True)
            one(1, 1, False, True)
            with eng.Fori(2, NB - 2, 2) as b:
                one(b, 0, False, True)
                one(b + 1, 1, False, True)
            one(NB - 2, 0, False, True)
            one(NB - 1, 1, False, False)
            finish(NB - 1, 1)
            for step in range(STEPS):
                tail(NB - 1, 1, step)

        def nothing(*args):
            pass

        @block.sync
        def _(sp):
            for j, n in enumerate(("W_q", "W_k", "W_v", "W_o")):
                sp.dma_start(w_rows[:, j, :], sh.dram["L0_xattn_" + n]).then_inc(w_loaded, 16)

            def front(b, par, first, step):
                if step:
                    return
                if not first:
                    sp.wait_ge(stacks.stacked_ready, 16 * stacks.LOADS * b)
                    sp.sem_inc(stacks.free, 1)
                if not (isinstance(b, int) and b < 2):
                    sp.wait_ge(scored, U * (b - 1))
                    sp.sem_inc(stacks.free, 1)
                stacks.load(sp, b, par)

            run(sp, front, nothing, nothing, nothing)

        @block.gpsimd
        def _(pool):
            clear_retired(pool, sh)
            pool.memset(v_one[:, :, :, :, :], 0.0).then_inc(ones_set, 1)
            pool.wait_ge(ones_set, 1)
            pool.memset(v_one[:, :, :, :, DH:DH + 1], 1.0).then_inc(ones_set, 1)

            def front(b, par, first, step):
                if step:
                    return
                if not first:
                    pool.wait_ge(front_filled, 3 * b)
                pool.tensor_copy(ctx_now[:, :], sh.ctxT[:, bass.ds(b * S, S)]).then_inc(ctx_ready, 1)
                pool_rstd(pool, sh, moments, moments_done, rstd_done, b)

            run(pool, front, nothing, nothing, nothing)

        @block.tensor
        def _(pe):
            pe.wait_ge(w_loaded, 64)
            for j in range(4):
                last = pe.transpose(front_bank[:, P * j:P * (j + 1)], w_rows[:, j, :], sh.ident[:, :])
            last.then_inc(w_turned, 1)
            pe.wait_ge(w_copied, 1)

            def front(b, par, first, step):
                if step == 1:
                    pe.wait_ge(normed, QT * (b + 1))
                    if not first:
                        pe.wait_ge(front_copied, 3 * b)
                    for q in range(QT):
                        last = pe.transpose(front_bank[:, P * q:P * (q + 1)], xn[:, q, :], sh.ident[:, :])
                    last.then_inc(front_filled, 1)
                elif step == 2:
                    pe.wait_ge(front_copied, 3 * b + 1)
                    pe.wait_ge(ctx_ready, b + 1)
                    pe.matmul(front_bank[:, 0:S], wT[:, 0, :], xnT[:, :], start=True, stop=True)
                    pe.matmul(front_bank[:, S:2 * S], wT[:, 1, :], ctx_now[:, :], start=True, stop=True).then_inc(front_filled, 1)
                elif step == 3:
                    pe.wait_ge(front_copied, 3 * b + 2)
                    for t in range(QT):
                        last = pe.matmul(front_bank[:, D * t:D * (t + 1)], ctx_now[:, P * t:P * (t + 1)], wT[:, 2, :],
                                         start=True, stop=True)
                    last.then_inc(front_filled, 1)

            def value_products(b, par, u):
                g, t = u // 2, u % 2
                pe.wait_ge(clipped, U * b + u + 1)
                if u == 0:
                    pe.wait_ge(front_copied, 3 * b + 3)
                if u in (0, 4) and not (isinstance(b, int) and b == 0):
                    pe.wait_ge(out_copied, 2 * b - 1 + u // 4)
                for j in range(G):
                    last = pe.matmul(out_sums[W * j:W * (j + 1), g, :], v_one[:, par, t, G * g + j, :],
                                     probs[:, u % 2, j, :], start=(t == 0), stop=(t == QT - 1))
                last.then_inc(summed, 1)

            def unit(b, par, u, first):
                g, t = u // 2, u % 2
                if u == 0:
                    pe.wait_ge(stacks.stacked_ready, 16 * stacks.LOADS * (b + 1))
                if not (first and u < 2):
                    pe.wait_ge(exp_done, U * b + u - 1)
                for j in range(G):
                    h = G * g + j
                    last = pe.matmul(scores[u % 2][:, j, :], stacks.stacked[:, par, 1, h, P * t:P * (t + 1)],
                                     stacks.stacked[:, par, 0, h, :], start=True, stop=True)
                last.then_inc(scored, 1)
                if u:
                    value_products(b, par, u - 1)
                elif not first:
                    value_products(b - 1, 1 - par, U - 1)

            def tail(b, par, step):
                if step < QT:
                    if step:
                        pe.wait_ge(mixed_ready, QT * b + step)
                    else:
                        pe.wait_ge(out_copied, 2 * (b + 1))
                        if not (isinstance(b, int) and b == 0):
                            pe.wait_ge(tail_copied, 2 * b)
                    for g in range(G):
                        last = pe.transpose(tail_bank[:, P * g:P * (g + 1)], outT[:, g, P * step:P * (step + 1)], sh.ident[:, :])
                    last.then_inc(tail_filled, 1)
                elif step == 2:
                    pe.wait_ge(mixed_ready, QT * (b + 1))
                    for q in range(QT):
                        last = pe.transpose(tail_bank[:, P * q:P * (q + 1)],
                                            mixed[:, q, :, :].rearrange("p h d -> p (h d)"), sh.ident[:, :])
                    last.then_inc(tail_filled, 1)
                else:
                    pe.wait_ge(tail_copied, 2 * b + 1)
                    for q in range(QT):
                        last = pe.matmul(tail_bank[:, D * q:D * (q + 1)], mixedT[:, P * q:P * (q + 1)], wT[:, 3, :],
                                         start=True, stop=True)
                    last.then_inc(tail_filled, 1)

            run(pe, front, unit, lambda b, par: value_products(b, par, U - 1), tail)

        @block.scalar
        def _(act):
            act.wait_ge(w_turned, 1)
            act.activation(wT[:, 0:2, :].rearrange("p j (d h) -> p j d h", h=H),
                           front_bank[:, 0:2 * P].rearrange("p (j h d) -> p j d h", j=2, h=H), ACT.Copy)
            act.activation(wT[:, 2:4, :], front_bank[:, 2 * P:4 * P].rearrange("p (j d) -> p j d", j=2), ACT.Copy).then_inc(w_copied, 1)
            act.wait_ge(ones_set, 2)

            def front(b, par, first, step):
                if step == 0:
                    return
                act.wait_ge(front_filled, 3 * b + step)
                if step == 1:
                    act.activation(xnT[:, :], front_bank[:, 0:S], ACT.Copy).then_inc(front_copied, 1)
                elif step == 2:
                    if not first:
                        act.wait_ge(stacks.split, 4 * b)
                    act.activation(stacks.exact[:, 0, :], front_bank[:, 0:S], ACT.Copy, scale=float(DH) ** -0.5)
                    act.activation(stacks.exact[:, 1, :], front_bank[:, S:2 * S], ACT.Copy).then_inc(front_copied, 1)
                else:
                    act.activation(v_one[:, par, :, :, 0:DH],
                                   front_bank[:, 0:S].rearrange("p (t h d) -> p t h d", t=QT, h=H), ACT.Copy).then_inc(front_copied, 1)

            def copy_out(b, half):
                act.wait_ge(summed, U * b + 4 * (half + 1))
                if not (isinstance(b, int) and b == 0):
                    act.wait_ge(tail_filled, 4 * b - 2)
                act.activation(outT[:, 2 * half:2 * half + 2, :], out_sums[:, 2 * half:2 * half + 2, :], ACT.Copy).then_inc(out_copied, 1)

            def unit(b, par, u, first):
                act.wait_ge(scored, U * b + u + 1)
                if not (first and u < 2):
                    act.wait_ge(summed, U * b + u - 1)
                act.activation(probs[:, u % 2, :, :], scores[u % 2][:, :, :], ACT.Exp).then_inc(exp_done, 1)
                if u == 5:
                    copy_out(b, 0)
                if u == 1 and not first:
                    copy_out(b - 1, 1)

            run(act, front, unit, lambda b, par: copy_out(b, 1), nothing)

        @block.vector
        def _(dve):
            def front(b, par, first, step):
                if step == 0:
                    if not first:
                        dve.wait_ge(front_filled, 3 * b - 2)
                    rows = [sh.x_all[:, bass.ds(b * QT + q, 1), :].rearrange("p o d -> p (o d)") for q in range(QT)]
                    dve_layernorm(dve, rows, [xn[:, q, :] for q in range(QT)], stats, moments, stats_done,
                                  moments_done, rstd_done, normed, LN_EPS, b)
                elif step == 2:
                    dve.wait_ge(front_copied, 3 * b + 2)
                    if not first:
                        dve.wait_ge(stacks.stored, 16 * b)
                    stacks.split_parts(dve, b)

            def unit(b, par, u, first):
                dve.wait_ge(exp_done, U * b + u + 1)
                buf = probs[:, u % 2, :, :]
                dve.tensor_scalar(buf, buf, EXP_LOW, EXP_HIGH, ALU.max, ALU.min).then_inc(clipped, 1)

            def tail(b, par, step):
                sums = tail_bank[:, :].rearrange("p (h w) -> p h w", w=W)
                dve.wait_ge(tail_filled, 4 * b + step + 1)
                if step < QT:
                    q = step
                    dve.reciprocal(inverse[:, q, :], sums[:, :, DH]).then_inc(inverted, 1)
                    dve.wait_ge(inverted, 2 * (QT * b + q) + 1)
                    dve.tensor_scalar(inverse[:, q, :], inverse[:, q, :],
                                      sh.query_mask[:, bass.ds(b * QT + q, 1)], None, ALU.mult).then_inc(inverted, 1)
                    dve.wait_ge(inverted, 2 * (QT * b + q) + 2)
                    dve.tensor_tensor(mixed[:, q, :, :], sums[:, :, 0:DH],
                                      inverse[:, q, :].unsqueeze(2).to_broadcast([P, H, DH]), ALU.mult).then_inc(mixed_ready, 1)
                elif step == 2:
                    dve.tensor_copy(mixedT[:, :], tail_bank[:, 0:S]).then_inc(tail_copied, 1)
                else:
                    rows = sh.x_all[:, bass.ds(b * QT, QT), :]
                    dve.tensor_tensor(rows, rows, tail_bank[:, 0:S].rearrange("p (q d) -> p q d", q=QT),
                                      ALU.add).then_inc(tail_copied, 1)

            run(dve, front, unit, nothing, tail)
        ph.retire(sh)


def dve_quantise(dve, rows, width, rms, rounded, quant, deq, w_mean, step, n, row_sum, root, quantised, b):
    dve.tensor_reduce(rms[:, :, 3], rows[:, :, :], AX.X, ALU.max, apply_absolute_value=True).then_inc(step, n.up())
    dve.wait_ge(step, n.all(b))
    dve.tensor_scalar(rms[:, :, 0], rms[:, :, 2], 1.0 / width, RMS_EPS, ALU.mult, ALU.add).then_inc(row_sum, 1)
    dve.wait_ge(root, b + 1)
    dve.tensor_tensor(rms[:, :, 2], rms[:, :, 3], rms[:, :, 1], ALU.mult).then_inc(step, n.up())
    for q in range(QT):
        dve.tensor_scalar(rounded[:, q, :], rows[:, q, :], rms[:, q, 1:2], None, ALU.mult).then_inc(step, n.up())
    dve.wait_ge(step, n.all(b))
    dve.tensor_scalar(rms[:, :, 2], rms[:, :, 2], QUANT_EPS, None, ALU.max).then_inc(step, n.up())
    dve.wait_ge(step, n.all(b))
    dve.reciprocal(rms[:, :, 3], rms[:, :, 2]).then_inc(step, n.up())
    dve.tensor_scalar(deq[:, :], rms[:, :, 2], w_mean, 1.0 / 127.0, ALU.mult, ALU.mult).then_inc(step, n.up())
    dve.wait_ge(step, n.all(b))
    dve.tensor_scalar(rms[:, :, 3], rms[:, :, 3], 127.0, None, ALU.mult).then_inc(step, n.up())
    dve.wait_ge(step, n.all(b))
    for q in range(QT):
        dve.tensor_scalar(rounded[:, q, :], rounded[:, q, :], rms[:, q, 3:4], ROUND, ALU.mult, ALU.add).then_inc(step, n.up())
    dve.wait_ge(step, n.all(b))
    dve.tensor_scalar(rounded[:, :, :], rounded[:, :, :], ROUND, -128.0, ALU.subtract, ALU.max).then_inc(step, n.up())
    dve.wait_ge(step, n.all(b))
    dve.tensor_scalar(quant[:, :, :], rounded[:, :, :], 127.0, None, ALU.min).then_inc(quantised, 1)


def phase_ternary_ffn(nc, sh):
    F = 512
    C = F // P
    STEPS = 2 + 2 * 11
    with ExitStack() as ctx:
        ph = Phase(nc, ctx, "l0f")
        step = ph.sem("step")
        w1_rows = ph.sbuf("w1_rows", [P, C, D])
        w2_rows = ph.sbuf("w2_rows", [P, F])
        magnitude = ph.sbuf("magnitude", [P, 2])
        w_scale = ph.sbuf("w_scale", [P, 2, 2])
        w_round = ph.sbuf("w_round", [P, 2, F])
        w_tern = ph.sbuf("w_tern", [P, 2, F], BF16)
        w1q = ph.sbuf("w1q", [P, F], BF16)
        w2q = ph.sbuf("w2q", [P, C, D], BF16)
        bias1 = ph.sbuf("bias1", [P, F])
        bias2 = ph.sbuf("bias2", [P, D])
        stats = ph.sbuf("stats", [P, QT, 6])
        moments = ph.sbuf("moments", [P, QT, 4])
        xn = ph.sbuf("xn", [P, QT, D])
        squares = ph.sbuf("squares", [P, QT, F])
        rms1 = ph.sbuf("rms1", [P, QT, 4])
        rms2 = ph.sbuf("rms2", [P, QT, 4])
        deq1 = ph.sbuf("deq1", [P, QT])
        deq2 = ph.sbuf("deq2", [P, QT])
        rounded1 = ph.sbuf("rounded1", [P, QT, D])
        quant1 = ph.sbuf("quant1", [P, QT, D], BF16)
        quant1T = ph.sbuf("quant1T", [P, QT, P], BF16)
        hidden = ph.sbuf("hidden", [P, QT, F])
        gelu = ph.sbuf("gelu", [P, QT, F])
        rounded2 = ph.sbuf("rounded2", [P, QT, F])
        quant2 = ph.sbuf("quant2", [P, QT, F], BF16)
        quant2T = ph.sbuf("quant2T", [P, QT, C, P], BF16)
        turned1 = ph.psum("turned1", [P, QT, 512], BF16)
        turned2 = ph.psum("turned2", [P, QT, 1024], BF16)
        up = ph.psum("up", [P, QT, F])
        down = ph.psum("down", [P, 512])
        (loaded, summed, totals, scaled, wrounded, ternary, w_turned, w_copied, stats_done, moments_done, rstd_done,
         normed, row1, root1, scale1, quantised1, turned1_done, copied1, up_done, hidden_done, gelu_done, squared2,
         row2, root2, scale2, quantised2, turned2_done, copied2, down_done, added) = [ph.sem(n) for n in (
             "loaded", "summed", "totals", "scaled", "wrounded", "ternary", "w_turned", "w_copied", "stats_done",
             "moments_done", "rstd_done", "normed", "row1", "root1", "scale1", "quantised1", "turned1_done",
             "copied1", "up_done", "hidden_done", "gelu_done", "squared2", "row2", "root2", "scale2",
             "quantised2", "turned2_done", "copied2", "down_done", "added")]
        block = ctx.enter_context(nc.Block())

        @block.sync
        def _(sp):
            sp.dma_start(w1_rows[:, :, :], sh.dram["L0_ffn_w1"].rearrange("(c p) i -> p c i", p=P)).then_inc(loaded, 16)
            sp.dma_start(w2_rows[:, :], sh.dram["L0_ffn_w2"]).then_inc(loaded, 16)
            sp.dma_start(bias1[:, :], sh.dram["L0_ffn_b1"].rearrange("(o f) -> o f", o=1).to_broadcast([P, F])).then_inc(loaded, 16)
            sp.dma_start(bias2[:, :], sh.dram["L0_ffn_b2"].rearrange("(o f) -> o f", o=1).to_broadcast([P, D])).then_inc(loaded, 16)

        @block.gpsimd
        def _(pool):
            clear_retired(pool, sh)
            with pool.Fori(0, NB) as b:
                pool_rstd(pool, sh, moments, moments_done, rstd_done, b)
                pool.wait_ge(row1, b + 1)
                pool.tensor_tensor(rms1[:, :, 1:2], rms1[:, :, 0:1], sh.half[:, 0:QT].unsqueeze(2), ALU.pow).then_inc(root1, 1)
                pool.wait_ge(row2, b + 1)
                pool.tensor_tensor(rms2[:, :, 1:2], rms2[:, :, 0:1], sh.half[:, 0:QT].unsqueeze(2), ALU.pow).then_inc(root2, 1)

        @block.tensor
        def _(pe):
            pe.wait_ge(summed, 2)
            pe.matmul(down[:, 0:2], sh.ones[:, :], magnitude[:, :], start=True, stop=True).then_inc(totals, 1)
            pe.wait_ge(ternary, 2)
            for j in range(2):
                for c in range(C):
                    last = pe.transpose(turned2[:, j, P * c:P * (c + 1)], w_tern[:, j, P * c:P * (c + 1)], sh.ident_bf[:, :])
            last.then_inc(w_turned, 1)
            pe.wait_ge(w_copied, 2)
            with pe.Fori(0, NB) as b:
                pe.wait_ge(quantised1, b + 1)
                for q in range(QT):
                    last = pe.transpose(turned1[:, q, 0:P], quant1[:, q, :], sh.ident_bf[:, :])
                last.then_inc(turned1_done, 1)
                pe.wait_ge(copied1, b + 1)
                for q in range(QT):
                    pe.matmul(up[:, q, :], quant1T[:, q, :], w1q[:, :], start=True, stop=True).then_inc(up_done, 1)
                pe.wait_ge(quantised2, b + 1)
                for q in range(QT):
                    for c in range(C):
                        last = pe.transpose(turned2[:, q, P * c:P * (c + 1)], quant2[:, q, P * c:P * (c + 1)], sh.ident_bf[:, :])
                    last.then_inc(turned2_done, 1)
                for q in range(QT):
                    pe.wait_ge(copied2, QT * b + q + 1)
                    for c in range(C):
                        last = pe.matmul(down[:, D * q:D * (q + 1)], quant2T[:, q, c, :], w2q[:, c, :],
                                         start=(c == 0), stop=(c == C - 1))
                last.then_inc(down_done, 1)

        @block.scalar
        def _(act):
            act.wait_ge(w_turned, 1)
            act.activation(w1q[:, :], turned2[:, 0, 0:F], ACT.Copy).then_inc(w_copied, 1)
            act.activation(w2q[:, :, :], turned2[:, 1, 0:F].rearrange("p (c o) -> p c o", c=C), ACT.Copy).then_inc(w_copied, 1)
            with act.Fori(0, NB) as b:
                act.wait_ge(turned1_done, b + 1)
                act.activation(quant1T[:, :, :], turned1[:, :, 0:P], ACT.Copy).then_inc(copied1, 1)
                for q in range(QT):
                    act.wait_ge(hidden_done, QT * b + q + 1)
                    act.activation(gelu[:, q, :], hidden[:, q, :], ACT.Gelu).then_inc(gelu_done, 1)
                for q in range(QT):
                    act.wait_ge(gelu_done, QT * b + q + 1)
                    act.activation(squares[:, q, :], gelu[:, q, :], ACT.Square, accum_out=rms2[:, q, 2:3]).then_inc(squared2, 1)
                for q in range(QT):
                    act.wait_ge(turned2_done, QT * b + q + 1)
                    act.activation(quant2T[:, q, :, :], turned2[:, q, 0:F].rearrange("p (c t) -> p c t", c=C), ACT.Copy).then_inc(copied2, 1)

        @block.vector
        def _(dve):
            dve.wait_ge(loaded, 64)
            dve.tensor_reduce(magnitude[:, 0:1], w1_rows[:, :, :].rearrange("p c i -> p (c i)"), AX.X, ALU.add, apply_absolute_value=True).then_inc(summed, 1)
            dve.tensor_reduce(magnitude[:, 1:2], w2_rows[:, :], AX.X, ALU.add, apply_absolute_value=True).then_inc(summed, 1)
            dve.wait_ge(totals, 1)
            dve.tensor_scalar(w_scale[:, :, 0], down[:, 0:2], 1.0 / (F * D), QUANT_EPS, ALU.mult, ALU.max).then_inc(scaled, 1)
            dve.wait_ge(scaled, 1)
            dve.reciprocal(w_scale[:, :, 1], w_scale[:, :, 0]).then_inc(scaled, 1)
            dve.wait_ge(scaled, 2)
            for j, w in enumerate((w1_rows[:, :, :].rearrange("p c i -> p (c i)"), w2_rows[:, :])):
                dve.tensor_scalar(w_round[:, j, :], w, w_scale[:, j, 1:2], ROUND, ALU.mult, ALU.add).then_inc(wrounded, 1)
            for j in range(2):
                dve.wait_ge(wrounded, 2 + j)
                dve.tensor_scalar(w_round[:, j, :], w_round[:, j, :], ROUND, 1.0, ALU.subtract, ALU.min).then_inc(wrounded, 1)
            dve.wait_ge(wrounded, 4)
            for j in range(2):
                dve.tensor_scalar(w_tern[:, j, :], w_round[:, j, :], -1.0, None, ALU.max).then_inc(ternary, 1)

            with dve.Fori(0, NB) as b:
                rows = [sh.x_all[:, bass.ds(b * QT + q, 1), :].rearrange("p o d -> p (o d)") for q in range(QT)]
                dve_layernorm(dve, rows, [xn[:, q, :] for q in range(QT)], stats, moments, stats_done,
                              moments_done, rstd_done, normed, LN_EPS, b)
                dve.wait_ge(normed, QT * (b + 1))
                n = Counter(STEPS)
                dve.tensor_tensor(squares[:, :, 0:D], xn[:, :, :], xn[:, :, :], ALU.mult).then_inc(step, n.up())
                dve.wait_ge(step, n.all(b))
                dve.tensor_reduce(rms1[:, :, 2], squares[:, :, 0:D], AX.X, ALU.add).then_inc(step, n.up())
                dve_quantise(dve, xn, D, rms1, rounded1, quant1, deq1, w_scale[:, 0, 0:1], step, n, row1, root1, quantised1, b)
                for q in range(QT):
                    dve.wait_ge(up_done, QT * b + q + 1)
                    dve.scalar_tensor_tensor(out=hidden[:, q, :], in0=up[:, q, :], scalar=deq1[:, q:q + 1],
                                             in1=bias1[:, :], op0=ALU.mult, op1=ALU.add).then_inc(hidden_done, 1)
                dve.wait_ge(squared2, QT * (b + 1))
                dve_quantise(dve, gelu, F, rms2, rounded2, quant2, deq2, w_scale[:, 1, 0:1], step, n, row2, root2, quantised2, b)
                n.close()
                dve.wait_ge(down_done, b + 1)
                for q in range(QT):
                    dve.scalar_tensor_tensor(out=xn[:, q, :], in0=down[:, D * q:D * (q + 1)], scalar=deq2[:, q:q + 1],
                                             in1=bias2[:, :], op0=ALU.mult, op1=ALU.add).then_inc(added, 1)
                dve.wait_ge(added, (QT + 1) * b + QT)
                out_rows = sh.x_all[:, bass.ds(b * QT, QT), :]
                dve.tensor_tensor(out_rows, out_rows, xn[:, :, :], ALU.add).then_inc(added, 1)
                dve.wait_ge(added, (QT + 1) * (b + 1))
        ph.retire(sh)


def phase_softmax_attention(nc, sh, multi_query):
    H, G, U = 16, 4, 8
    DH = 64 if multi_query else 8
    W = 64 if multi_query else 32
    C = H * W // P
    CU = C * QT // U
    FC = 5 if multi_query else 3
    after = ["F0", "F1", "F2", "F3", "F4", "T0", "", ""]
    FILLS = range(5) if multi_query else range(2, 5)
    with ExitStack() as ctx:
        ph = Phase(nc, ctx, "l2a" if multi_query else "l1a")
        if multi_query:
            wq = ph.sbuf("wq", [P, H * DH])
            wkv = ph.sbuf("wkv", [P, 3 * DH])
        else:
            w_rows = ph.sbuf("w_rows", [P, 4, D])
            wo_rows = ph.sbuf("wo_rows", [P, H, W])
            wT = ph.sbuf("wT", [P, 3, D])
            bias_cols = ph.sbuf("bias_cols", [P, 2])
            bias_q = ph.sbuf("bias_q", [P, 1])
            bias_rows = ph.sbuf("bias_rows", [1, 2, D])
            stats = ph.sbuf("stats", [P, QT, 6])
            moments = ph.sbuf("moments", [P, QT, 4])
            xn = ph.sbuf("xn", [P, QT, D])
            xnT = ph.sbuf("xnT", [P, S])
            stacks = Stacks(ph, H, DH)
        ctx_now = ph.sbuf("ctx_now", [P, S])
        if multi_query:
            qT = ph.sbuf("qT", [P, 2, C, S])
            kT = ph.sbuf("kT", [P, 2, S])
        wo = ph.sbuf("wo", [P, C, D])
        values = ph.sbuf("values", [P, 2, QT, 1 if multi_query else H, W])
        mask = ph.sbuf("mask", [P, 2, QT, S])
        masked = ph.sbuf("masked", [P, 2, G, S])
        minus_max = ph.sbuf("minus_max", [P, 2, G])
        probs = ph.sbuf("probs", [P, 4, G, S])
        sums = ph.sbuf("sums", [P, 4, G])
        inverse = ph.sbuf("inverse", [P, 4, G])
        probsT = ph.sbuf("probsT", [P, 2, G, QT, P])
        mixedT = ph.sbuf("mixedT", [P, 2, QT, C, P])
        scores = [ph.psum(f"scores{i}", [P, G, S]) for i in range(2)]
        turned = ph.psum("turned", [P, G, QT, P])
        out_sums = ph.psum("out_sums", [P, 512])
        side = ph.psum("side", [P, 512])
        out_view = out_sums[:, 0:CU * P].rearrange("p (c q) -> p c q", c=CU)
        (w_loaded, w_turned, w_copied, bias_scaled, stats_done, moments_done, rstd_done, normed, front_filled,
         front_copied, tail_filled, tail_copied, ctx_ready, mask_ready, mask_used, scored, mask_added, max_ready, exp_done,
         turned_done, turned_copied, summed, inverted, scaled, mixed_ready, added, padded) = [ph.sem(n) for n in (
             "w_loaded", "w_turned", "w_copied", "bias_scaled", "stats_done", "moments_done", "rstd_done",
             "normed", "front_filled", "front_copied", "tail_filled", "tail_copied", "ctx_ready", "mask_ready", "mask_used",
             "scored", "mask_added", "max_ready", "exp_done", "turned_done", "turned_copied", "summed",
             "inverted", "scaled", "mixed_ready", "added", "padded")]
        block = ctx.enter_context(nc.Block())

        def head_of(j):
            return 2 * (j % 2) + j // 2 if multi_query else j

        def run(eng, front, unit, finish, tail):
            def one(b, par, first, more):
                before = ("F", FC - 1, b) if isinstance(b, int) and b < 2 else ("T", b - 2)
                for u in range(U):
                    unit(b, par, u, first)
                    for name in after[u].split():
                        kind, k = name[0], int(name[1])
                        if kind == "F" and more:
                            front(b + 1, 1 - par, False, k, before)
                            if k in FILLS:
                                before = ("F", FILLS.index(k), b + 1)
                        if kind == "T" and not first:
                            tail(b - 1, 1 - par, before)
                            before = ("T", b - 1)

            before = None
            for k in range(5):
                front(0, 0, True, k, before)
                if k in FILLS:
                    before = ("F", FILLS.index(k), 0)
            one(0, 0, True, True)
            one(1, 1, False, True)
            with eng.Fori(2, NB - 2, 2) as b:
                one(b, 0, False, True)
                one(b + 1, 1, False, True)
            one(NB - 2, 0, False, True)
            one(NB - 1, 1, False, False)
            finish(NB - 1, 1)
            tail(NB - 1, 1, ("T", NB - 2))

        def behind(work, b, par, u, lag, first):
            if u >= lag:
                work(b, par, u - lag)
            elif not first:
                work(b - 1, 1 - par, U + u - lag)

        def wait_side_free(pe, before):
            if before is not None:
                if before[0] == "F":
                    pe.wait_ge(front_copied, FC * before[2] + before[1] + 1)
                else:
                    pe.wait_ge(tail_copied, before[1] + 1)

        def nothing(*args):
            pass

        @block.sync
        def _(sp):
            if multi_query:
                sp.dma_start(wq[:, :], sh.dram["L2_xattn_Wq"]).then_inc(w_loaded, 16)
                for j in range(2):
                    sp.dma_start(wkv[:, DH * j:DH * (j + 1)], sh.dram["L2_xattn_Wkv"][:, 0:DH]).then_inc(w_loaded, 16)
                sp.dma_start(wkv[:, 2 * DH:3 * DH], sh.dram["L2_xattn_Wkv"][:, DH:2 * DH]).then_inc(w_loaded, 16)
                sp.dma_start(wo[:, :, :], sh.dram["L2_xattn_Wout"].rearrange("(c p) d -> p c d", p=P)).then_inc(w_loaded, 16)

                def front(b, par, first, k, before):
                    if k:
                        return
                    if not first:
                        sp.wait_ge(mask_ready, 16 * b)
                    if not (isinstance(b, int) and b < 2):
                        sp.wait_ge(mask_used, b - 1)
                    sp.dma_start(mask[:, par, :, :], sh.dram["mask_BxSxS2_ff0"][bass.ds(b, 1), :, :]
                                 .rearrange("o (q p) k -> p (o q) k", p=P)).then_inc(mask_ready, 16)
            else:
                for j, n in enumerate(("wq", "wk", "wv", "wo")):
                    sp.dma_start(w_rows[:, j, :], sh.dram["L1_xattn_" + n]).then_inc(w_loaded, 16)
                with nc.allow_non_contiguous_dma(reason="bias columns"):
                    for j, n in enumerate(("bq", "bk")):
                        column = sh.dram["L1_xattn_" + n].rearrange("(h d o) -> d h o", h=H, o=1)
                        for d in range(DH):
                            sp.dma_start(bias_cols[H * d:H * (d + 1), j:j + 1], column[d]).then_inc(w_loaded, 16)
                for j, n in enumerate(("bv", "bo")):
                    sp.dma_start(bias_rows[:, j, :], sh.dram["L1_xattn_" + n].rearrange("(o d) -> o d", o=1)).then_inc(w_loaded, 16)

                def front(b, par, first, k, before):
                    if k:
                        return
                    if not first:
                        sp.wait_ge(stacks.stacked_ready, 16 * stacks.LOADS * b)
                        sp.sem_inc(stacks.free, 1)
                    if not (isinstance(b, int) and b < 2):
                        sp.wait_ge(scored, U * (b - 1))
                        sp.sem_inc(stacks.free, 1)
                    stacks.load(sp, b, par)

            run(sp, front, nothing, nothing, nothing)

        @block.gpsimd
        def _(pool):
            clear_retired(pool, sh)
            if not multi_query:
                pool.memset(values[:, :, :, :, :], 0.0).then_inc(padded, 1)
                pool.memset(wo_rows[:, :, :], 0.0).then_inc(padded, 1)
                pool.wait_ge(padded, 2)
                pool.wait_ge(w_loaded, 16 * (6 + 2 * DH))
                pool.tensor_copy(wo_rows[:, :, 0:DH], w_rows[:, 3, :].rearrange("p (h d) -> p h d", h=H)).then_inc(padded, 1)

            def scale(b, par, u):
                pool.wait_ge(inverted, U * b + u + 1)
                buf = probs[:, u % 4, :, :]
                pool.tensor_tensor(buf, buf, inverse[:, u % 4, :].unsqueeze(2).to_broadcast([P, G, S]), ALU.mult).then_inc(scaled, 1)

            def front(b, par, first, k, before):
                if k:
                    return
                if not first:
                    pool.wait_ge(front_filled, FC * b)
                source = sh.cnT_all if multi_query else sh.ctxT
                pool.tensor_copy(ctx_now[:, :], source[:, bass.ds(b * S, S)]).then_inc(ctx_ready, 1)
                if not multi_query:
                    pool_rstd(pool, sh, moments, moments_done, rstd_done, b)

            run(pool, front, lambda b, par, u, first: behind(scale, b, par, u, 1, first),
                lambda b, par: scale(b, par, U - 1), nothing)

        @block.tensor
        def _(pe):
            if not multi_query:
                pe.wait_ge(w_loaded, 16 * (6 + 2 * DH))
                for j in range(3):
                    last = pe.transpose(side[:, P * j:P * (j + 1)], w_rows[:, j, :], sh.ident[:, :])
                last.then_inc(w_turned, 1)
                pe.wait_ge(padded, 3)
                for c in range(C):
                    last = pe.transpose(out_sums[:, P * c:P * (c + 1)],
                                        wo_rows[:, G * c:G * (c + 1), :].rearrange("p g d -> p (g d)"), sh.ident[:, :])
                last.then_inc(w_turned, 1)
                pe.wait_ge(w_copied, 2)
            else:
                pe.wait_ge(w_loaded, 80)

            def front(b, par, first, k, before):
                if k not in FILLS:
                    return
                wait_side_free(pe, before)
                fill = FILLS.index(k)
                if multi_query:
                    if fill < 4:
                        for j in range(2):
                            last = pe.matmul(side[:, S * j:S * (j + 1)], wq[:, P * (2 * fill + j):P * (2 * fill + j + 1)],
                                             sh.xnT_all[:, bass.ds(b * S, S)], start=True, stop=True)
                    else:
                        pe.wait_ge(ctx_ready, b + 1)
                        pe.matmul(side[:, 0:S], wkv[:, 0:2 * DH], ctx_now[:, :], start=True, stop=True)
                        for t in range(QT):
                            last = pe.matmul(side[:, S + DH * t:S + DH * (t + 1)], ctx_now[:, P * t:P * (t + 1)],
                                             wkv[:, 2 * DH:3 * DH], start=True, stop=True)
                elif fill == 0:
                    pe.wait_ge(normed, QT * (b + 1))
                    for q in range(QT):
                        last = pe.transpose(side[:, P * q:P * (q + 1)], xn[:, q, :], sh.ident[:, :])
                elif fill == 1:
                    pe.wait_ge(ctx_ready, b + 1)
                    pe.wait_ge(front_copied, FC * b + 1)
                    pe.matmul(side[:, 0:S], wT[:, 0, :], xnT[:, :], start=True, stop=True)
                    last = pe.matmul(side[:, S:2 * S], wT[:, 1, :], ctx_now[:, :], start=True, stop=True)
                else:
                    for t in range(QT):
                        pe.matmul(side[:, D * t:D * (t + 1)], ctx_now[:, P * t:P * (t + 1)], wT[:, 2, :], start=True, stop=False)
                        last = pe.matmul(side[:, D * t:D * (t + 1)], sh.ones[0:1, :], bias_rows[:, 0, :], start=False, stop=True)
                last.then_inc(front_filled, 1)

            def turn(b, par, u):
                pe.wait_ge(scaled, U * b + u + 1)
                if not (isinstance(b, int) and b == 0 and u == 0):
                    pe.wait_ge(turned_copied, U * b + u)
                for j in range(G):
                    for t in range(QT):
                        last = pe.transpose(turned[:, j, t, :], probs[:, u % 4, j, P * t:P * (t + 1)], sh.ident[:, :])
                last.then_inc(turned_done, 1)

            def value_products(b, par, u):
                pe.wait_ge(turned_copied, U * b + u + 1)
                if not (isinstance(b, int) and b == 0 and u == 0):
                    pe.wait_ge(mixed_ready, U * b + u)
                for t in range(QT):
                    if multi_query:
                        for odd in range(2):
                            last = pe.matmul(out_view[W * odd:W * (odd + 1), :, :], values[:, par, t, 0, :],
                                             probsT[:, u % 2, 2 * odd:2 * odd + 2, t, :], start=(t == 0), stop=(t == QT - 1))
                    else:
                        for j in range(G):
                            last = pe.matmul(out_view[W * j:W * (j + 1), 0, :], values[:, par, t, G * (u % 4) + j, :],
                                             probsT[:, u % 2, j, t, :], start=(t == 0), stop=(t == QT - 1))
                last.then_inc(summed, 1)

            def unit(b, par, u, first):
                q, g = u // 4, u % 4
                if u == 0:
                    pe.wait_ge(front_copied, FC * (b + 1))
                    if not multi_query:
                        pe.wait_ge(stacks.stacked_ready, 16 * stacks.LOADS * (b + 1))
                if not (first and u < 2):
                    pe.wait_ge(mask_added, U * b + u - 1)
                for j in range(G):
                    h = G * g + head_of(j)
                    if multi_query:
                        rows = slice(DH * (h % 2), DH * (h % 2 + 1))
                        last = pe.matmul(scores[u % 2][:, j, :], qT[rows, par, h // 2, P * q:P * (q + 1)],
                                         kT[rows, par, :], start=True, stop=True)
                    else:
                        last = pe.matmul(scores[u % 2][:, j, :], stacks.stacked[:, par, 0, h, P * q:P * (q + 1)],
                                         stacks.stacked[:, par, 1, h, :], start=True, stop=True)
                last.then_inc(scored, 1)
                behind(turn, b, par, u, 3, first)
                behind(value_products, b, par, u, 4, first)

            def finish(b, par):
                value_products(b, par, U - 4)
                for u in range(U - 3, U):
                    turn(b, par, u)
                    value_products(b, par, u)

            def tail(b, par, before):
                wait_side_free(pe, before)
                pe.wait_ge(mixed_ready, U * (b + 1))
                for q in range(QT):
                    for c in range(C):
                        last = pe.matmul(side[:, D * q:D * (q + 1)], mixedT[:, par, q, c, :], wo[:, c, :],
                                         start=(c == 0), stop=(multi_query and c == C - 1))
                    if not multi_query:
                        last = pe.matmul(side[:, D * q:D * (q + 1)], sh.ones[0:1, :], bias_rows[:, 1, :], start=False, stop=True)
                last.then_inc(tail_filled, 1)

            run(pe, front, unit, finish, tail)

        @block.scalar
        def _(act):
            if not multi_query:
                act.wait_ge(padded, 2)
                act.wait_ge(w_turned, 1)
                act.activation(wT[:, 0:2, :].rearrange("p j (d h) -> p j d h", h=H),
                               side[:, 0:2 * P].rearrange("p (j h d) -> p j d h", j=2, h=H), ACT.Copy)
                act.activation(wT[:, 2, :], side[:, 2 * P:3 * P], ACT.Copy).then_inc(w_copied, 1)
                act.wait_ge(w_turned, 2)
                act.activation(wo[:, :, :], out_sums[:, :].rearrange("p (c d) -> p c d", c=C), ACT.Copy).then_inc(w_copied, 1)
                act.activation(bias_q[:, :], bias_cols[:, 0:1], ACT.Copy, scale=float(DH) ** -0.5).then_inc(bias_scaled, 1)
                act.wait_ge(bias_scaled, 1)

            def front(b, par, first, k, before):
                if k not in FILLS:
                    return
                fill = FILLS.index(k)
                act.wait_ge(front_filled, FC * b + fill + 1)
                if multi_query:
                    if fill < 4:
                        last = act.activation(qT[:, par, 2 * fill:2 * fill + 2, :], side[:, :].rearrange("p (c s) -> p c s", c=2),
                                              ACT.Copy, scale=float(DH) ** -0.5)
                    else:
                        act.activation(kT[:, par, :], side[:, 0:S], ACT.Copy)
                        last = act.activation(values[:, par, :, 0, :], side[:, S:S + QT * DH].rearrange("p (t d) -> p t d", t=QT), ACT.Copy)
                elif fill == 0:
                    last = act.activation(xnT[:, :], side[:, 0:S], ACT.Copy)
                elif fill == 1:
                    if not first:
                        act.wait_ge(stacks.split, 4 * b)
                    act.activation(stacks.exact[:, 0, :], side[:, 0:S], ACT.Identity, scale=float(DH) ** -0.5, bias=bias_q[:, :])
                    last = act.activation(stacks.exact[:, 1, :], side[:, S:2 * S], ACT.Identity, bias=bias_cols[:, 1:2])
                else:
                    last = act.activation(values[:, par, :, :, 0:DH],
                                          side[:, 0:QT * D].rearrange("p (t h d) -> p t h d", t=QT, h=H), ACT.Copy)
                last.then_inc(front_copied, 1)

            def copy_turned(b, par, u):
                act.wait_ge(turned_done, U * b + u + 1)
                if not (isinstance(b, int) and b == 0 and u < 2):
                    act.wait_ge(summed, U * b + u - 1)
                act.activation(probsT[:, u % 2, :, :, :], turned[:, :, :, :], ACT.Copy).then_inc(turned_copied, 1)

            def unit(b, par, u, first):
                behind(copy_turned, b, par, u, 3, first)
                act.wait_ge(max_ready, U * b + u + 1)
                if not (first and u < 4):
                    act.wait_ge(turned_done, U * b + u - 3)
                for j in range(G):
                    last = act.activation(probs[:, u % 4, j, :], masked[:, u % 2, j, :], ACT.Exp,
                                          bias=minus_max[:, u % 2, j:j + 1], accum_out=sums[:, u % 4, j:j + 1])
                last.then_inc(exp_done, 1)

            def finish(b, par):
                for u in range(U - 3, U):
                    copy_turned(b, par, u)

            run(act, front, unit, finish, nothing)

        @block.vector
        def _(dve):
            def front(b, par, first, k, before):
                if multi_query:
                    return
                rows = [sh.x_all[:, bass.ds(b * QT + q, 1), :].rearrange("p o d -> p (o d)") for q in range(QT)]
                out = [xn[:, q, :] for q in range(QT)]
                if k == 0:
                    dve_moments(dve, rows, stats, moments, stats_done, moments_done, LN_EPS, b)
                elif k == 1:
                    if not first:
                        dve.wait_ge(front_filled, FC * b - 2)
                    dve_normalise(dve, rows, out, moments, rstd_done, normed, b)
                    for q in range(QT):
                        dve.tensor_scalar(mask[:, par, q, :], sh.key_index[:, :], sh.last_patch[:, bass.ds(b * QT + q, 1)],
                                          MASKED, ALU.is_gt, ALU.mult).then_inc(mask_ready, 8)
                elif k == 3:
                    dve.wait_ge(front_copied, FC * b + 2)
                    if not first:
                        dve.wait_ge(stacks.stored, 16 * b)
                    stacks.split_parts(dve, b)

            def invert(b, par, u):
                dve.wait_ge(exp_done, U * b + u + 1)
                dve.reciprocal(inverse[:, u % 4, :], sums[:, u % 4, :]).then_inc(inverted, 1)

            def copy_out(b, par, u):
                dve.wait_ge(summed, U * b + u + 1)
                g = u % 4
                dve.tensor_copy(mixedT[:, par, u // 4, CU * g:CU * (g + 1), :], out_view[:, :, :]).then_inc(mixed_ready, 1)

            def unit(b, par, u, first):
                if u == 0:
                    dve.wait_ge(mask_ready, 16 * (b + 1))
                dve.wait_ge(scored, U * b + u + 1)
                if not (first and u < 2):
                    dve.wait_ge(exp_done, U * b + u - 1)
                dve.tensor_tensor(masked[:, u % 2, :, :], scores[u % 2][:, :, :],
                                  mask[:, par, u // 4, :].unsqueeze(1).to_broadcast([P, G, S]), ALU.add).then_inc(mask_added, 1)
                dve.wait_ge(mask_added, U * b + u + 1)
                dve.tensor_reduce(minus_max[:, u % 2, :], masked[:, u % 2, :, :], AX.X, ALU.max, negate=True).then_inc(max_ready, 1)
                if u == U - 1:
                    dve.sem_inc(mask_used, 1)
                behind(invert, b, par, u, 1, first)
                behind(copy_out, b, par, u, 4, first)

            def finish(b, par):
                invert(b, par, U - 1)
                for u in range(U - 4, U):
                    copy_out(b, par, u)

            def tail(b, par, before):
                dve.wait_ge(tail_filled, b + 1)
                rows = sh.x_all[:, bass.ds(b * QT, QT), :]
                if multi_query:
                    dve.tensor_tensor(rows, rows, sh.y_all[:, bass.ds(b * QT, QT), :], ALU.add).then_inc(added, 1)
                    dve.wait_ge(added, b + 1)
                dve.tensor_tensor(rows, rows, side[:, 0:QT * D].rearrange("p (q d) -> p q d", q=QT), ALU.add).then_inc(tail_copied, 1)

            run(dve, front, unit, finish, tail)
        ph.retire(sh)


def phase_expert_ffn(nc, sh):
    E, F, T = 8, 352, 32
    CH = [(0, P), (P, P), (2 * P, F - 2 * P)]
    HALF = 4
    with ExitStack() as ctx:
        ph = Phase(nc, ctx, "l1f")
        w_gate = ph.sbuf("w_gate", [P, E, F])
        w_up = ph.sbuf("w_up", [P, E, F])
        w_down = ph.sbuf("w_down", [P, E, 3, D])
        stats = ph.sbuf("stats", [P, QT, 6])
        moments = ph.sbuf("moments", [P, QT, 4])
        xn = ph.sbuf("xn", [P, QT, D])
        x_expert = ph.sbuf("x_expert", [P, E, NB, T])
        silu = ph.sbuf("silu", [P, 2, F])
        hidden = ph.sbuf("hidden", [P, 2, F])
        hiddenT = ph.sbuf("hiddenT", [P, 2, 3, P])
        xT = ph.psum("xT", [P, 512])
        gate = ph.psum("gate", [P, 2, 512])
        up = ph.psum("up", [P, 2, 512])
        turned = ph.psum("turned", [P, 512])
        down = ph.psum("down", [P, 2, 512])
        (w_loaded, stats_done, moments_done, rstd_done, normed, xT_done, xT_copied, up_done, silu_done,
         hidden_done, turned_done, turned_copied, down_done, added) = [ph.sem(n) for n in (
             "w_loaded", "stats_done", "moments_done", "rstd_done", "normed", "xT_done", "xT_copied", "up_done",
             "silu_done", "hidden_done", "turned_done", "turned_copied", "down_done", "added")]
        block = ctx.enter_context(nc.Block())

        @block.sync
        def _(sp):
            sp.dma_start(w_gate[:, :, :], sh.dram["L1_ffn_w1"].rearrange("e d f -> d e f")).then_inc(w_loaded, 16)
            sp.dma_start(w_up[:, :, :], sh.dram["L1_ffn_w3"].rearrange("e d f -> d e f")).then_inc(w_loaded, 16)
            w2 = sh.dram["L1_ffn_w2"]
            for c, (at, n) in enumerate(CH):
                sp.dma_start(w_down[0:n, :, c, :], w2[:, at:at + n, :].rearrange("e f d -> f e d")).then_inc(w_loaded, 16)

        @block.gpsimd
        def _(pool):
            clear_retired(pool, sh)
            with pool.Fori(0, NB) as b:
                pool_rstd(pool, sh, moments, moments_done, rstd_done, b)

        units = [(e, half) for e in range(E) for half in range(2)]

        @block.tensor
        def _(pe):
            with pe.Fori(0, NB) as b:
                pe.wait_ge(normed, QT * (b + 1))
                for q in range(QT):
                    last = pe.transpose(xT[:, P * q:P * (q + 1)], xn[:, q, :], sh.ident[:, :])
                last.then_inc(xT_done, 1)
                pe.wait_ge(xT_copied, b + 1)
            pe.wait_ge(w_loaded, 80)

            def down_products(u):
                e, half = units[u]
                pe.wait_ge(hidden_done, u + 1)
                if u >= 1:
                    pe.wait_ge(turned_copied, u)
                for c, (at, n) in enumerate(CH):
                    last = pe.transpose(turned[0:n, P * c:P * (c + 1)], hidden[:, u % 2, at:at + n], sh.ident[:, :])
                last.then_inc(turned_done, 1)
                pe.wait_ge(turned_copied, u + 1)
                if u >= 2:
                    pe.wait_ge(added, 4 * (u - 1))
                for c, (at, n) in enumerate(CH):
                    last = pe.matmul(down[:, u % 2, 0:D], hiddenT[0:n, u % 2, c, :], w_down[0:n, e, c, :],
                                     start=(c == 0), stop=(c == 2))
                last.then_inc(down_done, 1)

            for u, (e, half) in enumerate(units):
                rows = x_expert[:, e, HALF * half:HALF * (half + 1), :].rearrange("p b t -> p (b t)")
                if u >= 2:
                    pe.wait_ge(hidden_done, u - 1)
                pe.matmul(gate[:, u % 2, 0:F], rows, w_gate[:, e, :], start=True, stop=True)
                pe.matmul(up[:, u % 2, 0:F], rows, w_up[:, e, :], start=True, stop=True).then_inc(up_done, 1)
                if u:
                    down_products(u - 1)
            down_products(len(units) - 1)

        @block.scalar
        def _(act):
            with act.Fori(0, NB) as b:
                act.wait_ge(xT_done, b + 1)
                act.activation(x_expert[:, :, bass.ds(b, 1), :].rearrange("p e o t -> p e (o t)"),
                               xT[:, 0:S].rearrange("p (e t) -> p e t", e=E), ACT.Copy).then_inc(xT_copied, 1)

            def copy_turned(u):
                act.wait_ge(turned_done, u + 1)
                for c, (at, n) in enumerate(CH):
                    last = act.activation(hiddenT[0:n, u % 2, c, :], turned[0:n, P * c:P * (c + 1)], ACT.Copy)
                last.then_inc(turned_copied, 1)

            for u in range(len(units)):
                act.wait_ge(up_done, u + 1)
                if u >= 2:
                    act.wait_ge(hidden_done, u - 1)
                act.activation(silu[:, u % 2, :], gate[:, u % 2, 0:F], ACT.Silu).then_inc(silu_done, 1)
                if u:
                    copy_turned(u - 1)
            copy_turned(len(units) - 1)

        @block.vector
        def _(dve):
            with dve.Fori(0, NB) as b:
                rows = [sh.x_all[:, bass.ds(b * QT + q, 1), :].rearrange("p o d -> p (o d)") for q in range(QT)]
                dve_layernorm(dve, rows, [xn[:, q, :] for q in range(QT)], stats, moments, stats_done,
                              moments_done, rstd_done, normed, LN_EPS, b)
                dve.wait_ge(xT_done, b + 1)

            def add_down(u):
                e, half = units[u]
                dve.wait_ge(down_done, u + 1)
                at = T * (e % 4)
                for j in range(HALF):
                    b = HALF * half + j
                    rows = sh.x_all[at:at + T, QT * b + e // 4, :]
                    dve.tensor_tensor(rows, rows, down[T * j:T * (j + 1), u % 2, 0:D], ALU.add).then_inc(added, 1)

            for u in range(len(units)):
                dve.wait_ge(silu_done, u + 1)
                if u >= 2:
                    dve.wait_ge(turned_done, u - 1)
                dve.tensor_tensor(hidden[:, u % 2, :], silu[:, u % 2, :], up[:, u % 2, 0:F], ALU.mult).then_inc(hidden_done, 1)
                if u:
                    add_down(u - 1)
            add_down(len(units) - 1)
        ph.retire(sh)


def phase_multi_query_inputs(nc, sh):
    F = 512
    C = F // P
    with ExitStack() as ctx:
        ph = Phase(nc, ctx, "l2f")
        ctx_rows = ph.sbuf("ctx_rows", [P, NT, D])
        w1 = ph.sbuf("w1", [P, 2 * F])
        w2 = ph.sbuf("w2", [P, C, D])
        affine = ph.sbuf("affine", [P, 4, D])
        stats = [ph.sbuf(f"stats{i}", [P, QT, 6]) for i in range(3)]
        moments = [ph.sbuf(f"moments{i}", [P, QT, 4]) for i in range(3)]
        x_mid = ph.sbuf("x_mid", [P, QT, D])
        normed_rows = ph.sbuf("normed_rows", [P, 2, QT, D])
        scaled_rows = ph.sbuf("scaled_rows", [P, 2, QT, D])
        affine_rows = ph.sbuf("affine_rows", [P, 2, QT, D])
        rowsT = ph.sbuf("rowsT", [P, S])
        silu = ph.sbuf("silu", [P, QT, F])
        hidden = ph.sbuf("hidden", [P, QT, F])
        hiddenT = ph.sbuf("hiddenT", [P, QT, C, P])
        turned_rows = ph.psum("turned_rows", [P, 2, S])
        up = ph.psum("up", [P, QT, 2, F])
        turned = ph.psum("turned", [P, QT, C, P])
        down = ph.psum("down", [P, 512])
        stats_done = [ph.sem(f"stats_done{i}") for i in range(3)]
        moments_done = [ph.sem(f"moments_done{i}") for i in range(3)]
        rstd_done = [ph.sem(f"rstd_done{i}") for i in range(3)]
        normed = [ph.sem(f"normed{i}") for i in range(3)]
        (w_loaded, scaled, affine_done, rows_turned, rows_copied, up_done, silu_done, hidden_done, hidden_turned,
         hidden_copied, down_done, y_done) = [ph.sem(n) for n in (
             "w_loaded", "scaled", "affine_done", "rows_turned", "rows_copied", "up_done", "silu_done",
             "hidden_done", "hidden_turned", "hidden_copied", "down_done", "y_done")]
        block = ctx.enter_context(nc.Block())

        @block.sync
        def _(sp):
            sp.dma_start(ctx_rows[:, :, :], sh.dram["ctx_1024"].rearrange("b (q p) d -> p (b q) d", p=P)).then_inc(w_loaded, 16)
            sp.dma_start(w1[:, :], sh.dram["L2_xattn_W1"]).then_inc(w_loaded, 16)
            sp.dma_start(w2[:, :, :], sh.dram["L2_xattn_W2"].rearrange("(c p) d -> p c d", p=P)).then_inc(w_loaded, 16)
            for j, n in enumerate(("ln_g", "ln_b", "cln_g", "cln_b")):
                sp.dma_start(affine[:, j, :], sh.dram["L2_xattn_" + n].rearrange("(o d) -> o d", o=1).to_broadcast([P, D])).then_inc(w_loaded, 16)

        @block.gpsimd
        def _(pool):
            clear_retired(pool, sh)
            with pool.Fori(0, NB) as b:
                for i in (0, 2, 1):
                    pool_rstd(pool, sh, moments[i], moments_done[i], rstd_done[i], b)

        @block.tensor
        def _(pe):
            pe.wait_ge(w_loaded, 112)
            with pe.Fori(0, NB) as b:
                pe.wait_ge(affine_done, b + 1)
                for j in range(2):
                    for q in range(QT):
                        last = pe.transpose(turned_rows[:, j, P * q:P * (q + 1)], affine_rows[:, j, q, :], sh.ident[:, :])
                last.then_inc(rows_turned, 1)
                pe.wait_ge(rows_copied, b + 1)
                for q in range(QT):
                    for j in range(2):
                        last = pe.matmul(up[:, q, j, :], rowsT[:, P * q:P * (q + 1)], w1[:, F * j:F * (j + 1)], start=True, stop=True)
                    last.then_inc(up_done, 1)
                for q in range(QT):
                    pe.wait_ge(hidden_done, QT * b + q + 1)
                    for c in range(C):
                        last = pe.transpose(turned[:, q, c, :], hidden[:, q, P * c:P * (c + 1)], sh.ident[:, :])
                    last.then_inc(hidden_turned, 1)
                for q in range(QT):
                    pe.wait_ge(hidden_copied, QT * b + q + 1)
                    for c in range(C):
                        last = pe.matmul(down[:, D * q:D * (q + 1)], hiddenT[:, q, c, :], w2[:, c, :], start=(c == 0), stop=(c == C - 1))
                last.then_inc(down_done, 1)

        @block.scalar
        def _(act):
            with act.Fori(0, NB) as b:
                act.wait_ge(rows_turned, b + 1)
                act.activation(sh.xnT_all[:, bass.ds(b * S, S)], turned_rows[:, 0, :], ACT.Copy)
                act.activation(sh.cnT_all[:, bass.ds(b * S, S)], turned_rows[:, 1, :], ACT.Copy)
                act.activation(rowsT[:, :], turned_rows[:, 0, :], ACT.Copy).then_inc(rows_copied, 1)
                for q in range(QT):
                    act.wait_ge(up_done, QT * b + q + 1)
                    act.activation(silu[:, q, :], up[:, q, 1, :], ACT.Silu).then_inc(silu_done, 1)
                for q in range(QT):
                    act.wait_ge(hidden_turned, QT * b + q + 1)
                    act.activation(hiddenT[:, q, :, :], turned[:, q, :, :], ACT.Copy).then_inc(hidden_copied, 1)

        @block.vector
        def _(dve):
            dve.wait_ge(w_loaded, 112)
            with dve.Fori(0, NB) as b:
                x_rows = [sh.x_all[:, bass.ds(b * QT + q, 1), :].rearrange("p o d -> p (o d)") for q in range(QT)]
                c_rows = [ctx_rows[:, bass.ds(b * QT + q, 1), :].rearrange("p o d -> p (o d)") for q in range(QT)]
                mid = [x_mid[:, q, :] for q in range(QT)]
                dve_layernorm(dve, x_rows, mid, stats[0], moments[0], stats_done[0], moments_done[0], rstd_done[0], normed[0], LN_EPS, b)
                dve_layernorm(dve, c_rows, [normed_rows[:, 1, q, :] for q in range(QT)], stats[2], moments[2],
                              stats_done[2], moments_done[2], rstd_done[2], normed[2], LN_EPS, b)
                dve.wait_ge(normed[0], QT * (b + 1))
                dve_layernorm(dve, mid, [normed_rows[:, 0, q, :] for q in range(QT)], stats[1], moments[1],
                              stats_done[1], moments_done[1], rstd_done[1], normed[1], LN_EPS, b)
                dve.wait_ge(normed[1], QT * (b + 1))
                dve.wait_ge(normed[2], QT * (b + 1))
                for j in range(2):
                    dve.tensor_tensor(scaled_rows[:, j, :, :], normed_rows[:, j, :, :],
                                      affine[:, 2 * j, :].unsqueeze(1).to_broadcast([P, QT, D]), ALU.mult).then_inc(scaled, 1)
                dve.wait_ge(scaled, 2 * (b + 1))
                for j in range(2):
                    last = dve.tensor_tensor(affine_rows[:, j, :, :], scaled_rows[:, j, :, :],
                                             affine[:, 2 * j + 1, :].unsqueeze(1).to_broadcast([P, QT, D]), ALU.add)
                last.then_inc(affine_done, 1)
                for q in range(QT):
                    dve.wait_ge(silu_done, QT * b + q + 1)
                    dve.tensor_tensor(hidden[:, q, :], silu[:, q, :], up[:, q, 0, :], ALU.mult).then_inc(hidden_done, 1)
                dve.wait_ge(down_done, b + 1)
                dve.tensor_copy(sh.y_all[:, bass.ds(b * QT, QT), :], down[:, 0:QT * D].rearrange("p (q d) -> p q d", q=QT)).then_inc(y_done, 1)
        ph.retire(sh)


def phase_routed_ffn(nc, sh):
    E, F = 8, 512
    C = F // P
    STEPS = 10
    with ExitStack() as ctx:
        ph = Phase(nc, ctx, "l2r")
        cent_rows = ph.sbuf("cent_rows", [E, D])
        centT = ph.sbuf("centT", [P, E])
        affine = ph.sbuf("affine", [E, 2, D])
        w1 = ph.sbuf("w1", [P, E, F])
        w2 = ph.sbuf("w2", [P, C, E, D])
        bias1 = ph.sbuf("bias1", [E, F])
        bias2 = ph.sbuf("bias2", [E, D])
        stats = [ph.sbuf(f"stats{i}", [P, QT, 6]) for i in range(2)]
        moments = [ph.sbuf(f"moments{i}", [P, QT, 4]) for i in range(2)]
        x_in = ph.sbuf("x_in", [P, QT, D])
        x_inT = ph.sbuf("x_inT", [P, QT, P])
        xn = ph.sbuf("xn", [P, QT, D])
        logits = ph.sbuf("logits", [P, QT, E])
        top = ph.sbuf("top", [P, QT])
        first = ph.sbuf("first", [P, QT])
        onehot = ph.sbuf("onehot", [P, QT, E])
        onehotT = ph.sbuf("onehotT", [E, QT, P])
        alpha = ph.sbuf("alpha", [P, QT, 3])
        expert_rows = ph.sbuf("expert_rows", [P, QT, E, D])
        expert_rowsT = ph.sbuf("expert_rowsT", [P, QT, E, P])
        relu = ph.sbuf("relu", [P, QT, F])
        reluT = ph.sbuf("reluT", [P, QT, C, P])
        y = ph.sbuf("y", [P, QT, D])
        small = ph.psum("small", [P, 512])
        gathered = ph.psum("gathered", [P, QT, 2, D])
        turned = ph.psum("turned", [P, QT, 4, P])
        up = ph.psum("up", [P, 512])
        down = ph.psum("down", [P, E, D])
        bias_out = ph.psum("bias_out", [P, 512])
        stats_done = [ph.sem(f"stats_done{i}") for i in range(2)]
        moments_done = [ph.sem(f"moments_done{i}") for i in range(2)]
        rstd_done = [ph.sem(f"rstd_done{i}") for i in range(2)]
        normed = [ph.sem(f"normed{i}") for i in range(2)]
        (w_loaded, cent_turned, cent_copied, step, x_turned, x_copied, logits_done, logits_copied, chosen,
         choice_turned, choice_copied, gather_done, exp_done, rows_ready, rows_turned, rows_copied, up_done,
         relu_done, relu_turned, relu_copied, down_done, selected, selected_step, y_done) = [ph.sem(n) for n in (
             "w_loaded", "cent_turned", "cent_copied", "step", "x_turned", "x_copied", "logits_done",
             "logits_copied", "chosen", "choice_turned", "choice_copied", "gather_done", "exp_done",
             "rows_ready", "rows_turned", "rows_copied", "up_done", "relu_done", "relu_turned", "relu_copied",
             "down_done", "selected", "selected_step", "y_done")]
        block = ctx.enter_context(nc.Block())

        @block.sync
        def _(sp):
            sp.dma_start(cent_rows[:, :], sh.dram["L2_ffn_centroids"]).then_inc(w_loaded, 16)
            sp.dma_start(affine[:, 0, :], sh.dram["L2_ffn_ln_g"]).then_inc(w_loaded, 16)
            sp.dma_start(affine[:, 1, :], sh.dram["L2_ffn_ln_b"]).then_inc(w_loaded, 16)
            sp.dma_start(bias1[:, :], sh.dram["L2_ffn_b1"]).then_inc(w_loaded, 16)
            sp.dma_start(bias2[:, :], sh.dram["L2_ffn_b2"]).then_inc(w_loaded, 16)
            sp.dma_start(w1[:, :, :], sh.dram["L2_ffn_w1"].rearrange("e d f -> d e f")).then_inc(w_loaded, 16)
            for c in range(C):
                sp.dma_start(w2[:, c, :, :], sh.dram["L2_ffn_w2"][:, P * c:P * (c + 1), :].rearrange("e f d -> f e d")).then_inc(w_loaded, 16)

        @block.gpsimd
        def _(pool):
            clear_retired(pool, sh)
            with pool.Fori(0, NB) as b:
                for i in range(2):
                    pool_rstd(pool, sh, moments[i], moments_done[i], rstd_done[i], b)

        @block.tensor
        def _(pe):
            pe.wait_ge(w_loaded, 160)
            pe.transpose(small[:, 0:E], cent_rows[:, :], sh.ident[0:E, 0:E]).then_inc(cent_turned, 1)
            pe.wait_ge(cent_copied, 1)
            with pe.Fori(0, NB) as b:
                pe.wait_ge(normed[0], QT * (b + 1))
                for q in range(QT):
                    last = pe.transpose(small[:, P * q:P * (q + 1)], x_in[:, q, :], sh.ident[:, :])
                last.then_inc(x_turned, 1)
                pe.wait_ge(x_copied, b + 1)
                for q in range(QT):
                    last = pe.matmul(small[:, 2 * P + E * q:2 * P + E * (q + 1)], x_inT[:, q, :], centT[:, :], start=True, stop=True)
                last.then_inc(logits_done, 1)
                pe.wait_ge(logits_copied, b + 1)
                pe.wait_ge(chosen, b + 1)
                for q in range(QT):
                    last = pe.transpose(small[0:E, P * q:P * (q + 1)], onehot[:, q, :], sh.ident[:, :])
                last.then_inc(choice_turned, 1)
                pe.wait_ge(choice_copied, b + 1)
                for q in range(QT):
                    pe.matmul(gathered[:, q, :, :], onehotT[:, q, :], affine[:, :, :], start=True, stop=True)
                    last = pe.matmul(bias_out[:, D * q:D * (q + 1)], onehotT[:, q, :], bias2[:, :], start=True, stop=True)
                last.then_inc(gather_done, 1)
                for q in range(QT):
                    pe.wait_ge(rows_ready, QT * b + q + 1)
                    for g in range(2):
                        if (q, g) != (0, 0):
                            pe.wait_ge(rows_copied, 2 * QT * b + 2 * q + g)
                        for j in range(4):
                            last = pe.transpose(turned[:, g, j, :], expert_rows[:, q, 4 * g + j, :], sh.ident[:, :])
                        last.then_inc(rows_turned, 1)
                    pe.wait_ge(rows_copied, 2 * QT * b + 2 * q + 2)
                    if q:
                        pe.wait_ge(relu_done, QT * b + q)
                    for e in range(E):
                        pe.matmul(up[:, :], expert_rowsT[:, q, e, :], w1[:, e, :], start=(e == 0), stop=False)
                    pe.matmul(up[:, :], onehotT[:, q, :], bias1[:, :], start=False, stop=True).then_inc(up_done, 1)
                    pe.wait_ge(relu_done, QT * b + q + 1)
                    for c in range(C):
                        last = pe.transpose(turned[:, 0, c, :], relu[:, q, P * c:P * (c + 1)], sh.ident[:, :])
                    last.then_inc(relu_turned, 1)
                    pe.wait_ge(relu_copied, QT * b + q + 1)
                    if q:
                        pe.wait_ge(selected, QT * b + q)
                    for g in range(2):
                        for c in range(C):
                            last = pe.matmul(down[:, 4 * g:4 * g + 4, :], reluT[:, q, c, :], w2[:, c, 4 * g:4 * g + 4, :],
                                             start=(c == 0), stop=(c == C - 1))
                    last.then_inc(down_done, 1)

        @block.scalar
        def _(act):
            act.wait_ge(cent_turned, 1)
            act.activation(centT[:, :], small[:, 0:E], ACT.Copy).then_inc(cent_copied, 1)
            with act.Fori(0, NB) as b:
                act.wait_ge(x_turned, b + 1)
                act.activation(x_inT[:, :, :], small[:, 0:S].rearrange("p (q t) -> p q t", q=QT), ACT.Copy).then_inc(x_copied, 1)
                act.wait_ge(logits_done, b + 1)
                act.activation(logits[:, :, :], small[:, 2 * P:2 * P + QT * E].rearrange("p (q e) -> p q e", q=QT), ACT.Copy).then_inc(logits_copied, 1)
                act.wait_ge(choice_turned, b + 1)
                act.activation(onehotT[:, :, :], small[0:E, 0:S].rearrange("p (q t) -> p q t", q=QT), ACT.Copy).then_inc(choice_copied, 1)
                act.activation(alpha[:, :, 0], top[:, :], ACT.Exp, scale=-1.0).then_inc(exp_done, 1)
                for q in range(QT):
                    for g in range(2):
                        act.wait_ge(rows_turned, 2 * QT * b + 2 * q + g + 1)
                        act.activation(expert_rowsT[:, q, 4 * g:4 * g + 4, :], turned[:, g, :, :], ACT.Copy).then_inc(rows_copied, 1)
                    act.wait_ge(up_done, QT * b + q + 1)
                    act.activation(relu[:, q, :], up[:, :], ACT.Relu).then_inc(relu_done, 1)
                    act.wait_ge(relu_turned, QT * b + q + 1)
                    act.activation(reluT[:, q, :, :], turned[:, 0, :, :], ACT.Copy).then_inc(relu_copied, 1)

        @block.vector
        def _(dve):
            with dve.Fori(0, NB) as b:
                n = Counter(STEPS)
                rows = [sh.x_all[:, bass.ds(b * QT + q, 1), :].rearrange("p o d -> p (o d)") for q in range(QT)]
                inner = [x_in[:, q, :] for q in range(QT)]
                dve_layernorm(dve, rows, inner, stats[0], moments[0], stats_done[0], moments_done[0], rstd_done[0], normed[0], LN_EPS, b)
                dve.wait_ge(normed[0], QT * (b + 1))
                dve_layernorm(dve, inner, [xn[:, q, :] for q in range(QT)], stats[1], moments[1], stats_done[1],
                              moments_done[1], rstd_done[1], normed[1], LN_EPS, b)
                dve.wait_ge(logits_copied, b + 1)
                dve_choose(dve, sh, logits[:, :, :], top, first, onehot, step, n, b)
                dve.sem_inc(chosen, 1)
                dve.wait_ge(exp_done, b + 1)
                dve.tensor_scalar(alpha[:, :, 1], alpha[:, :, 0], 1.0, None, ALU.add).then_inc(step, n.up())
                dve.wait_ge(step, n.all(b))
                dve.reciprocal(alpha[:, :, 2], alpha[:, :, 1]).then_inc(step, n.up())
                dve.wait_ge(gather_done, b + 1)
                dve.wait_ge(normed[1], QT * (b + 1))
                dve.tensor_tensor(xn[:, :, :], xn[:, :, :], gathered[:, :, 0, :], ALU.mult).then_inc(step, n.up())
                dve.wait_ge(step, n.all(b))
                dve.tensor_tensor(xn[:, :, :], xn[:, :, :], gathered[:, :, 1, :], ALU.add).then_inc(step, n.up())
                dve.wait_ge(step, n.all(b))
                for q in range(QT):
                    for e in range(E):
                        last = dve.tensor_scalar(expert_rows[:, q, e, :], xn[:, q, :], onehot[:, q, e:e + 1], None, ALU.mult)
                    last.then_inc(rows_ready, 1)
                for q in range(QT):
                    dve.wait_ge(down_done, QT * b + q + 1)
                    for e in range(E):
                        before = bias_out[:, D * q:D * (q + 1)] if e == 0 else y[:, q, :]
                        if e == 0:
                            dve.tensor_copy(y[:, q, :], before).then_inc(selected_step, 1)
                            dve.wait_ge(selected_step, (E + 1) * (QT * b + q) + 1)
                        dve.scalar_tensor_tensor(out=y[:, q, :], in0=down[:, e, :], scalar=onehot[:, q, e:e + 1],
                                                 in1=y[:, q, :], op0=ALU.mult, op1=ALU.add).then_inc(selected_step, 1)
                        dve.wait_ge(selected_step, (E + 1) * (QT * b + q) + e + 2)
                    dve.sem_inc(selected, 1)
                for q in range(QT):
                    dve.scalar_tensor_tensor(out=y[:, q, :], in0=y[:, q, :], scalar=alpha[:, q, 2:3],
                                             in1=x_in[:, q, :], op0=ALU.mult, op1=ALU.add).then_inc(y_done, 1)
                dve.wait_ge(y_done, (QT + 1) * b + QT)
                out_rows = sh.x_all[:, bass.ds(b * QT, QT), :]
                dve.tensor_tensor(out_rows, out_rows, y[:, :, :], ALU.add).then_inc(y_done, 1)
                dve.wait_ge(y_done, (QT + 1) * (b + 1))
                n.close()
        ph.retire(sh)


def phase_head_softmax_attention(nc, sh):
    H, DH, U = 8, 16, 4
    G = 4
    W = P // G
    C = H // G
    with ExitStack() as ctx:
        ph = Phase(nc, ctx, "l3a")
        w_rows = ph.sbuf("w_rows", [P, 4, D])
        wo_rows = ph.sbuf("wo_rows", [P, H, W])
        wT = ph.sbuf("wT", [P, 3, D])
        wo = ph.sbuf("wo", [P, C, D])
        stats = ph.sbuf("stats", [P, NT, 6])
        moments = ph.sbuf("moments", [P, NT, 4])
        xn = ph.sbuf("xn", [P, NT, D])
        ctx_now = ph.sbuf("ctx_now", [P, S])
        q_head = ph.sbuf("q_head", [P, 2, H, S])
        kT = ph.sbuf("kT", [P, 2, S])
        values = ph.sbuf("values", [P, 2, QT, H, W])
        largest = ph.sbuf("largest", [P, 2, P])
        lowered = ph.sbuf("lowered", [P, 2, H, P])
        probs = ph.sbuf("probs", [P, 4, H, P])
        total = ph.sbuf("total", [P, 2, P])
        inverse = ph.sbuf("inverse", [P, 2, P])
        pairs = ph.sbuf("pairs", [P, 2, H // 2, P])
        mixedT = ph.sbuf("mixedT", [P, 2, QT, C, P])
        scores = [ph.psum(f"scores{i}", [P, H, P]) for i in range(2)]
        out_sums = [ph.psum(f"out_sums{i}", [P, 512]) for i in range(QT)]
        front_bank = ph.psum("front_bank", [P, 512])
        tail_bank = ph.psum("tail_bank", [P, 512])
        names = ["w_loaded", "padded", "w_turned", "w_copied", "stats_done", "moments_done", "rstd_done",
                 "normed", "x_turned", "x_copied", "front_filled", "front_copied", "ctx_ready", "scored", "exp_done",
                 "max_ready", "lowered_ready", "paired", "totalled", "inverted", "shared", "summed", "out_copied", "tail_filled", "tail_copied"]
        (w_loaded, padded, w_turned, w_copied, stats_done, moments_done, rstd_done, normed, x_turned, x_copied, front_filled,
         front_copied, ctx_ready, scored, exp_done, max_ready, lowered_ready, paired, totalled, inverted, shared, summed, out_copied,
         tail_filled, tail_copied) = [ph.sem(n) for n in names]
        block = ctx.enter_context(nc.Block())

        def run(eng, front, unit, finish, tail):
            def one(b, par, first, more):
                for u in range(U):
                    unit(b, par, u, first)
                    if u < 3 and more:
                        front(b + 1, 1 - par, False, u)
                    if u == 0 and not (isinstance(b, int) and b < 2):
                        tail(b - 2, par)

            for step in range(3):
                front(0, 0, True, step)
            one(0, 0, True, True)
            one(1, 1, False, True)
            with eng.Fori(2, NB - 2, 2) as b:
                one(b, 0, False, True)
                one(b + 1, 1, False, True)
            one(NB - 2, 0, False, True)
            one(NB - 1, 1, False, False)
            finish(NB - 1, 1)
            tail(NB - 2, 0)
            tail(NB - 1, 1)

        def behind(work, b, par, u, lag, first):
            if u >= lag:
                work(b, par, u - lag)
            elif not first:
                work(b - 1, 1 - par, U + u - lag)

        def nothing(*args):
            pass

        @block.sync
        def _(sp):
            for j, n in enumerate(("W_Q", "W_K", "W_V", "W_O")):
                sp.dma_start(w_rows[:, j, :], sh.dram["L3_xattn_" + n]).then_inc(w_loaded, 16)

        @block.gpsimd
        def _(pool):
            clear_retired(pool, sh)
            pool.memset(values[:, :, :, :, :], 0.0).then_inc(padded, 1)
            pool.memset(wo_rows[:, :, :], 0.0).then_inc(padded, 1)
            pool.wait_ge(moments_done, NT + 1)
            pool.tensor_tensor(moments[:, :, 3:4], moments[:, :, 2:3],
                               sh.half[:, 0:1].unsqueeze(2).to_broadcast([P, NT, 1]), ALU.pow).then_inc(rstd_done, 1)
            pool.wait_ge(padded, 2)
            pool.wait_ge(w_loaded, 64)
            pool.tensor_copy(wo_rows[:, :, 0:DH], w_rows[:, 3, :].rearrange("p (h d) -> p h d", h=H)).then_inc(padded, 1)

            def share(b, par, u):
                pool.wait_ge(inverted, U * b + u + 1)
                buf = probs[:, u, :, :]
                pool.tensor_tensor(buf, buf, inverse[:, u % 2, :].unsqueeze(1).to_broadcast([P, H, P]), ALU.mult).then_inc(shared, 1)

            def unit(b, par, u, first):
                pool.wait_ge(exp_done, U * b + u + 1)
                if not (first and u < 2):
                    pool.wait_ge(totalled, U * b + u - 1)
                pool.tensor_tensor(pairs[:, u % 2, :, :], probs[:, u, 0:H // 2, :], probs[:, u, H // 2:H, :], ALU.add).then_inc(paired, 1)
                behind(share, b, par, u, 1, first)

            run(pool, nothing, unit, lambda b, par: share(b, par, U - 1), nothing)

        @block.tensor
        def _(pe):
            pe.wait_ge(w_loaded, 64)
            for j in range(3):
                last = pe.transpose(front_bank[:, P * j:P * (j + 1)], w_rows[:, j, :], sh.ident[:, :])
            last.then_inc(w_turned, 1)
            for g in range(NT // 4):
                pe.wait_ge(normed, 4 * (g + 1))
                if g >= 2:
                    pe.wait_ge(x_copied, g - 1)
                for j in range(4):
                    last = pe.transpose(out_sums[g % 2][:, P * j:P * (j + 1)], xn[:, 4 * g + j, :], sh.ident[:, :])
                last.then_inc(x_turned, 1)
            pe.wait_ge(padded, 3)
            for c in range(C):
                last = pe.transpose(tail_bank[:, P * c:P * (c + 1)],
                                    wo_rows[:, G * c:G * (c + 1), :].rearrange("p g d -> p (g d)"), sh.ident[:, :])
            last.then_inc(w_turned, 1)
            pe.wait_ge(w_copied, 2)
            pe.wait_ge(x_copied, NT // 4)

            def front(b, par, first, step):
                if step == 1:
                    pe.wait_ge(ctx_ready, b + 1)
                    if not first:
                        pe.wait_ge(front_copied, 2 * b)
                    pe.matmul(front_bank[:, 0:S], wT[:, 0, :], sh.xnT_all[:, bass.ds(b * S, S)], start=True, stop=True)
                    pe.matmul(front_bank[:, S:2 * S], wT[:, 1, :], ctx_now[:, :], start=True, stop=True).then_inc(front_filled, 1)
                elif step == 2:
                    pe.wait_ge(front_copied, 2 * b + 1)
                    for t in range(QT):
                        last = pe.matmul(front_bank[:, D * t:D * (t + 1)], ctx_now[:, P * t:P * (t + 1)], wT[:, 2, :],
                                         start=True, stop=True)
                    last.then_inc(front_filled, 1)

            def value_products(b, par, u):
                q, t = u // 2, u % 2
                pe.wait_ge(shared, U * b + u + 1)
                if t == 0 and not (isinstance(b, int) and b == 0):
                    pe.wait_ge(out_copied, QT * (b - 1) + q + 1)
                for c in range(C):
                    for j in range(G):
                        last = pe.matmul(out_sums[q][W * j:W * (j + 1), P * c:P * (c + 1)], values[:, par, t, G * c + j, :],
                                         probs[:, u, G * c + j, :], start=(t == 0 and c == 0), stop=(t == QT - 1), skip_group_check=True)
                last.then_inc(summed, 1)

            def unit(b, par, u, first):
                q, t = u // 2, u % 2
                if u == 0:
                    pe.wait_ge(front_copied, 2 * (b + 1))
                if not (first and u < 2):
                    pe.wait_ge(lowered_ready, U * b + u - 1)
                for g in range(2):
                    last = pe.matmul(scores[u % 2][:, 4 * g:4 * g + 4, :], kT[:, par, P * t:P * (t + 1)],
                                     q_head[:, par, 4 * g:4 * g + 4, P * q:P * (q + 1)], start=True, stop=True)
                last.then_inc(scored, 1)
                behind(value_products, b, par, u, 3, first)

            def finish(b, par):
                value_products(b, par, U - 3)
                value_products(b, par, U - 2)
                value_products(b, par, U - 1)

            def tail(b, par):
                pe.wait_ge(out_copied, QT * (b + 1))
                if isinstance(b, int):
                    pe.wait_ge(tail_copied, b)
                for q in range(QT):
                    for c in range(C):
                        last = pe.matmul(tail_bank[:, D * q:D * (q + 1)], mixedT[:, par, q, c, :], wo[:, c, :],
                                         start=(c == 0), stop=(c == C - 1))
                last.then_inc(tail_filled, 1)

            run(pe, front, unit, finish, tail)

        @block.scalar
        def _(act):
            act.wait_ge(w_turned, 1)
            act.activation(wT[:, :, :], front_bank[:, 0:3 * P].rearrange("p (j d) -> p j d", j=3), ACT.Copy).then_inc(w_copied, 1)
            for g in range(NT // 4):
                act.wait_ge(x_turned, g + 1)
                act.activation(sh.xnT_all[:, 4 * P * g:4 * P * (g + 1)], out_sums[g % 2][:, :], ACT.Copy).then_inc(x_copied, 1)
            act.wait_ge(w_turned, 2)
            act.activation(wo[:, :, :], tail_bank[:, 0:C * P].rearrange("p (c d) -> p c d", c=C), ACT.Copy).then_inc(w_copied, 1)
            act.wait_ge(padded, 2)

            def front(b, par, first, step):
                if step == 0:
                    if not first:
                        act.wait_ge(front_filled, 2 * b)
                    act.activation(ctx_now[:, :], sh.ctxT[:, bass.ds(b * S, S)], ACT.Copy).then_inc(ctx_ready, 1)
                    return
                act.wait_ge(front_filled, 2 * b + step)
                if step == 1:
                    for h in range(H):
                        act.activation(q_head[:, par, h, :], front_bank[:, 0:S], ACT.Copy, scale=sh.head16[:, h:h + 1])
                    act.activation(kT[:, par, :], front_bank[:, S:2 * S], ACT.Copy, scale=float(DH) ** -0.5).then_inc(front_copied, 1)
                else:
                    act.activation(values[:, par, :, :, 0:DH],
                                   front_bank[:, 0:S].rearrange("p (t h d) -> p t h d", t=QT, h=H), ACT.Copy).then_inc(front_copied, 1)

            def copy_out(b, par, u):
                if u % 2 == 0:
                    return
                act.wait_ge(summed, U * b + u + 1)
                if not (isinstance(b, int) and b < 2):
                    act.wait_ge(tail_filled, b - 1)
                act.activation(mixedT[:, par, u // 2, :, :], out_sums[u // 2][:, 0:C * P].rearrange("p (c q) -> p c q", c=C),
                               ACT.Copy).then_inc(out_copied, 1)

            def unit(b, par, u, first):
                behind(copy_out, b, par, u, 4, first)
                act.wait_ge(lowered_ready, U * b + u + 1)
                if not first:
                    act.wait_ge(summed, U * b + u - 3)
                act.activation(probs[:, u, :, :], lowered[:, u % 2, :, :], ACT.Exp).then_inc(exp_done, 1)

            def finish(b, par):
                copy_out(b, par, 1)
                copy_out(b, par, 3)

            run(act, front, unit, finish, nothing)

        @block.vector
        def _(dve):
            for n in range(NT):
                dve.bn_stats(stats[:, n, :], sh.x_all[:, n, :]).then_inc(stats_done, 1)
            dve.wait_ge(stats_done, NT)
            for n in range(NT):
                dve.bn_aggr(moments[:, n, 0:2], stats[:, n, :]).then_inc(moments_done, 1)
            dve.wait_ge(moments_done, NT)
            dve.tensor_scalar(moments[:, :, 2:3], moments[:, :, 1:2], LN_EPS, None, ALU.add).then_inc(moments_done, 1)
            dve.wait_ge(rstd_done, 1)
            for n in range(NT):
                dve.tensor_scalar(xn[:, n, :], sh.x_all[:, n, :], moments[:, n, 0:1], moments[:, n, 3:4],
                                  ALU.subtract, ALU.mult).then_inc(normed, 1)

            def sum_heads(b, par, u):
                dve.wait_ge(paired, U * b + u + 1)
                dve.tensor_reduce(total[:, u % 2, :], pairs[:, u % 2, :, :].rearrange("p h q -> p q h"), AX.X, ALU.add).then_inc(totalled, 1)
                dve.wait_ge(totalled, U * b + u + 1)
                if not (isinstance(b, int) and b == 0 and u < 2):
                    dve.wait_ge(shared, U * b + u - 1)
                dve.reciprocal(inverse[:, u % 2, :], total[:, u % 2, :]).then_inc(inverted, 1)

            def unit(b, par, u, first):
                dve.wait_ge(scored, U * b + u + 1)
                dve.tensor_reduce(largest[:, u % 2, :], scores[u % 2][:, :, :].rearrange("p h q -> p q h"), AX.X, ALU.max).then_inc(max_ready, 1)
                dve.wait_ge(max_ready, U * b + u + 1)
                if not (first and u < 2):
                    dve.wait_ge(exp_done, U * b + u - 1)
                dve.tensor_tensor(lowered[:, u % 2, :, :], scores[u % 2][:, :, :],
                                  largest[:, u % 2, :].unsqueeze(1).to_broadcast([P, H, P]), ALU.subtract).then_inc(lowered_ready, 1)
                behind(sum_heads, b, par, u, 1, first)

            def tail(b, par):
                dve.wait_ge(tail_filled, b + 1)
                rows = sh.x_all[:, bass.ds(b * QT, QT), :]
                dve.tensor_tensor(rows, rows, tail_bank[:, 0:S].rearrange("p (q d) -> p q d", q=QT),
                                  ALU.add).then_inc(tail_copied, 1)

            run(dve, nothing, unit, lambda b, par: sum_heads(b, par, U - 1), tail)
        ph.retire(sh)


def phase_hard_expert_ffn(nc, sh):
    E, F = 4, 512
    C = F // P
    LN3_EPS = 1e-12
    STEPS = 6 + 2
    with ExitStack() as ctx:
        ph = Phase(nc, ctx, "l3f")
        router = ph.sbuf("router", [P, E])
        w1 = ph.sbuf("w1", [P, E, F])
        wo = ph.sbuf("wo", [P, C, D])
        bias1 = ph.sbuf("bias1", [E, F])
        bias_out = ph.sbuf("bias_out", [P, 3, D])
        stats = [ph.sbuf(f"stats{i}", [P, QT, 6]) for i in range(2)]
        moments = [ph.sbuf(f"moments{i}", [P, QT, 4]) for i in range(2)]
        x_in = ph.sbuf("x_in", [P, QT, D])
        x_inT = ph.sbuf("x_inT", [P, QT, P])
        logits = ph.sbuf("logits", [P, QT, E])
        top = ph.sbuf("top", [P, QT])
        first = ph.sbuf("first", [P, QT])
        onehot = ph.sbuf("onehot", [P, QT, E])
        onehotT = ph.sbuf("onehotT", [E, QT, P])
        expert_rows = ph.sbuf("expert_rows", [P, QT, E, D])
        expert_rowsT = ph.sbuf("expert_rowsT", [P, QT, E, P])
        gelu = ph.sbuf("gelu", [P, QT, F])
        geluT = ph.sbuf("geluT", [P, QT, C, P])
        y = ph.sbuf("y", [P, QT, D])
        yn = ph.sbuf("yn", [P, QT, D])
        small = ph.psum("small", [P, 512])
        turned = ph.psum("turned", [P, QT, 4, P])
        up = ph.psum("up", [P, QT, 512])
        down = ph.psum("down", [P, 512])
        stats_done = [ph.sem(f"stats_done{i}") for i in range(2)]
        moments_done = [ph.sem(f"moments_done{i}") for i in range(2)]
        rstd_done = [ph.sem(f"rstd_done{i}") for i in range(2)]
        normed = [ph.sem(f"normed{i}") for i in range(2)]
        (w_loaded, step, x_turned, x_copied, logits_done, logits_copied, chosen, choice_turned, choice_copied,
         rows_ready, rows_turned, rows_copied, up_done, gelu_done, gelu_turned, gelu_copied, down_done,
         y_ready, stored) = [ph.sem(n) for n in (
             "w_loaded", "step", "x_turned", "x_copied", "logits_done", "logits_copied", "chosen", "choice_turned",
             "choice_copied", "rows_ready", "rows_turned", "rows_copied", "up_done", "gelu_done", "gelu_turned",
             "gelu_copied", "down_done", "y_ready", "stored")]
        block = ctx.enter_context(nc.Block())

        @block.sync
        def _(sp):
            sp.dma_start(router[:, :], sh.dram["L3_ffn_W_router"]).then_inc(w_loaded, 16)
            sp.dma_start(bias1[:, :], sh.dram["L3_ffn_b1"]).then_inc(w_loaded, 16)
            for j, n in enumerate(("bo", "ln_gamma", "ln_beta")):
                sp.dma_start(bias_out[:, j, :], sh.dram["L3_ffn_" + n].rearrange("(o d) -> o d", o=1).to_broadcast([P, D])).then_inc(w_loaded, 16)
            sp.dma_start(w1[:, :, :], sh.dram["L3_ffn_W1"].rearrange("e d f -> d e f")).then_inc(w_loaded, 16)
            sp.dma_start(wo[:, :, :], sh.dram["L3_ffn_Wo"].rearrange("(c p) d -> p c d", p=P)).then_inc(w_loaded, 16)

        @block.gpsimd
        def _(pool):
            clear_retired(pool, sh)
            with pool.Fori(0, NB) as b:
                for i in range(2):
                    pool_rstd(pool, sh, moments[i], moments_done[i], rstd_done[i], b)

        @block.tensor
        def _(pe):
            pe.wait_ge(w_loaded, 112)
            with pe.Fori(0, NB) as b:
                pe.wait_ge(normed[0], QT * (b + 1))
                for q in range(QT):
                    last = pe.transpose(small[:, P * q:P * (q + 1)], x_in[:, q, :], sh.ident[:, :])
                last.then_inc(x_turned, 1)
                pe.wait_ge(x_copied, b + 1)
                for q in range(QT):
                    last = pe.matmul(small[:, 2 * P + E * q:2 * P + E * (q + 1)], x_inT[:, q, :], router[:, :], start=True, stop=True)
                last.then_inc(logits_done, 1)
                pe.wait_ge(logits_copied, b + 1)
                pe.wait_ge(chosen, b + 1)
                for q in range(QT):
                    last = pe.transpose(small[0:E, P * q:P * (q + 1)], onehot[:, q, :], sh.ident[:, :])
                last.then_inc(choice_turned, 1)
                pe.wait_ge(rows_ready, b + 1)
                for q in range(QT):
                    for e in range(E):
                        last = pe.transpose(turned[:, q, e, :], expert_rows[:, q, e, :], sh.ident[:, :])
                    last.then_inc(rows_turned, 1)
                pe.wait_ge(choice_copied, b + 1)
                for q in range(QT):
                    pe.wait_ge(rows_copied, QT * b + q + 1)
                    for e in range(E):
                        pe.matmul(up[:, q, :], expert_rowsT[:, q, e, :], w1[:, e, :], start=(e == 0), stop=False)
                    pe.matmul(up[:, q, :], onehotT[:, q, :], bias1[:, :], start=False, stop=True).then_inc(up_done, 1)
                for q in range(QT):
                    pe.wait_ge(gelu_done, QT * b + q + 1)
                    for c in range(C):
                        last = pe.transpose(turned[:, q, c, :], gelu[:, q, P * c:P * (c + 1)], sh.ident[:, :])
                    last.then_inc(gelu_turned, 1)
                for q in range(QT):
                    pe.wait_ge(gelu_copied, QT * b + q + 1)
                    for c in range(C):
                        last = pe.matmul(down[:, D * q:D * (q + 1)], geluT[:, q, c, :], wo[:, c, :], start=(c == 0), stop=(c == C - 1))
                last.then_inc(down_done, 1)

        @block.scalar
        def _(act):
            with act.Fori(0, NB) as b:
                act.wait_ge(x_turned, b + 1)
                act.activation(x_inT[:, :, :], small[:, 0:S].rearrange("p (q t) -> p q t", q=QT), ACT.Copy).then_inc(x_copied, 1)
                act.wait_ge(logits_done, b + 1)
                act.activation(logits[:, :, :], small[:, 2 * P:2 * P + QT * E].rearrange("p (q e) -> p q e", q=QT), ACT.Copy).then_inc(logits_copied, 1)
                act.wait_ge(choice_turned, b + 1)
                act.activation(onehotT[:, :, :], small[0:E, 0:S].rearrange("p (q t) -> p q t", q=QT), ACT.Copy).then_inc(choice_copied, 1)
                for q in range(QT):
                    act.wait_ge(rows_turned, QT * b + q + 1)
                    act.activation(expert_rowsT[:, q, :, :], turned[:, q, :, :], ACT.Copy).then_inc(rows_copied, 1)
                for q in range(QT):
                    act.wait_ge(up_done, QT * b + q + 1)
                    act.activation(gelu[:, q, :], up[:, q, :], ACT.Gelu).then_inc(gelu_done, 1)
                for q in range(QT):
                    act.wait_ge(gelu_turned, QT * b + q + 1)
                    act.activation(geluT[:, q, :, :], turned[:, q, :, :], ACT.Copy).then_inc(gelu_copied, 1)

        @block.vector
        def _(dve):
            dve.wait_ge(w_loaded, 112)
            with dve.Fori(0, NB) as b:
                n = Counter(STEPS)
                rows = [sh.x_all[:, bass.ds(b * QT + q, 1), :].rearrange("p o d -> p (o d)") for q in range(QT)]
                inner = [x_in[:, q, :] for q in range(QT)]
                dve_layernorm(dve, rows, inner, stats[0], moments[0], stats_done[0], moments_done[0], rstd_done[0], normed[0], LN_EPS, b)
                dve.wait_ge(logits_copied, b + 1)
                dve_choose(dve, sh, logits[:, :, :], top, first, onehot, step, n, b)
                dve.sem_inc(chosen, 1)
                for q in range(QT):
                    for e in range(E):
                        last = dve.tensor_scalar(expert_rows[:, q, e, :], x_in[:, q, :], onehot[:, q, e:e + 1], None, ALU.mult)
                last.then_inc(rows_ready, 1)
                dve.tensor_tensor(y[:, :, :], x_in[:, :, :], bias_out[:, 0, :].unsqueeze(1).to_broadcast([P, QT, D]), ALU.add).then_inc(y_ready, 1)
                dve.wait_ge(down_done, b + 1)
                dve.wait_ge(y_ready, 3 * b + 1)
                dve.tensor_tensor(y[:, :, :], y[:, :, :], down[:, 0:QT * D].rearrange("p (q d) -> p q d", q=QT), ALU.add).then_inc(y_ready, 1)
                dve.wait_ge(y_ready, 3 * b + 2)
                dve_layernorm(dve, [y[:, q, :] for q in range(QT)], [yn[:, q, :] for q in range(QT)], stats[1], moments[1],
                              stats_done[1], moments_done[1], rstd_done[1], normed[1], LN3_EPS, b)
                dve.wait_ge(normed[1], QT * (b + 1))
                dve.tensor_tensor(yn[:, :, :], yn[:, :, :], bias_out[:, 1, :].unsqueeze(1).to_broadcast([P, QT, D]), ALU.mult).then_inc(step, n.up())
                dve.wait_ge(step, n.all(b))
                dve.tensor_tensor(yn[:, :, :], yn[:, :, :], bias_out[:, 2, :].unsqueeze(1).to_broadcast([P, QT, D]), ALU.add).then_inc(step, n.up())
                dve.wait_ge(step, n.all(b))
                out_rows = sh.x_all[:, bass.ds(b * QT, QT), :]
                dve.tensor_tensor(out_rows, out_rows, yn[:, :, :], ALU.add).then_inc(y_ready, 1)
                dve.wait_ge(y_ready, 3 * (b + 1))
                n.close()
        ph.retire(sh)


INPUTS = [
    "x",
    "ctx_1024",
    "mask_BxS_bf1",
    "mask_BxS_ik0",
    "mask_BxSxS2_ff0",
    "L0_xattn_W_q",
    "L0_xattn_W_k",
    "L0_xattn_W_v",
    "L0_xattn_W_o",
    "L0_ffn_w1",
    "L0_ffn_b1",
    "L0_ffn_w2",
    "L0_ffn_b2",
    "L1_xattn_wq",
    "L1_xattn_wk",
    "L1_xattn_wv",
    "L1_xattn_wo",
    "L1_xattn_bq",
    "L1_xattn_bk",
    "L1_xattn_bv",
    "L1_xattn_bo",
    "L1_ffn_w1",
    "L1_ffn_w3",
    "L1_ffn_w2",
    "L2_xattn_ln_g",
    "L2_xattn_ln_b",
    "L2_xattn_cln_g",
    "L2_xattn_cln_b",
    "L2_xattn_Wq",
    "L2_xattn_Wkv",
    "L2_xattn_Wout",
    "L2_xattn_W1",
    "L2_xattn_W2",
    "L2_ffn_centroids",
    "L2_ffn_ln_g",
    "L2_ffn_ln_b",
    "L2_ffn_w1",
    "L2_ffn_b1",
    "L2_ffn_w2",
    "L2_ffn_b2",
    "L3_xattn_W_Q",
    "L3_xattn_W_K",
    "L3_xattn_W_V",
    "L3_xattn_W_O",
    "L3_ffn_W_router",
    "L3_ffn_W1",
    "L3_ffn_b1",
    "L3_ffn_Wo",
    "L3_ffn_bo",
    "L3_ffn_ln_gamma",
    "L3_ffn_ln_beta",
]


def build(nc, dram, out):
    with ExitStack() as ctx:
        sh = Shared(nc, ctx, dram)
        phase_setup(nc, sh)
        phase_clipped_attention(nc, sh)
        phase_ternary_ffn(nc, sh)
        phase_softmax_attention(nc, sh, False)
        phase_expert_ffn(nc, sh)
        phase_multi_query_inputs(nc, sh)
        phase_softmax_attention(nc, sh, True)
        phase_routed_ffn(nc, sh)
        phase_head_softmax_attention(nc, sh)
        phase_hard_expert_ffn(nc, sh)
        with ExitStack() as end:
            stored = end.enter_context(nc.semaphore("stored"))
            block = end.enter_context(nc.Block())

            @block.sync
            def _(sp):
                sp.dma_start(out.rearrange("b (q p) d -> p (b q) d", p=P), sh.x_all[:, :, :]).then_inc(stored, 16)
                sp.wait_ge(stored, 16)


def kernel(**inputs):
    import numpy as np
    import concourse.bacc as bacc
    from concourse.bass_utils import run_bass_kernel_spmd

    nc = bacc.Bacc("TRN2", target_bir_lowering=False, num_devices=1)
    arrays, dram = {}, {}
    for name in INPUTS:
        a = np.ascontiguousarray(inputs[name])
        if a.dtype == np.bool_:
            a = a.view(np.uint8)
        arrays["in_" + name] = a
        dram[name] = nc.dram_tensor("in_" + name, a.shape, mybir.dt.from_np(a.dtype), kind="ExternalInput").ap()
    shape = (NB, S, D)
    out = nc.dram_tensor("out", shape, F32, kind="ExternalOutput").ap()
    build(nc, dram, out)
    return run_bass_kernel_spmd(nc, [arrays], core_ids=[0]).results[0]["out"]
```

```python
from contextlib import ExitStack

import concourse.bass as bass
from concourse import mybir

F32 = mybir.dt.float32
BF16 = mybir.dt.bfloat16
ALU = mybir.AluOpType
ACT = mybir.ActivationFunctionType
AX = mybir.AxisListType

P = 128
D = 128
NB = 8
S = 256
QT = S // P
NT = NB * QT
LN_EPS = 1e-5
RMS_EPS = 1e-6
QUANT_EPS = 1e-5
ROUND = 1.5 * 2.0 ** 23
MASKED = -1e30
LARGEST = 3.4e38
EXP_LOW, EXP_HIGH = 1.9287498479639178e-22, 5.184705528587072e21


class Shared:

    def __init__(self, nc, ctx, dram):
        self.dram = dram
        self.retired_ctx, self.retired = ExitStack(), []
        self.x_all = ctx.enter_context(nc.sbuf_tensor("x_all", [P, NT, D], F32))
        self.ctxT = ctx.enter_context(nc.sbuf_tensor("ctxT", [P, NB * S], F32))
        self.ident = ctx.enter_context(nc.sbuf_tensor("ident", [P, P], F32))
        self.ident_bf = ctx.enter_context(nc.sbuf_tensor("ident_bf", [P, P], BF16))
        self.tri = ctx.enter_context(nc.sbuf_tensor("tri", [P, P], F32))
        self.ones = ctx.enter_context(nc.sbuf_tensor("ones", [P, P], F32))
        self.half = ctx.enter_context(nc.sbuf_tensor("half", [P, 4], F32))
        self.head8 = ctx.enter_context(nc.sbuf_tensor("head8", [P, 16], F32))
        self.head16 = ctx.enter_context(nc.sbuf_tensor("head16", [P, 8], F32))
        self.key_index = ctx.enter_context(nc.sbuf_tensor("key_index", [P, S], F32))
        self.expert_index = ctx.enter_context(nc.sbuf_tensor("expert_index", [P, 8], F32))
        self.query_mask = ctx.enter_context(nc.sbuf_tensor("query_mask", [P, NT], F32))
        self.last_patch = ctx.enter_context(nc.sbuf_tensor("last_patch", [P, NT], F32))
        self.xnT_all = ctx.enter_context(nc.sbuf_tensor("xnT_all", [P, NB * S], F32))
        self.cnT_all = ctx.enter_context(nc.sbuf_tensor("cnT_all", [P, NB * S], F32))
        self.y_all = ctx.enter_context(nc.sbuf_tensor("y_all", [P, NT, D], F32))


class Phase:

    def __init__(self, nc, ctx, name):
        self.nc, self.ctx, self.name = nc, ctx, name
        self.sem_ctx, self.sems = ExitStack(), []

    def sbuf(self, name, shape, dtype=F32):
        return self.ctx.enter_context(self.nc.sbuf_tensor(f"{self.name}_{name}", shape, dtype, align_bytes=64))

    def psum(self, name, shape, dtype=F32):
        return self.ctx.enter_context(self.nc.psum_tensor(f"{self.name}_{name}", shape, dtype))

    def sem(self, name):
        s = self.sem_ctx.enter_context(self.nc.semaphore(f"{self.name}_{name}"))
        self.sems.append(s)
        return s

    def retire(self, sh):
        sh.retired_ctx.close()
        sh.retired_ctx, sh.retired = self.sem_ctx, self.sems


def clear_retired(pool, sh):
    for s in sh.retired:
        pool.sem_clear(s)


class Counter:

    def __init__(self, per_batch):
        self.per_batch, self.n = per_batch, 0

    def up(self):
        self.n += 1
        return 1

    def all(self, b):
        return self.per_batch * b + self.n

    def close(self):
        assert self.n == self.per_batch, (self.n, self.per_batch)


def later(b, n=1):
    return not (isinstance(b, int) and b < n)


def overlapped(eng, order, front, back):
    def one(b, par, more):
        for name in order.split():
            if name[0] == "B":
                back(b, par, int(name[1:]))
            elif more:
                front(b + 1, 1 - par, int(name[1:]))

    for name in order.split():
        if name[0] == "F":
            front(0, 0, int(name[1:]))
    one(0, 0, True)
    one(1, 1, True)
    with eng.Fori(2, NB - 2, 2) as b:
        one(b, 0, True)
        one(b + 1, 1, True)
    one(NB - 2, 0, True)
    one(NB - 1, 1, False)


def nothing(*args):
    pass


def dve_choose(dve, sh, logits, top, first, onehot, step, n, b):
    E = logits.shape[2]
    index = sh.expert_index[:, 0:E].unsqueeze(1).to_broadcast([P, QT, E])
    dve.tensor_reduce(top[:, :], logits, AX.X, ALU.max).then_inc(step, n.up())
    dve.wait_ge(step, n.all(b))
    dve.tensor_tensor(onehot[:, :, :], logits, top[:, :].unsqueeze(2).to_broadcast([P, QT, E]), ALU.is_lt).then_inc(step, n.up())
    dve.wait_ge(step, n.all(b))
    dve.tensor_scalar(onehot[:, :, :], onehot[:, :, :], 16.0, None, ALU.mult).then_inc(step, n.up())
    dve.wait_ge(step, n.all(b))
    dve.tensor_tensor(onehot[:, :, :], onehot[:, :, :], index, ALU.add).then_inc(step, n.up())
    dve.wait_ge(step, n.all(b))
    dve.tensor_reduce(first[:, :], onehot[:, :, :], AX.X, ALU.min).then_inc(step, n.up())
    dve.wait_ge(step, n.all(b))
    dve.tensor_tensor(onehot[:, :, :], index, first[:, :].unsqueeze(2).to_broadcast([P, QT, E]), ALU.is_equal).then_inc(step, n.up())
    dve.wait_ge(step, n.all(b))


def phase_setup(nc, sh):
    with ExitStack() as ctx:
        ph = Phase(nc, ctx, "setup")
        ctx_rows = ph.sbuf("ctx_rows", [P, NT, D])
        mask_u8 = ph.sbuf("mask_u8", [P, NT], mybir.dt.uint8)
        mask_i32 = ph.sbuf("mask_i32", [P, NT], mybir.dt.int32)
        steps = ph.sbuf("steps", [P, NT])
        turned = [ph.psum(f"turned{i}", [P, 4, P]) for i in range(2)]
        sums = ph.psum("sums", [P, 512])
        loaded = ph.sem("loaded")
        masks_loaded = ph.sem("masks_loaded")
        blank = ph.sem("blank")
        consts = ph.sem("consts")
        steps_ready = ph.sem("steps_ready")
        sums_done = ph.sem("sums_done")
        turned_done = ph.sem("turned_done")
        turned_copied = ph.sem("turned_copied")
        block = ctx.enter_context(nc.Block())

        @block.sync
        def _(sp):
            sp.dma_start(ctx_rows[:, :, :], sh.dram["ctx_1024"].rearrange("b (q p) d -> p (b q) d", p=P)).then_inc(loaded, 16)
            sp.dma_start(sh.x_all[:, :, :], sh.dram["x"].rearrange("b (q p) d -> p (b q) d", p=P)).then_inc(loaded, 16)
            with nc.allow_non_contiguous_dma(reason="mask columns"):
                sp.dma_start(mask_u8[:, :], sh.dram["mask_BxS_bf1"].rearrange("b (q p) -> p (b q)", p=P)).then_inc(masks_loaded, 16)
                sp.dma_start(mask_i32[:, :], sh.dram["mask_BxS_ik0"].rearrange("b (q p) -> p (b q)", p=P)).then_inc(masks_loaded, 16)

        @block.gpsimd
        def _(pool):
            clear_retired(pool, sh)
            pool.memset(sh.ident[:, :], 0.0).then_inc(blank, 1)
            pool.memset(sh.ones[:, :], 1.0).then_inc(blank, 1)
            pool.memset(sh.tri[:, :], 1.0).then_inc(blank, 1)
            pool.memset(sh.head8[:, :], 1.0).then_inc(blank, 1)
            pool.memset(sh.head16[:, :], 1.0).then_inc(blank, 1)
            pool.memset(sh.half[:, :], -0.5).then_inc(blank, 1)
            pool.wait_ge(blank, 6)
            pool.affine_select(out=sh.ident[:, :], in_=sh.ident[:, :], compare_op=ALU.not_equal, fill=1.0,
                               base=0, pattern=[[-1, P]], channel_multiplier=1).then_inc(consts, 1)
            pool.affine_select(out=sh.tri[:, :], in_=sh.tri[:, :], compare_op=ALU.is_ge, fill=0.0,
                               base=0, pattern=[[1, P]], channel_multiplier=-1).then_inc(consts, 1)
            pool.affine_select(out=sh.head8[:, :], in_=sh.head8[:, :], compare_op=ALU.is_ge, fill=0.0,
                               base=0, pattern=[[-8, 16]], channel_multiplier=1).then_inc(consts, 1)
            pool.affine_select(out=sh.head16[:, :], in_=sh.head16[:, :], compare_op=ALU.is_ge, fill=0.0,
                               base=0, pattern=[[-16, 8]], channel_multiplier=1).then_inc(consts, 1)
            pool.iota(sh.key_index[:, :], [[1, S]], base=0, channel_multiplier=0,
                      allow_small_or_imprecise_dtypes=True).then_inc(consts, 1)
            pool.iota(sh.expert_index[:, :], [[1, 8]], base=0, channel_multiplier=0,
                      allow_small_or_imprecise_dtypes=True).then_inc(consts, 1)
            pool.wait_ge(consts, 6)
            pool.affine_select(out=sh.head8[:, :], in_=sh.head8[:, :], compare_op=ALU.is_ge, fill=0.0,
                               base=7, pattern=[[8, 16]], channel_multiplier=-1).then_inc(consts, 1)
            pool.affine_select(out=sh.head16[:, :], in_=sh.head16[:, :], compare_op=ALU.is_ge, fill=0.0,
                               base=15, pattern=[[16, 8]], channel_multiplier=-1).then_inc(consts, 1)
            pool.tensor_copy(sh.ident_bf[:, :], sh.ident[:, :]).then_inc(consts, 1)

        @block.tensor
        def _(pe):
            pe.wait_ge(consts, 6)
            pe.wait_ge(steps_ready, 2)
            pe.matmul(sums[:, 0:NT], sh.tri[:, :], steps[:, :], start=True, stop=True)
            pe.matmul(sums[:, NT:2 * NT], sh.ones[:, :], steps[:, :], start=True, stop=True).then_inc(sums_done, 1)
            pe.wait_ge(loaded, 32)
            for g in range(NT // 4):
                if g >= 2:
                    pe.wait_ge(turned_copied, g - 1)
                for j in range(4):
                    last = pe.transpose(turned[g % 2][:, j, :], ctx_rows[:, 4 * g + j, :], sh.ident[:, :])
                last.then_inc(turned_done, 1)

        @block.scalar
        def _(act):
            for g in range(NT // 4):
                act.wait_ge(turned_done, g + 1)
                act.activation(sh.ctxT[:, 512 * g:512 * (g + 1)].rearrange("p (a b) -> p a b", a=4),
                               turned[g % 2][:, :, :], ACT.Copy).then_inc(turned_copied, 1)

        @block.vector
        def _(dve):
            dve.wait_ge(masks_loaded, 32)
            dve.tensor_copy(sh.query_mask[:, :], mask_u8[:, :]).then_inc(steps_ready, 1)
            dve.tensor_copy(steps[:, :], mask_i32[:, :]).then_inc(steps_ready, 1)
            dve.wait_ge(sums_done, 1)
            dve.tensor_copy(sh.last_patch[:, :], sums[:, 0:NT]).then_inc(steps_ready, 1)
            dve.wait_ge(steps_ready, 3)
            odd = sh.last_patch[:, :].rearrange("p (b q) -> p b q", q=QT)[:, :, 1]
            even_total = sums[:, NT:2 * NT].rearrange("p (b q) -> p b q", q=QT)[:, :, 0]
            dve.tensor_tensor(odd, odd, even_total, ALU.add).then_inc(steps_ready, 1)

        ph.retire(sh)


def dve_moments(dve, src, stats, moments, stats_done, moments_done, eps, b):
    for q in range(QT):
        dve.bn_stats(stats[:, q, :], src[q]).then_inc(stats_done, 1)
    dve.wait_ge(stats_done, (QT + 1) * b + QT)
    dve.sem_inc(stats_done, 1)
    for q in range(QT):
        dve.bn_aggr(moments[:, q, 0:2], stats[:, q, :]).then_inc(moments_done, 1)
    dve.wait_ge(moments_done, (QT + 1) * b + QT)
    dve.tensor_scalar(moments[:, :, 2:3], moments[:, :, 1:2], eps, None, ALU.add).then_inc(moments_done, 1)


def dve_normalise(dve, src, out, moments, rstd_done, normed, b):
    dve.wait_ge(rstd_done, b + 1)
    for q in range(QT):
        dve.tensor_scalar(out[q], src[q], moments[:, q, 0:1], moments[:, q, 3:4],
                          ALU.subtract, ALU.mult).then_inc(normed, 1)


def dve_layernorm(dve, src, out, stats, moments, stats_done, moments_done, rstd_done, normed, eps, b):
    dve_moments(dve, src, stats, moments, stats_done, moments_done, eps, b)
    dve_normalise(dve, src, out, moments, rstd_done, normed, b)


def pool_rstd(pool, sh, moments, moments_done, rstd_done, b):
    pool.wait_ge(moments_done, (QT + 1) * (b + 1))
    pool.tensor_tensor(moments[:, :, 3:4], moments[:, :, 2:3], sh.half[:, 0:QT].rearrange("p (q o) -> p q o", o=1),
                       ALU.pow).then_inc(rstd_done, 1)


def dve_layernorm_all(dve, sh, out, stats, moments, stats_done, moments_done, rstd_done, normed):
    for n in range(NT):
        dve.bn_stats(stats[:, n, :], sh.x_all[:, n, :]).then_inc(stats_done, 1)
    dve.wait_ge(stats_done, NT)
    for n in range(NT):
        dve.bn_aggr(moments[:, n, 0:2], stats[:, n, :]).then_inc(moments_done, 1)
    dve.wait_ge(moments_done, NT)
    dve.tensor_scalar(moments[:, :, 2:3], moments[:, :, 1:2], LN_EPS, None, ALU.add).then_inc(moments_done, 1)
    dve.wait_ge(rstd_done, 1)
    for n in range(NT):
        dve.tensor_scalar(out[:, n, :], sh.x_all[:, n, :], moments[:, n, 0:1], moments[:, n, 3:4],
                          ALU.subtract, ALU.mult).then_inc(normed, 1)


def pool_rstd_all(pool, sh, moments, moments_done, rstd_done):
    pool.wait_ge(moments_done, NT + 1)
    pool.tensor_tensor(moments[:, :, 3:4], moments[:, :, 2:3],
                       sh.half[:, 0:1].unsqueeze(2).to_broadcast([P, NT, 1]), ALU.pow).then_inc(rstd_done, 1)


class Stacks:

    def __init__(self, ph, heads, width):
        self.heads, self.width = heads, width
        pairs = [(i, j) for i in range(3) for j in range(3)]
        if len(pairs) * width > P:
            pairs = [(i, j) for i, j in pairs if i + j <= 2]
        self.counts = [sum(1 for first, _ in pairs if first == i) for i in range(3)]
        self.LOADS = len(pairs) + 3
        self.rows = len(pairs) * width
        self.exact = ph.sbuf("exact", [P, 2, S])
        self.rest = ph.sbuf("rest", [P, 2, S])
        self.parts = ph.sbuf("parts", [P, 2, 3, S], BF16)
        self.stacked = ph.sbuf("stacked", [self.rows, 2, 2, heads, S], BF16)
        self.bounce = ph.nc.dram_tensor(f"{ph.name}_bounce", [2, 3, P, S], BF16, kind="Internal").ap()
        self.split = ph.sem("split")
        self.stored = ph.sem("stored")
        self.stacked_ready = ph.sem("stacked_ready")
        self.free = ph.sem("free")

    def split_parts(self, dve, b):
        parts, rest = self.parts, self.rest
        dve.tensor_copy(parts[:, :, 0, :], self.exact[:, :, :]).then_inc(self.split, 1)
        dve.wait_ge(self.split, 4 * b + 1)
        dve.tensor_tensor(rest[:, :, :], self.exact[:, :, :], parts[:, :, 0, :], ALU.subtract).then_inc(self.split, 1)
        dve.wait_ge(self.split, 4 * b + 2)
        dve.tensor_copy(parts[:, :, 1, :], rest[:, :, :]).then_inc(self.split, 1)
        dve.wait_ge(self.split, 4 * b + 3)
        dve.tensor_tensor(parts[:, :, 2, :], rest[:, :, :], parts[:, :, 1, :], ALU.subtract).then_inc(self.split, 1)

    def load(self, sp, b, par):
        sp.wait_ge(self.split, 4 * (b + 1))
        sp.dma_start(self.bounce.rearrange("s a p t -> p (s a) t"),
                     self.parts[:, :, :, :].rearrange("p s a t -> p (s a) t")).then_inc(self.stored, 16)
        sp.wait_ge(self.stored, 16 * (b + 1))
        row, width = 0, self.width
        for i, count in enumerate(self.counts):
            query_part = self.bounce[0, i, :, :].rearrange("(d h) t -> d h t", h=self.heads)
            key_parts = self.bounce[1, 0:count, :, :].rearrange("a (d h) t -> (a d) h t", h=self.heads)
            sp.dma_start(self.stacked[row:row + width * count, par, 1, :, :], key_parts).then_inc(self.stacked_ready, 16)
            for _ in range(count):
                sp.dma_start(self.stacked[row:row + width, par, 0, :, :], query_part).then_inc(self.stacked_ready, 16)
                row += width


def phase_clipped_attention(nc, sh):
    H, DH, G, U = 16, 8, 4, 8
    after = ["F2", "F4 F3", "T0", "T1", "T2", "T3 G0", "G5", "G1"]
    W = P // G
    with ExitStack() as ctx:
        ph = Phase(nc, ctx, "l0a")
        w_rows = ph.sbuf("w_rows", [P, 4, D])
        wT = ph.sbuf("wT", [P, 4, D])
        stats = ph.sbuf("stats", [P, QT, 6])
        moments = ph.sbuf("moments", [P, QT, 4])
        xn = ph.sbuf("xn", [P, QT, D])
        xnT = ph.sbuf("xnT", [P, S])
        ctx_now = ph.sbuf("ctx_now", [P, S])
        stacks = Stacks(ph, H, DH)
        v_one = ph.sbuf("v_one", [P, 2, QT, H, W])
        probs = ph.sbuf("probs", [P, 2, G, S])
        outT = ph.sbuf("outT", [P, G, S])
        inverse = ph.sbuf("inverse", [P, QT, H])
        mixed = ph.sbuf("mixed", [P, QT, H, DH])
        mixedT = ph.sbuf("mixedT", [P, S])
        scores = [ph.psum(f"scores{i}", [P, G, S]) for i in range(2)]
        out_sums = ph.psum("out_sums", [P, G, S])
        front_bank = ph.psum("front_bank", [P, 512])
        tail_bank = ph.psum("tail_bank", [P, 512])
        (w_loaded, w_turned, w_copied, ones_set, stats_done, moments_done, rstd_done, normed, front_filled,
         front_copied, ctx_ready, scored, exp_done, clipped, summed, out_copied, inverted, mixed_ready,
         tail_filled, tail_copied) = [ph.sem(n) for n in (
             "w_loaded", "w_turned", "w_copied", "ones_set", "stats_done", "moments_done", "rstd_done", "normed",
             "front_filled", "front_copied", "ctx_ready", "scored", "exp_done", "clipped", "summed", "out_copied",
             "inverted", "mixed_ready", "tail_filled", "tail_copied")]
        block = ctx.enter_context(nc.Block())

        def run(eng, front, unit, finish, tail):
            def one(b, par, first, more=True, second=True):
                for u in range(U):
                    unit(b, par, u, first)
                    for name in after[u].split():
                        kind, k = name[0], int(name[1])
                        if kind == "F" and more:
                            front(b + 1, 1 - par, False, k)
                        if kind == "G" and second:
                            front(b + 2, par, False, k)
                        if kind == "T" and not first:
                            tail(b - 1, 1 - par, k)

            for step in (0, 5, 1, 2, 3, 4):
                front(0, 0, True, step)
            for step in (0, 5, 1):
                front(1, 1, False, step)
            one(0, 0, True)
            one(1, 1, False)
            with eng.Fori(1, NB // 2 - 1) as pair:
                one(pair * 2, 0, False)
                one(pair * 2 + 1, 1, False)
            one(NB - 2, 0, False, True, False)
            one(NB - 1, 1, False, False, False)
            finish(NB - 1, 1)
            for step in range(4):
                tail(NB - 1, 1, step)

        def nothing(*args):
            pass

        @block.sync
        def _(sp):
            for j, n in enumerate(("W_q", "W_k", "W_v", "W_o")):
                sp.dma_start(w_rows[:, j, :], sh.dram["L0_xattn_" + n]).then_inc(w_loaded, 16)

            def front(b, par, first, step):
                if step:
                    return
                if not first:
                    sp.wait_ge(stacks.stacked_ready, 16 * stacks.LOADS * b)
                    sp.sem_inc(stacks.free, 1)
                if not (isinstance(b, int) and b < 2):
                    sp.wait_ge(scored, U * (b - 1))
                    sp.sem_inc(stacks.free, 1)
                stacks.load(sp, b, par)

            run(sp, front, nothing, nothing, nothing)

        @block.gpsimd
        def _(pool):
            clear_retired(pool, sh)
            pool.memset(v_one[:, :, :, :, :], 0.0).then_inc(ones_set, 1)
            pool.wait_ge(ones_set, 1)
            pool.memset(v_one[:, :, :, :, DH:DH + 1], 1.0).then_inc(ones_set, 1)

            def front(b, par, first, step):
                if step:
                    return
                if not first:
                    pool.wait_ge(front_filled, 3 * b)
                pool.tensor_copy(ctx_now[:, :], sh.ctxT[:, bass.ds(b * S, S)]).then_inc(ctx_ready, 1)
                pool_rstd(pool, sh, moments, moments_done, rstd_done, b)

            run(pool, front, nothing, nothing, nothing)

        @block.tensor
        def _(pe):
            pe.wait_ge(w_loaded, 64)
            for j in range(4):
                last = pe.transpose(front_bank[:, P * j:P * (j + 1)], w_rows[:, j, :], sh.ident[:, :])
            last.then_inc(w_turned, 1)
            pe.wait_ge(w_copied, 1)

            def front(b, par, first, step):
                if step == 1:
                    pe.wait_ge(normed, QT * (b + 1))
                    if not first:
                        pe.wait_ge(front_copied, 3 * b)
                    for q in range(QT):
                        last = pe.transpose(front_bank[:, P * q:P * (q + 1)], xn[:, q, :], sh.ident[:, :])
                    last.then_inc(front_filled, 1)
                elif step == 2:
                    pe.wait_ge(front_copied, 3 * b + 1)
                    pe.wait_ge(ctx_ready, b + 1)
                    pe.matmul(front_bank[:, 0:S], wT[:, 0, :], xnT[:, :], start=True, stop=True)
                    pe.matmul(front_bank[:, S:2 * S], wT[:, 1, :], ctx_now[:, :], start=True, stop=True).then_inc(front_filled, 1)
                elif step == 3:
                    pe.wait_ge(front_copied, 3 * b + 2)
                    for t in range(QT):
                        last = pe.matmul(front_bank[:, D * t:D * (t + 1)], ctx_now[:, P * t:P * (t + 1)], wT[:, 2, :],
                                         start=True, stop=True)
                    last.then_inc(front_filled, 1)

            def value_products(b, par, u):
                g, t = u // 2, u % 2
                pe.wait_ge(clipped, U * b + u + 1)
                if u == 0:
                    pe.wait_ge(front_copied, 3 * b + 3)
                if u in (0, 4) and not (isinstance(b, int) and b == 0):
                    pe.wait_ge(out_copied, 2 * b - 1 + u // 4)
                for j in range(G):
                    last = pe.matmul(out_sums[W * j:W * (j + 1), g, :], v_one[:, par, t, G * g + j, :],
                                     probs[:, u % 2, j, :], start=(t == 0), stop=(t == QT - 1))
                last.then_inc(summed, 1)

            def unit(b, par, u, first):
                g, t = u // 2, u % 2
                if u == 0:
                    pe.wait_ge(stacks.stacked_ready, 16 * stacks.LOADS * (b + 1))
                if not (first and u < 2):
                    pe.wait_ge(exp_done, U * b + u - 1)
                for j in range(G):
                    h = G * g + j
                    last = pe.matmul(scores[u % 2][:, j, :], stacks.stacked[:, par, 1, h, P * t:P * (t + 1)],
                                     stacks.stacked[:, par, 0, h, :], start=True, stop=True)
                last.then_inc(scored, 1)
                if u:
                    value_products(b, par, u - 1)
                elif not first:
                    value_products(b - 1, 1 - par, U - 1)

            def tail(b, par, step):
                if step < QT:
                    if step:
                        pe.wait_ge(mixed_ready, QT * b + step)
                    else:
                        pe.wait_ge(out_copied, 2 * (b + 1))
                        if not (isinstance(b, int) and b == 0):
                            pe.wait_ge(tail_copied, 2 * b)
                    for g in range(G):
                        last = pe.transpose(tail_bank[:, P * g:P * (g + 1)], outT[:, g, P * step:P * (step + 1)], sh.ident[:, :])
                    last.then_inc(tail_filled, 1)
                elif step == 2:
                    pe.wait_ge(mixed_ready, QT * (b + 1))
                    for q in range(QT):
                        last = pe.transpose(tail_bank[:, P * q:P * (q + 1)],
                                            mixed[:, q, :, :].rearrange("p h d -> p (h d)"), sh.ident[:, :])
                    last.then_inc(tail_filled, 1)
                else:
                    pe.wait_ge(tail_copied, 2 * b + 1)
                    for q in range(QT):
                        last = pe.matmul(tail_bank[:, D * q:D * (q + 1)], mixedT[:, P * q:P * (q + 1)], wT[:, 3, :],
                                         start=True, stop=True)
                    last.then_inc(tail_filled, 1)

            run(pe, front, unit, lambda b, par: value_products(b, par, U - 1), tail)

        @block.scalar
        def _(act):
            act.wait_ge(w_turned, 1)
            act.activation(wT[:, 0:2, :].rearrange("p j (d h) -> p j d h", h=H),
                           front_bank[:, 0:2 * P].rearrange("p (j h d) -> p j d h", j=2, h=H), ACT.Copy)
            act.activation(wT[:, 2:4, :], front_bank[:, 2 * P:4 * P].rearrange("p (j d) -> p j d", j=2), ACT.Copy).then_inc(w_copied, 1)
            act.wait_ge(ones_set, 2)

            def front(b, par, first, step):
                if step not in (1, 2, 3):
                    return
                act.wait_ge(front_filled, 3 * b + step)
                if step == 1:
                    act.activation(xnT[:, :], front_bank[:, 0:S], ACT.Copy).then_inc(front_copied, 1)
                elif step == 2:
                    if not first:
                        act.wait_ge(stacks.split, 4 * b)
                    act.activation(stacks.exact[:, 0, :], front_bank[:, 0:S], ACT.Copy, scale=float(DH) ** -0.5)
                    act.activation(stacks.exact[:, 1, :], front_bank[:, S:2 * S], ACT.Copy).then_inc(front_copied, 1)
                else:
                    act.activation(v_one[:, par, :, :, 0:DH],
                                   front_bank[:, 0:S].rearrange("p (t h d) -> p t h d", t=QT, h=H), ACT.Copy).then_inc(front_copied, 1)

            def copy_out(b, half):
                act.wait_ge(summed, U * b + 4 * (half + 1))
                if not (isinstance(b, int) and b == 0):
                    act.wait_ge(tail_filled, 4 * b - 2)
                act.activation(outT[:, 2 * half:2 * half + 2, :], out_sums[:, 2 * half:2 * half + 2, :], ACT.Copy).then_inc(out_copied, 1)

            def unit(b, par, u, first):
                act.wait_ge(scored, U * b + u + 1)
                if not (first and u < 2):
                    act.wait_ge(summed, U * b + u - 1)
                act.activation(probs[:, u % 2, :, :], scores[u % 2][:, :, :], ACT.Exp).then_inc(exp_done, 1)
                if u == 5:
                    copy_out(b, 0)
                if u == 1 and not first:
                    copy_out(b - 1, 1)

            run(act, front, unit, lambda b, par: copy_out(b, 1), nothing)

        @block.vector
        def _(dve):
            def front(b, par, first, step):
                rows = [sh.x_all[:, bass.ds(b * QT + q, 1), :].rearrange("p o d -> p (o d)") for q in range(QT)]
                if step == 0:
                    dve_moments(dve, rows, stats, moments, stats_done, moments_done, LN_EPS, b)
                elif step == 5:
                    if not first:
                        dve.wait_ge(front_filled, 3 * b - 2)
                    dve_normalise(dve, rows, [xn[:, q, :] for q in range(QT)], moments, rstd_done, normed, b)
                elif step == 4:
                    dve.wait_ge(front_copied, 3 * b + 2)
                    if not first:
                        dve.wait_ge(stacks.stored, 16 * b)
                    stacks.split_parts(dve, b)

            def unit(b, par, u, first):
                dve.wait_ge(exp_done, U * b + u + 1)
                buf = probs[:, u % 2, :, :]
                dve.tensor_scalar(buf, buf, EXP_LOW, EXP_HIGH, ALU.max, ALU.min).then_inc(clipped, 1)

            def tail(b, par, step):
                sums = tail_bank[:, :].rearrange("p (h w) -> p h w", w=W)
                dve.wait_ge(tail_filled, 4 * b + step + 1)
                if step < QT:
                    q = step
                    dve.reciprocal(inverse[:, q, :], sums[:, :, DH]).then_inc(inverted, 1)
                    dve.wait_ge(inverted, 2 * (QT * b + q) + 1)
                    dve.tensor_scalar(inverse[:, q, :], inverse[:, q, :],
                                      sh.query_mask[:, bass.ds(b * QT + q, 1)], None, ALU.mult).then_inc(inverted, 1)
                    dve.wait_ge(inverted, 2 * (QT * b + q) + 2)
                    dve.tensor_tensor(mixed[:, q, :, :], sums[:, :, 0:DH],
                                      inverse[:, q, :].unsqueeze(2).to_broadcast([P, H, DH]), ALU.mult).then_inc(mixed_ready, 1)
                elif step == 2:
                    dve.tensor_copy(mixedT[:, :], tail_bank[:, 0:S]).then_inc(tail_copied, 1)
                else:
                    rows = sh.x_all[:, bass.ds(b * QT, QT), :]
                    dve.tensor_tensor(rows, rows, tail_bank[:, 0:S].rearrange("p (q d) -> p q d", q=QT),
                                      ALU.add).then_inc(tail_copied, 1)

            run(dve, front, unit, nothing, tail)
        ph.retire(sh)


class Quantiser:

    def __init__(self, ph, dve, name, rows, width, rms, rounded, quant, deq, w_mean, row_sum, root, quantised, counts_before):
        self.dve, self.rows, self.width, self.rms, self.rounded, self.quant = dve, rows, width, rms, rounded, quant
        self.deq, self.w_mean, self.row_sum, self.root, self.quantised = deq, w_mean, row_sum, root, quantised
        self.step, self.per_batch = ph.sem(name + "_step"), counts_before + 7 + 2 * QT
        self.n = Counter(self.per_batch)

    def begin(self):
        self.n = Counter(self.per_batch)

    def largest(self, b):
        dve, rms, step, n = self.dve, self.rms, self.step, self.n
        dve.tensor_reduce(rms[:, :, 3], self.rows[:, :, :], AX.X, ALU.max, apply_absolute_value=True).then_inc(step, n.up())
        dve.wait_ge(step, n.all(b))
        dve.tensor_scalar(rms[:, :, 0], rms[:, :, 2], 1.0 / self.width, RMS_EPS, ALU.mult, ALU.add).then_inc(self.row_sum, 1)

    def scales(self, b):
        dve, rms, step, n = self.dve, self.rms, self.step, self.n
        dve.wait_ge(self.root, b + 1)
        dve.tensor_tensor(rms[:, :, 2], rms[:, :, 3], rms[:, :, 1], ALU.mult).then_inc(step, n.up())
        for q in range(QT):
            dve.tensor_scalar(self.rounded[:, q, :], self.rows[:, q, :], rms[:, q, 1:2], None, ALU.mult).then_inc(step, n.up())
        dve.wait_ge(step, n.all(b))
        dve.tensor_scalar(rms[:, :, 2], rms[:, :, 2], QUANT_EPS, None, ALU.max).then_inc(step, n.up())
        dve.wait_ge(step, n.all(b))
        dve.reciprocal(rms[:, :, 3], rms[:, :, 2]).then_inc(step, n.up())
        dve.tensor_scalar(self.deq[:, :], rms[:, :, 2], self.w_mean, 1.0 / 127.0, ALU.mult, ALU.mult).then_inc(step, n.up())
        dve.wait_ge(step, n.all(b))
        dve.tensor_scalar(rms[:, :, 3], rms[:, :, 3], 127.0, None, ALU.mult).then_inc(step, n.up())
        dve.wait_ge(step, n.all(b))

    def round(self, b):
        dve, rms, step, n, rounded = self.dve, self.rms, self.step, self.n, self.rounded
        for q in range(QT):
            dve.tensor_scalar(rounded[:, q, :], rounded[:, q, :], rms[:, q, 3:4], ROUND, ALU.mult, ALU.add).then_inc(step, n.up())
        dve.wait_ge(step, n.all(b))
        dve.tensor_scalar(rounded[:, :, :], rounded[:, :, :], ROUND, -128.0, ALU.subtract, ALU.max).then_inc(step, n.up())
        dve.wait_ge(step, n.all(b))
        dve.tensor_scalar(self.quant[:, :, :], rounded[:, :, :], 127.0, None, ALU.min).then_inc(self.quantised, 1)
        n.close()


def phase_ternary_ffn(nc, sh):
    F = 512
    C = F // P
    with ExitStack() as ctx:
        ph = Phase(nc, ctx, "l0f")
        w1_rows = ph.sbuf("w1_rows", [P, C, D])
        w2_rows = ph.sbuf("w2_rows", [P, F])
        magnitude = ph.sbuf("magnitude", [P, 2])
        w_scale = ph.sbuf("w_scale", [P, 2, 2])
        w_round = ph.sbuf("w_round", [P, 2, F])
        w_tern = ph.sbuf("w_tern", [P, 2, F], BF16)
        w1q = ph.sbuf("w1q", [P, F], BF16)
        w2q = ph.sbuf("w2q", [P, C, D], BF16)
        bias1 = ph.sbuf("bias1", [P, F])
        bias2 = ph.sbuf("bias2", [P, D])
        stats = ph.sbuf("stats", [P, QT, 6])
        moments = ph.sbuf("moments", [P, QT, 4])
        xn = ph.sbuf("xn", [P, QT, D])
        x_squares = ph.sbuf("x_squares", [P, QT, D])
        out = ph.sbuf("out", [P, QT, D])
        squares = ph.sbuf("squares", [P, QT, F])
        rms1 = ph.sbuf("rms1", [P, QT, 4])
        rms2 = ph.sbuf("rms2", [P, QT, 4])
        deq1 = ph.sbuf("deq1", [P, QT])
        deq2 = ph.sbuf("deq2", [P, QT])
        rounded1 = ph.sbuf("rounded1", [P, QT, D])
        quant1 = ph.sbuf("quant1", [P, QT, D], BF16)
        quant1T = ph.sbuf("quant1T", [P, QT, P], BF16)
        hidden = ph.sbuf("hidden", [P, QT, F])
        gelu = ph.sbuf("gelu", [P, QT, F])
        rounded2 = ph.sbuf("rounded2", [P, QT, F])
        quant2 = ph.sbuf("quant2", [P, QT, F], BF16)
        quant2T = ph.sbuf("quant2T", [P, QT, C, P], BF16)
        turned1 = ph.psum("turned1", [P, QT, 512], BF16)
        turned2 = ph.psum("turned2", [P, QT, 1024], BF16)
        up = ph.psum("up", [P, QT, F])
        down = ph.psum("down", [P, 512])
        (loaded, summed, totals, scaled, wrounded, ternary, w_turned, w_copied, stats_done, moments_done, rstd_done,
         normed, row1, root1, scale1, quantised1, turned1_done, copied1, up_done, hidden_done, gelu_done, squared2,
         row2, root2, scale2, quantised2, turned2_done, copied2, down_done, added) = [ph.sem(n) for n in (
             "loaded", "summed", "totals", "scaled", "wrounded", "ternary", "w_turned", "w_copied", "stats_done",
             "moments_done", "rstd_done", "normed", "row1", "root1", "scale1", "quantised1", "turned1_done",
             "copied1", "up_done", "hidden_done", "gelu_done", "squared2", "row2", "root2", "scale2",
             "quantised2", "turned2_done", "copied2", "down_done", "added")]
        block = ctx.enter_context(nc.Block())

        @block.sync
        def _(sp):
            sp.dma_start(w1_rows[:, :, :], sh.dram["L0_ffn_w1"].rearrange("(c p) i -> p c i", p=P)).then_inc(loaded, 16)
            sp.dma_start(w2_rows[:, :], sh.dram["L0_ffn_w2"]).then_inc(loaded, 16)
            sp.dma_start(bias1[:, :], sh.dram["L0_ffn_b1"].rearrange("(o f) -> o f", o=1).to_broadcast([P, F])).then_inc(loaded, 16)
            sp.dma_start(bias2[:, :], sh.dram["L0_ffn_b2"].rearrange("(o f) -> o f", o=1).to_broadcast([P, D])).then_inc(loaded, 16)

        ORDER = "F0 B0 F1 B1 F2 B2 F3 F4 B3"

        @block.gpsimd
        def _(pool):
            clear_retired(pool, sh)

            def front(b, par, k):
                if k == 0:
                    pool_rstd(pool, sh, moments, moments_done, rstd_done, b)
                elif k == 1:
                    pool.wait_ge(row1, b + 1)
                    pool.tensor_tensor(rms1[:, :, 1:2], rms1[:, :, 0:1], sh.half[:, 0:QT].unsqueeze(2), ALU.pow).then_inc(root1, 1)

            def back(b, par, k):
                if k == 1:
                    pool.wait_ge(row2, b + 1)
                    pool.tensor_tensor(rms2[:, :, 1:2], rms2[:, :, 0:1], sh.half[:, 0:QT].unsqueeze(2), ALU.pow).then_inc(root2, 1)

            overlapped(pool, ORDER, front, back)

        @block.tensor
        def _(pe):
            pe.wait_ge(summed, 2)
            pe.matmul(down[:, 0:2], sh.ones[:, :], magnitude[:, :], start=True, stop=True).then_inc(totals, 1)
            pe.wait_ge(ternary, 2)
            for j in range(2):
                for c in range(C):
                    last = pe.transpose(turned2[:, j, P * c:P * (c + 1)], w_tern[:, j, P * c:P * (c + 1)], sh.ident_bf[:, :])
            last.then_inc(w_turned, 1)
            pe.wait_ge(w_copied, 2)

            def front(b, par, k):
                if k == 4:
                    pe.wait_ge(quantised1, b + 1)
                    for q in range(QT):
                        last = pe.transpose(turned1[:, q, 0:P], quant1[:, q, :], sh.ident_bf[:, :])
                    last.then_inc(turned1_done, 1)

            def back(b, par, k):
                if k == 0:
                    pe.wait_ge(copied1, b + 1)
                    for q in range(QT):
                        pe.matmul(up[:, q, :], quant1T[:, q, :], w1q[:, :], start=True, stop=True).then_inc(up_done, 1)
                elif k == 2:
                    pe.wait_ge(quantised2, b + 1)
                    for q in range(QT):
                        for c in range(C):
                            last = pe.transpose(turned2[:, q, P * c:P * (c + 1)], quant2[:, q, P * c:P * (c + 1)], sh.ident_bf[:, :])
                        last.then_inc(turned2_done, 1)
                elif k == 3:
                    for q in range(QT):
                        pe.wait_ge(copied2, QT * b + q + 1)
                        for c in range(C):
                            last = pe.matmul(down[:, D * q:D * (q + 1)], quant2T[:, q, c, :], w2q[:, c, :],
                                             start=(c == 0), stop=(c == C - 1))
                    last.then_inc(down_done, 1)

            overlapped(pe, ORDER, front, back)

        @block.scalar
        def _(act):
            act.wait_ge(w_turned, 1)
            act.activation(w1q[:, :], turned2[:, 0, 0:F], ACT.Copy).then_inc(w_copied, 1)
            act.activation(w2q[:, :, :], turned2[:, 1, 0:F].rearrange("p (c o) -> p c o", c=C), ACT.Copy).then_inc(w_copied, 1)

            def front(b, par, k):
                if k == 4:
                    act.wait_ge(turned1_done, b + 1)
                    act.activation(quant1T[:, :, :], turned1[:, :, 0:P], ACT.Copy).then_inc(copied1, 1)

            def back(b, par, k):
                if k == 0:
                    for q in range(QT):
                        act.wait_ge(hidden_done, QT * b + q + 1)
                        act.activation(gelu[:, q, :], hidden[:, q, :], ACT.Gelu).then_inc(gelu_done, 1)
                    for q in range(QT):
                        act.wait_ge(gelu_done, QT * b + q + 1)
                        act.activation(squares[:, q, :], gelu[:, q, :], ACT.Square, accum_out=rms2[:, q, 2:3]).then_inc(squared2, 1)
                elif k == 2:
                    for q in range(QT):
                        act.wait_ge(turned2_done, QT * b + q + 1)
                        act.activation(quant2T[:, q, :, :], turned2[:, q, 0:F].rearrange("p (c t) -> p c t", c=C), ACT.Copy).then_inc(copied2, 1)

            overlapped(act, ORDER, front, back)

        @block.vector
        def _(dve):
            dve.wait_ge(loaded, 64)
            dve.tensor_reduce(magnitude[:, 0:1], w1_rows[:, :, :].rearrange("p c i -> p (c i)"), AX.X, ALU.add, apply_absolute_value=True).then_inc(summed, 1)
            dve.tensor_reduce(magnitude[:, 1:2], w2_rows[:, :], AX.X, ALU.add, apply_absolute_value=True).then_inc(summed, 1)
            dve.wait_ge(totals, 1)
            dve.tensor_scalar(w_scale[:, :, 0], down[:, 0:2], 1.0 / (F * D), QUANT_EPS, ALU.mult, ALU.max).then_inc(scaled, 1)
            dve.wait_ge(scaled, 1)
            dve.reciprocal(w_scale[:, :, 1], w_scale[:, :, 0]).then_inc(scaled, 1)
            dve.wait_ge(scaled, 2)
            for j, w in enumerate((w1_rows[:, :, :].rearrange("p c i -> p (c i)"), w2_rows[:, :])):
                dve.tensor_scalar(w_round[:, j, :], w, w_scale[:, j, 1:2], ROUND, ALU.mult, ALU.add).then_inc(wrounded, 1)
            for j in range(2):
                dve.wait_ge(wrounded, 2 + j)
                dve.tensor_scalar(w_round[:, j, :], w_round[:, j, :], ROUND, 1.0, ALU.subtract, ALU.min).then_inc(wrounded, 1)
            dve.wait_ge(wrounded, 4)
            for j in range(2):
                dve.tensor_scalar(w_tern[:, j, :], w_round[:, j, :], -1.0, None, ALU.max).then_inc(ternary, 1)

            first = Quantiser(ph, dve, "first", xn, D, rms1, rounded1, quant1, deq1, w_scale[:, 0, 0:1], row1, root1, quantised1, 2)
            second = Quantiser(ph, dve, "second", gelu, F, rms2, rounded2, quant2, deq2, w_scale[:, 1, 0:1], row2, root2, quantised2, 0)

            def front(b, par, k):
                rows = [sh.x_all[:, bass.ds(b * QT + q, 1), :].rearrange("p o d -> p (o d)") for q in range(QT)]
                if k == 0:
                    dve_moments(dve, rows, stats, moments, stats_done, moments_done, LN_EPS, b)
                elif k == 1:
                    first.begin()
                    n, step = first.n, first.step
                    if later(b):
                        dve.wait_ge(quantised1, b)
                    dve_normalise(dve, rows, [xn[:, q, :] for q in range(QT)], moments, rstd_done, normed, b)
                    dve.wait_ge(normed, QT * (b + 1))
                    dve.tensor_tensor(x_squares[:, :, :], xn[:, :, :], xn[:, :, :], ALU.mult).then_inc(step, n.up())
                    dve.wait_ge(step, n.all(b))
                    dve.tensor_reduce(rms1[:, :, 2], x_squares[:, :, :], AX.X, ALU.add).then_inc(step, n.up())
                    first.largest(b)
                elif k == 2:
                    first.scales(b)
                elif k == 3:
                    if later(b):
                        dve.wait_ge(turned1_done, b)
                    first.round(b)

            def back(b, par, k):
                if k == 0:
                    for q in range(QT):
                        dve.wait_ge(up_done, QT * b + q + 1)
                        dve.scalar_tensor_tensor(out=hidden[:, q, :], in0=up[:, q, :], scalar=deq1[:, q:q + 1],
                                                 in1=bias1[:, :], op0=ALU.mult, op1=ALU.add).then_inc(hidden_done, 1)
                elif k == 1:
                    second.begin()
                    dve.wait_ge(squared2, QT * (b + 1))
                    second.largest(b)
                elif k == 2:
                    second.scales(b)
                    if later(b):
                        dve.wait_ge(turned2_done, QT * b)
                    second.round(b)
                else:
                    dve.wait_ge(down_done, b + 1)
                    for q in range(QT):
                        dve.scalar_tensor_tensor(out=out[:, q, :], in0=down[:, D * q:D * (q + 1)], scalar=deq2[:, q:q + 1],
                                                 in1=bias2[:, :], op0=ALU.mult, op1=ALU.add).then_inc(added, 1)
                    dve.wait_ge(added, (QT + 1) * b + QT)
                    out_rows = sh.x_all[:, bass.ds(b * QT, QT), :]
                    dve.tensor_tensor(out_rows, out_rows, out[:, :, :], ALU.add).then_inc(added, 1)
                    dve.wait_ge(added, (QT + 1) * (b + 1))

            overlapped(dve, ORDER, front, back)
        ph.retire(sh)


def phase_softmax_attention(nc, sh, multi_query):
    H, G, U = 16, 4, 8
    DH = 64 if multi_query else 8
    W = 64 if multi_query else 32
    C = H * W // P
    CU = C * QT // U
    FC = 5 if multi_query else 3
    if multi_query:
        after = ["F0", "F1", "F2", "F3", "F4", "T0", "T1", ""]
    else:
        after = ["F2", "F3", "F5", "F4", "", "T0", "T1 G0", "G1"]
    FILLS = range(5) if multi_query else range(2, 5)
    with ExitStack() as ctx:
        ph = Phase(nc, ctx, "l2a" if multi_query else "l1a")
        if multi_query:
            wq = ph.sbuf("wq", [P, H * DH])
            wkv = ph.sbuf("wkv", [P, 3 * DH])
        else:
            w_rows = ph.sbuf("w_rows", [P, 4, D])
            wo_rows = ph.sbuf("wo_rows", [P, H, W])
            wT = ph.sbuf("wT", [P, 3, D])
            bias_cols = ph.sbuf("bias_cols", [P, 2])
            bias_q = ph.sbuf("bias_q", [P, 1])
            bias_rows = ph.sbuf("bias_rows", [1, 2, D])
            stats = ph.sbuf("stats", [P, QT, 6])
            moments = ph.sbuf("moments", [P, QT, 4])
            xn = ph.sbuf("xn", [P, QT, D])
            xnT = ph.sbuf("xnT", [P, S])
            stacks = Stacks(ph, H, DH)
        ctx_now = ph.sbuf("ctx_now", [P, S])
        if multi_query:
            qT = ph.sbuf("qT", [P, 2, C, S])
            kT = ph.sbuf("kT", [P, 2, S])
        wo = ph.sbuf("wo", [P, C, D])
        values = ph.sbuf("values", [P, 2, QT, 1 if multi_query else H, W])
        mask = ph.sbuf("mask", [P, 2, QT, S])
        masked = ph.sbuf("masked", [P, 2, G, S])
        minus_max = ph.sbuf("minus_max", [P, 2, G])
        probs = ph.sbuf("probs", [P, 4, G, S])
        sums = ph.sbuf("sums", [P, 4, G])
        inverse = ph.sbuf("inverse", [P, 4, G])
        probsT = ph.sbuf("probsT", [P, 2, G, QT, P])
        mixedT = ph.sbuf("mixedT", [P, 2, QT, C, P])
        scores = [ph.psum(f"scores{i}", [P, G, S]) for i in range(2)]
        turned = ph.psum("turned", [P, G, QT, P])
        out_sums = ph.psum("out_sums", [P, 512])
        side = ph.psum("side", [P, 512])
        out_view = out_sums[:, 0:CU * P].rearrange("p (c q) -> p c q", c=CU)
        (w_loaded, wkv_loaded, wo_loaded, w_turned, w_copied, bias_scaled, stats_done, moments_done, rstd_done, normed, front_filled,
         front_copied, tail_filled, tail_copied, ctx_ready, mask_ready, waited, unit_begun, scored, max_ready, exp_done,
         turned_done, turned_copied, summed, inverted, scaled, mixed_ready, added, padded) = [ph.sem(n) for n in (
             "w_loaded", "wkv_loaded", "wo_loaded", "w_turned", "w_copied", "bias_scaled", "stats_done", "moments_done", "rstd_done",
             "normed", "front_filled", "front_copied", "tail_filled", "tail_copied", "ctx_ready", "mask_ready", "waited", "unit_begun",
             "scored", "max_ready", "exp_done", "turned_done", "turned_copied", "summed",
             "inverted", "scaled", "mixed_ready", "added", "padded")]
        block = ctx.enter_context(nc.Block())

        def head_of(j):
            return 2 * (j % 2) + j // 2 if multi_query else j

        def run(eng, front, unit, finish, tail):
            def one(b, par, first, more, second=True):
                before = ("F", FC - 1, b) if isinstance(b, int) and b < 2 else ("T", b - 2)
                for u in range(U):
                    unit(b, par, u, first)
                    for name in after[u].split():
                        kind, k = name[0], int(name[1])
                        if kind == "F" and more:
                            front(b + 1, 1 - par, False, k, before)
                            if k in FILLS:
                                before = ("F", FILLS.index(k), b + 1)
                        if kind == "G" and second:
                            front(b + 2, par, False, k, before)
                        if kind == "T" and not first:
                            tail(b - 1, 1 - par, k, before)
                            before = ("T", b - 1)

            before = None
            for k in range(6):
                front(0, 0, True, k, before)
                if k in FILLS:
                    before = ("F", FILLS.index(k), 0)
            for name in " ".join(after).split():
                if name[0] == "G":
                    front(1, 1, False, int(name[1]), before)
            one(0, 0, True, True)
            one(1, 1, False, True)
            with eng.Fori(1, NB // 2 - 1) as pair:
                one(pair * 2, 0, False, True)
                one(pair * 2 + 1, 1, False, True)
            one(NB - 2, 0, False, True, False)
            one(NB - 1, 1, False, False, False)
            finish(NB - 1, 1)
            for k in range(2):
                tail(NB - 1, 1, k, ("T", NB - 2))

        def behind(work, b, par, u, lag, first):
            if u >= lag:
                work(b, par, u - lag)
            elif not first:
                work(b - 1, 1 - par, U + u - lag)

        def wait_side_free(pe, before):
            if before is not None:
                if before[0] == "F":
                    pe.wait_ge(front_copied, FC * before[2] + before[1] + 1)
                else:
                    pe.wait_ge(tail_copied, before[1] + 1)

        def nothing(*args):
            pass

        @block.sync
        def _(sp):
            if multi_query:
                sp.dma_start(wq[:, :], sh.dram["L2_xattn_Wq"]).then_inc(w_loaded, 16)
                for j in range(2):
                    sp.dma_start(wkv[:, DH * j:DH * (j + 1)], sh.dram["L2_xattn_Wkv"][:, 0:DH]).then_inc(wkv_loaded, 16)
                sp.dma_start(wkv[:, 2 * DH:3 * DH], sh.dram["L2_xattn_Wkv"][:, DH:2 * DH]).then_inc(wkv_loaded, 16)
                sp.dma_start(wo[:, :, :], sh.dram["L2_xattn_Wout"].rearrange("(c p) d -> p c d", p=P)).then_inc(wo_loaded, 16)

                def front(b, par, first, k, before):
                    if k:
                        return
                    if not first:
                        sp.wait_ge(mask_ready, 16 * b)
                        sp.sem_inc(waited, 1)
                    if not (isinstance(b, int) and b < 2):
                        sp.wait_ge(max_ready, U * (b - 1))
                    sp.dma_start(mask[:, par, :, :], sh.dram["mask_BxSxS2_ff0"][bass.ds(b, 1), :, :]
                                 .rearrange("o (q p) k -> p (o q) k", p=P)).then_inc(mask_ready, 16)
            else:
                for j, n in enumerate(("wq", "wk", "wv", "wo")):
                    sp.dma_start(w_rows[:, j, :], sh.dram["L1_xattn_" + n]).then_inc(w_loaded, 16)
                with nc.allow_non_contiguous_dma(reason="bias columns"):
                    for j, n in enumerate(("bq", "bk")):
                        column = sh.dram["L1_xattn_" + n].rearrange("(h d o) -> d h o", h=H, o=1)
                        for d in range(DH):
                            sp.dma_start(bias_cols[H * d:H * (d + 1), j:j + 1], column[d]).then_inc(w_loaded, 16)
                for j, n in enumerate(("bv", "bo")):
                    sp.dma_start(bias_rows[:, j, :], sh.dram["L1_xattn_" + n].rearrange("(o d) -> o d", o=1)).then_inc(w_loaded, 16)

                def front(b, par, first, k, before):
                    if k:
                        return
                    if not first:
                        sp.wait_ge(stacks.stacked_ready, 16 * stacks.LOADS * b)
                        sp.sem_inc(stacks.free, 1)
                    if not (isinstance(b, int) and b < 2):
                        sp.wait_ge(scored, U * (b - 1))
                        sp.sem_inc(stacks.free, 1)
                    stacks.load(sp, b, par)

            run(sp, front, nothing, nothing, nothing)

        @block.gpsimd
        def _(pool):
            clear_retired(pool, sh)
            if not multi_query:
                pool.memset(values[:, :, :, :, :], 0.0).then_inc(padded, 1)
                pool.memset(wo_rows[:, :, :], 0.0).then_inc(padded, 1)
                pool.wait_ge(padded, 2)
                pool.wait_ge(w_loaded, 16 * (6 + 2 * DH))
                pool.tensor_copy(wo_rows[:, :, 0:DH], w_rows[:, 3, :].rearrange("p (h d) -> p h d", h=H)).then_inc(padded, 1)

            def scale(b, par, u):
                pool.wait_ge(inverted, U * b + u + 1)
                buf = probs[:, u % 4, :, :]
                pool.tensor_tensor(buf, buf, inverse[:, u % 4, :].unsqueeze(2).to_broadcast([P, G, S]), ALU.mult).then_inc(scaled, 1)

            def front(b, par, first, k, before):
                if k:
                    return
                if not first:
                    pool.wait_ge(front_filled, FC * b)
                source = sh.cnT_all if multi_query else sh.ctxT
                pool.tensor_copy(ctx_now[:, :], source[:, bass.ds(b * S, S)]).then_inc(ctx_ready, 1)
                if not multi_query:
                    pool_rstd(pool, sh, moments, moments_done, rstd_done, b)

            run(pool, front, lambda b, par, u, first: behind(scale, b, par, u, 1, first),
                lambda b, par: scale(b, par, U - 1), nothing)

        @block.tensor
        def _(pe):
            if not multi_query:
                pe.wait_ge(w_loaded, 16 * (6 + 2 * DH))
                for j in range(3):
                    last = pe.transpose(side[:, P * j:P * (j + 1)], w_rows[:, j, :], sh.ident[:, :])
                last.then_inc(w_turned, 1)
                pe.wait_ge(padded, 3)
                for c in range(C):
                    last = pe.transpose(out_sums[:, P * c:P * (c + 1)],
                                        wo_rows[:, G * c:G * (c + 1), :].rearrange("p g d -> p (g d)"), sh.ident[:, :])
                last.then_inc(w_turned, 1)
                pe.wait_ge(w_copied, 2)
            else:
                pe.wait_ge(w_loaded, 16)

            def front(b, par, first, k, before):
                if k not in FILLS:
                    return
                wait_side_free(pe, before)
                fill = FILLS.index(k)
                if multi_query:
                    if fill < 4:
                        for j in range(2):
                            last = pe.matmul(side[:, S * j:S * (j + 1)], wq[:, P * (2 * fill + j):P * (2 * fill + j + 1)],
                                             sh.xnT_all[:, bass.ds(b * S, S)], start=True, stop=True)
                    else:
                        if not later(b):
                            pe.wait_ge(wkv_loaded, 48)
                        pe.wait_ge(ctx_ready, b + 1)
                        pe.matmul(side[:, 0:S], wkv[:, 0:2 * DH], ctx_now[:, :], start=True, stop=True)
                        for t in range(QT):
                            last = pe.matmul(side[:, S + DH * t:S + DH * (t + 1)], ctx_now[:, P * t:P * (t + 1)],
                                             wkv[:, 2 * DH:3 * DH], start=True, stop=True)
                elif fill == 0:
                    pe.wait_ge(normed, QT * (b + 1))
                    for q in range(QT):
                        last = pe.transpose(side[:, P * q:P * (q + 1)], xn[:, q, :], sh.ident[:, :])
                elif fill == 1:
                    pe.wait_ge(ctx_ready, b + 1)
                    pe.wait_ge(front_copied, FC * b + 1)
                    pe.matmul(side[:, 0:S], wT[:, 0, :], xnT[:, :], start=True, stop=True)
                    last = pe.matmul(side[:, S:2 * S], wT[:, 1, :], ctx_now[:, :], start=True, stop=True)
                else:
                    for t in range(QT):
                        pe.matmul(side[:, D * t:D * (t + 1)], ctx_now[:, P * t:P * (t + 1)], wT[:, 2, :], start=True, stop=False)
                        last = pe.matmul(side[:, D * t:D * (t + 1)], sh.ones[0:1, :], bias_rows[:, 0, :], start=False, stop=True)
                last.then_inc(front_filled, 1)

            def turn(b, par, u):
                pe.wait_ge(scaled, U * b + u + 1)
                if not (isinstance(b, int) and b == 0 and u == 0):
                    pe.wait_ge(turned_copied, U * b + u)
                for j in range(G):
                    for t in range(QT):
                        last = pe.transpose(turned[:, j, t, :], probs[:, u % 4, j, P * t:P * (t + 1)], sh.ident[:, :])
                last.then_inc(turned_done, 1)

            def value_products(b, par, u):
                pe.wait_ge(turned_copied, U * b + u + 1)
                if not (isinstance(b, int) and b == 0 and u == 0):
                    pe.wait_ge(mixed_ready, U * b + u)
                for t in range(QT):
                    if multi_query:
                        for odd in range(2):
                            last = pe.matmul(out_view[W * odd:W * (odd + 1), :, :], values[:, par, t, 0, :],
                                             probsT[:, u % 2, 2 * odd:2 * odd + 2, t, :], start=(t == 0), stop=(t == QT - 1))
                    else:
                        for j in range(G):
                            last = pe.matmul(out_view[W * j:W * (j + 1), 0, :], values[:, par, t, G * (u % 4) + j, :],
                                             probsT[:, u % 2, j, t, :], start=(t == 0), stop=(t == QT - 1))
                last.then_inc(summed, 1)

            def unit(b, par, u, first):
                q, g = u // 4, u % 4
                if u == 0:
                    pe.wait_ge(front_copied, FC * (b + 1))
                    if not multi_query:
                        pe.wait_ge(stacks.stacked_ready, 16 * stacks.LOADS * (b + 1))
                if not (first and u < 2):
                    pe.wait_ge(max_ready, U * b + u - 1)
                for j in (0, 2, 1, 3):
                    h = G * g + head_of(j)
                    if multi_query:
                        rows = slice(DH * (h % 2), DH * (h % 2 + 1))
                        last = pe.matmul(scores[u % 2][:, j, :], qT[rows, par, h // 2, P * q:P * (q + 1)],
                                         kT[rows, par, :], start=True, stop=True)
                    else:
                        last = pe.matmul(scores[u % 2][:, j, :], stacks.stacked[:, par, 0, h, P * q:P * (q + 1)],
                                         stacks.stacked[:, par, 1, h, :], start=True, stop=True)
                last.then_inc(scored, 1)
                behind(turn, b, par, u, 3, first)
                behind(value_products, b, par, u, 4, first)

            def finish(b, par):
                value_products(b, par, U - 4)
                for u in range(U - 3, U):
                    turn(b, par, u)
                    value_products(b, par, u)

            def tail(b, par, k, before):
                if k:
                    return
                wait_side_free(pe, before)
                if multi_query and not later(b):
                    pe.wait_ge(wo_loaded, 16)
                pe.wait_ge(mixed_ready, U * (b + 1))
                for q in range(QT):
                    for c in range(C):
                        last = pe.matmul(side[:, D * q:D * (q + 1)], mixedT[:, par, q, c, :], wo[:, c, :],
                                         start=(c == 0), stop=(multi_query and c == C - 1))
                    if not multi_query:
                        last = pe.matmul(side[:, D * q:D * (q + 1)], sh.ones[0:1, :], bias_rows[:, 1, :], start=False, stop=True)
                last.then_inc(tail_filled, 1)

            run(pe, front, unit, finish, tail)

        @block.scalar
        def _(act):
            if not multi_query:
                act.wait_ge(padded, 2)
                act.wait_ge(w_turned, 1)
                act.activation(wT[:, 0:2, :].rearrange("p j (d h) -> p j d h", h=H),
                               side[:, 0:2 * P].rearrange("p (j h d) -> p j d h", j=2, h=H), ACT.Copy)
                act.activation(wT[:, 2, :], side[:, 2 * P:3 * P], ACT.Copy).then_inc(w_copied, 1)
                act.wait_ge(w_turned, 2)
                act.activation(wo[:, :, :], out_sums[:, :].rearrange("p (c d) -> p c d", c=C), ACT.Copy).then_inc(w_copied, 1)
                act.activation(bias_q[:, :], bias_cols[:, 0:1], ACT.Copy, scale=float(DH) ** -0.5).then_inc(bias_scaled, 1)
                act.wait_ge(bias_scaled, 1)

            def front(b, par, first, k, before):
                if k not in FILLS:
                    return
                fill = FILLS.index(k)
                act.wait_ge(front_filled, FC * b + fill + 1)
                if multi_query:
                    if fill < 4:
                        last = act.activation(qT[:, par, 2 * fill:2 * fill + 2, :], side[:, :].rearrange("p (c s) -> p c s", c=2),
                                              ACT.Copy, scale=float(DH) ** -0.5)
                    else:
                        act.activation(kT[:, par, :], side[:, 0:S], ACT.Copy)
                        last = act.activation(values[:, par, :, 0, :], side[:, S:S + QT * DH].rearrange("p (t d) -> p t d", t=QT), ACT.Copy)
                elif fill == 0:
                    last = act.activation(xnT[:, :], side[:, 0:S], ACT.Copy)
                elif fill == 1:
                    if not first:
                        act.wait_ge(stacks.split, 4 * b)
                    act.activation(stacks.exact[:, 0, :], side[:, 0:S], ACT.Identity, scale=float(DH) ** -0.5, bias=bias_q[:, :])
                    last = act.activation(stacks.exact[:, 1, :], side[:, S:2 * S], ACT.Identity, bias=bias_cols[:, 1:2])
                else:
                    last = act.activation(values[:, par, :, :, 0:DH],
                                          side[:, 0:QT * D].rearrange("p (t h d) -> p t h d", t=QT, h=H), ACT.Copy)
                last.then_inc(front_copied, 1)

            def copy_turned(b, par, u):
                act.wait_ge(turned_done, U * b + u + 1)
                if not (isinstance(b, int) and b == 0 and u < 2):
                    act.wait_ge(summed, U * b + u - 1)
                act.activation(probsT[:, u % 2, :, :, :], turned[:, :, :, :], ACT.Copy).then_inc(turned_copied, 1)

            def unit(b, par, u, first):
                behind(copy_turned, b, par, u, 3, first)
                act.wait_ge(max_ready, U * b + u + 1)
                if not (first and u < 4):
                    act.wait_ge(turned_done, U * b + u - 3)
                for j in range(G):
                    last = act.activation(probs[:, u % 4, j, :], masked[:, u % 2, j, :], ACT.Exp,
                                          scale=-1.0, bias=minus_max[:, u % 2, j:j + 1], accum_out=sums[:, u % 4, j:j + 1])
                last.then_inc(exp_done, 1)

            def finish(b, par):
                for u in range(U - 3, U):
                    copy_turned(b, par, u)

            run(act, front, unit, finish, nothing)

        @block.vector
        def _(dve):
            def front(b, par, first, k, before):
                if multi_query:
                    return
                rows = [sh.x_all[:, bass.ds(b * QT + q, 1), :].rearrange("p o d -> p (o d)") for q in range(QT)]
                out = [xn[:, q, :] for q in range(QT)]
                if k == 0:
                    dve_moments(dve, rows, stats, moments, stats_done, moments_done, LN_EPS, b)
                elif k == 1:
                    if not first:
                        dve.wait_ge(front_filled, FC * b - 2)
                    dve_normalise(dve, rows, out, moments, rstd_done, normed, b)
                    if later(b, 2):
                        dve.wait_ge(max_ready, U * (b - 1))
                    for q in range(QT):
                        dve.tensor_scalar(mask[:, par, q, :], sh.key_index[:, :], sh.last_patch[:, bass.ds(b * QT + q, 1)],
                                          MASKED, ALU.is_gt, ALU.mult).then_inc(mask_ready, 8)
                elif k == 5:
                    dve.wait_ge(front_copied, FC * b + 2)
                    if not first:
                        dve.wait_ge(stacks.stored, 16 * b)
                    stacks.split_parts(dve, b)

            def invert(b, par, u):
                dve.wait_ge(exp_done, U * b + u + 1)
                dve.reciprocal(inverse[:, u % 4, :], sums[:, u % 4, :]).then_inc(inverted, 1)

            def copy_out(b, par, u):
                dve.wait_ge(summed, U * b + u + 1)
                g = u % 4
                dve.tensor_copy(mixedT[:, par, u // 4, CU * g:CU * (g + 1), :], out_view[:, :, :]).then_inc(mixed_ready, 1)

            def unit(b, par, u, first):
                if u == 0:
                    dve.wait_ge(mask_ready, 16 * (b + 1))
                dve.wait_ge(scored, U * b + u + 1)
                if not (first and u < 2):
                    dve.wait_ge(exp_done, U * b + u - 1)
                dve.sem_inc(unit_begun, 1)
                for j in range(G):
                    last = dve.tensor_tensor_reduce(out=masked[:, u % 2, j, :], in0=scores[u % 2][:, j, :], in1=mask[:, par, u // 4, :],
                                                    scale=-1.0, scalar=LARGEST, op0=ALU.add, op1=ALU.min,
                                                    accum_out=minus_max[:, u % 2, j:j + 1])
                last.then_inc(max_ready, 1)
                behind(invert, b, par, u, 1, first)
                behind(copy_out, b, par, u, 4, first)

            def finish(b, par):
                invert(b, par, U - 1)
                for u in range(U - 4, U):
                    copy_out(b, par, u)

            def tail(b, par, k, before):
                if k == 0:
                    return
                dve.wait_ge(tail_filled, b + 1)
                rows = sh.x_all[:, bass.ds(b * QT, QT), :]
                if multi_query:
                    dve.tensor_tensor(rows, rows, sh.y_all[:, bass.ds(b * QT, QT), :], ALU.add).then_inc(added, 1)
                    dve.wait_ge(added, b + 1)
                dve.tensor_tensor(rows, rows, side[:, 0:QT * D].rearrange("p (q d) -> p q d", q=QT), ALU.add).then_inc(tail_copied, 1)

            run(dve, front, unit, finish, tail)
        ph.retire(sh)


def phase_expert_ffn(nc, sh):
    E, F, T = 8, 352, 32
    CH = [(0, P), (P, P), (2 * P, F - 2 * P)]
    HALF = 4
    with ExitStack() as ctx:
        ph = Phase(nc, ctx, "l1f")
        w_gate = ph.sbuf("w_gate", [P, E, F])
        w_up = ph.sbuf("w_up", [P, E, F])
        w_down = ph.sbuf("w_down", [P, E, 3, D])
        stats = ph.sbuf("stats", [P, NT, 6])
        moments = ph.sbuf("moments", [P, NT, 4])
        xn = ph.sbuf("xn", [P, NT, D])
        x_expert = ph.sbuf("x_expert", [P, E, NB, T])
        silu = ph.sbuf("silu", [P, 2, F])
        hidden = ph.sbuf("hidden", [P, 2, F])
        hiddenT = ph.sbuf("hiddenT", [P, 2, 3, P])
        gate = ph.psum("gate", [P, 2, 512])
        up = ph.psum("up", [P, 2, 512])
        turned = ph.psum("turned", [P, 512])
        xT = [ph.psum("xT", [P, 512]), turned]
        down = ph.psum("down", [P, 2, 512])
        (w_loaded, stats_done, moments_done, rstd_done, normed, xT_done, xT_copied, up_done, silu_done,
         hidden_done, turned_done, turned_copied, down_done, added) = [ph.sem(n) for n in (
             "w_loaded", "stats_done", "moments_done", "rstd_done", "normed", "xT_done", "xT_copied", "up_done",
             "silu_done", "hidden_done", "turned_done", "turned_copied", "down_done", "added")]
        block = ctx.enter_context(nc.Block())

        @block.sync
        def _(sp):
            sp.dma_start(w_gate[:, :, :], sh.dram["L1_ffn_w1"].rearrange("e d f -> d e f")).then_inc(w_loaded, 16)
            sp.dma_start(w_up[:, :, :], sh.dram["L1_ffn_w3"].rearrange("e d f -> d e f")).then_inc(w_loaded, 16)
            w2 = sh.dram["L1_ffn_w2"]
            for c, (at, n) in enumerate(CH):
                sp.dma_start(w_down[0:n, :, c, :], w2[:, at:at + n, :].rearrange("e f d -> f e d")).then_inc(w_loaded, 16)

        @block.gpsimd
        def _(pool):
            clear_retired(pool, sh)
            pool_rstd_all(pool, sh, moments, moments_done, rstd_done)

        units = [(e, half) for e in range(E) for half in range(2)]

        @block.tensor
        def _(pe):
            for b in range(NB):
                pe.wait_ge(normed, QT * (b + 1))
                if b >= 2:
                    pe.wait_ge(xT_copied, b - 1)
                for q in range(QT):
                    last = pe.transpose(xT[b % 2][:, P * q:P * (q + 1)], xn[:, QT * b + q, :], sh.ident[:, :])
                last.then_inc(xT_done, 1)
            pe.wait_ge(xT_copied, NB)
            pe.wait_ge(w_loaded, 80)

            def turn(u):
                pe.wait_ge(hidden_done, u + 1)
                if u >= 1:
                    pe.wait_ge(turned_copied, u)
                for c, (at, n) in enumerate(CH):
                    last = pe.transpose(turned[0:n, P * c:P * (c + 1)], hidden[:, u % 2, at:at + n], sh.ident[:, :])
                last.then_inc(turned_done, 1)

            def down_products(u):
                e, half = units[u]
                pe.wait_ge(turned_copied, u + 1)
                if u >= 2:
                    pe.wait_ge(added, 4 * (u - 1))
                for c, (at, n) in enumerate(CH):
                    last = pe.matmul(down[:, u % 2, 0:D], hiddenT[0:n, u % 2, c, :], w_down[0:n, e, c, :],
                                     start=(c == 0), stop=(c == 2))
                last.then_inc(down_done, 1)

            for u, (e, half) in enumerate(units):
                rows = x_expert[:, e, HALF * half:HALF * (half + 1), :].rearrange("p b t -> p (b t)")
                if u >= 2:
                    pe.wait_ge(hidden_done, u - 1)
                pe.matmul(gate[:, u % 2, 0:F], rows, w_gate[:, e, :], start=True, stop=True)
                pe.matmul(up[:, u % 2, 0:F], rows, w_up[:, e, :], start=True, stop=True).then_inc(up_done, 1)
                if u >= 1:
                    turn(u - 1)
                if u >= 2:
                    down_products(u - 2)
            turn(len(units) - 1)
            down_products(len(units) - 2)
            down_products(len(units) - 1)

        @block.scalar
        def _(act):
            for b in range(NB):
                act.wait_ge(xT_done, b + 1)
                act.activation(x_expert[:, :, b, :], xT[b % 2][:, 0:S].rearrange("p (e t) -> p e t", e=E), ACT.Copy).then_inc(xT_copied, 1)

            def copy_turned(u):
                act.wait_ge(turned_done, u + 1)
                if u >= 2:
                    act.wait_ge(down_done, u - 1)
                for c, (at, n) in enumerate(CH):
                    last = act.activation(hiddenT[0:n, u % 2, c, :], turned[0:n, P * c:P * (c + 1)], ACT.Copy)
                last.then_inc(turned_copied, 1)

            for u in range(len(units)):
                act.wait_ge(up_done, u + 1)
                if u >= 2:
                    act.wait_ge(hidden_done, u - 1)
                act.activation(silu[:, u % 2, :], gate[:, u % 2, 0:F], ACT.Silu).then_inc(silu_done, 1)
                if u:
                    copy_turned(u - 1)
            copy_turned(len(units) - 1)

        @block.vector
        def _(dve):
            dve_layernorm_all(dve, sh, xn, stats, moments, stats_done, moments_done, rstd_done, normed)

            def add_down(u):
                e, half = units[u]
                dve.wait_ge(down_done, u + 1)
                at = T * (e % 4)
                for j in range(HALF):
                    b = HALF * half + j
                    rows = sh.x_all[at:at + T, QT * b + e // 4, :]
                    dve.tensor_tensor(rows, rows, down[T * j:T * (j + 1), u % 2, 0:D], ALU.add).then_inc(added, 1)

            for u in range(len(units)):
                dve.wait_ge(silu_done, u + 1)
                if u >= 2:
                    dve.wait_ge(turned_done, u - 1)
                dve.tensor_tensor(hidden[:, u % 2, :], silu[:, u % 2, :], up[:, u % 2, 0:F], ALU.mult).then_inc(hidden_done, 1)
                if u >= 2:
                    add_down(u - 2)
            add_down(len(units) - 2)
            add_down(len(units) - 1)
        ph.retire(sh)


def phase_multi_query_inputs(nc, sh):
    F = 512
    C = F // P
    with ExitStack() as ctx:
        ph = Phase(nc, ctx, "l2f")
        ctx_rows = ph.sbuf("ctx_rows", [P, NT, D])
        w1 = ph.sbuf("w1", [P, 2 * F])
        w2 = ph.sbuf("w2", [P, C, D])
        affine = ph.sbuf("affine", [P, 4, D])
        stats = [ph.sbuf(f"stats{i}", [P, QT, 6]) for i in range(3)]
        moments = [ph.sbuf(f"moments{i}", [P, QT, 4]) for i in range(3)]
        x_mid = ph.sbuf("x_mid", [P, QT, D])
        normed_rows = ph.sbuf("normed_rows", [P, 2, QT, D])
        scaled_rows = ph.sbuf("scaled_rows", [P, 2, QT, D])
        affine_rows = ph.sbuf("affine_rows", [P, 2, QT, D])
        rowsT = ph.sbuf("rowsT", [P, S])
        silu = ph.sbuf("silu", [P, QT, F])
        hidden = ph.sbuf("hidden", [P, QT, F])
        hiddenT = ph.sbuf("hiddenT", [P, QT, C, P])
        turned_rows = ph.psum("turned_rows", [P, 2, S])
        up = ph.psum("up", [P, QT, 2, F])
        turned = ph.psum("turned", [P, QT, C, P])
        down = ph.psum("down", [P, 512])
        stats_done = [ph.sem(f"stats_done{i}") for i in range(3)]
        moments_done = [ph.sem(f"moments_done{i}") for i in range(3)]
        rstd_done = [ph.sem(f"rstd_done{i}") for i in range(3)]
        normed = [ph.sem(f"normed{i}") for i in range(3)]
        (rows_loaded, w_loaded, scaled, affine_done, rows_turned, rows_copied, up_done, silu_done, hidden_done, hidden_turned,
         hidden_copied, down_done, y_done) = [ph.sem(n) for n in (
             "rows_loaded", "w_loaded", "scaled", "affine_done", "rows_turned", "rows_copied", "up_done", "silu_done",
             "hidden_done", "hidden_turned", "hidden_copied", "down_done", "y_done")]
        block = ctx.enter_context(nc.Block())

        @block.sync
        def _(sp):
            sp.dma_start(ctx_rows[:, :, :], sh.dram["ctx_1024"].rearrange("b (q p) d -> p (b q) d", p=P)).then_inc(rows_loaded, 16)
            for j, n in enumerate(("ln_g", "ln_b", "cln_g", "cln_b")):
                sp.dma_start(affine[:, j, :], sh.dram["L2_xattn_" + n].rearrange("(o d) -> o d", o=1).to_broadcast([P, D])).then_inc(rows_loaded, 16)
            sp.dma_start(w1[:, :], sh.dram["L2_xattn_W1"]).then_inc(w_loaded, 16)
            sp.dma_start(w2[:, :, :], sh.dram["L2_xattn_W2"].rearrange("(c p) d -> p c d", p=P)).then_inc(w_loaded, 16)

        ORDER = "F0 B0 F1 B1 F2 B2 F3"

        @block.gpsimd
        def _(pool):
            clear_retired(pool, sh)

            def front(b, par, k):
                for i in {0: (0, 2), 1: (1,)}.get(k, ()):
                    pool_rstd(pool, sh, moments[i], moments_done[i], rstd_done[i], b)

            overlapped(pool, ORDER, front, nothing)

        @block.tensor
        def _(pe):

            def front(b, par, k):
                if k < 3:
                    return
                pe.wait_ge(affine_done, b + 1)
                if later(b):
                    pe.wait_ge(rows_copied, b)
                for j in range(2):
                    for q in range(QT):
                        last = pe.transpose(turned_rows[:, j, P * q:P * (q + 1)], affine_rows[:, j, q, :], sh.ident[:, :])
                last.then_inc(rows_turned, 1)

            def back(b, par, k):
                if k == 0:
                    if not later(b):
                        pe.wait_ge(w_loaded, 32)
                    pe.wait_ge(rows_copied, b + 1)
                    for q in range(QT):
                        if later(b):
                            pe.wait_ge(hidden_done, QT * (b - 1) + q + 1)
                        for j in range(2):
                            last = pe.matmul(up[:, q, j, :], rowsT[:, P * q:P * (q + 1)], w1[:, F * j:F * (j + 1)], start=True, stop=True)
                        last.then_inc(up_done, 1)
                elif k == 1:
                    for q in range(QT):
                        pe.wait_ge(hidden_done, QT * b + q + 1)
                        for c in range(C):
                            last = pe.transpose(turned[:, q, c, :], hidden[:, q, P * c:P * (c + 1)], sh.ident[:, :])
                        last.then_inc(hidden_turned, 1)
                else:
                    if later(b):
                        pe.wait_ge(y_done, b)
                    for q in range(QT):
                        pe.wait_ge(hidden_copied, QT * b + q + 1)
                        for c in range(C):
                            last = pe.matmul(down[:, D * q:D * (q + 1)], hiddenT[:, q, c, :], w2[:, c, :], start=(c == 0), stop=(c == C - 1))
                    last.then_inc(down_done, 1)

            overlapped(pe, ORDER, front, back)

        @block.scalar
        def _(act):
            def front(b, par, k):
                if k < 3:
                    return
                act.wait_ge(rows_turned, b + 1)
                act.activation(rowsT[:, :], turned_rows[:, 0, :], ACT.Copy)
                act.activation(sh.xnT_all[:, bass.ds(b * S, S)], turned_rows[:, 0, :], ACT.Copy)
                act.activation(sh.cnT_all[:, bass.ds(b * S, S)], turned_rows[:, 1, :], ACT.Copy).then_inc(rows_copied, 1)

            def back(b, par, k):
                if k == 0:
                    for q in range(QT):
                        act.wait_ge(up_done, QT * b + q + 1)
                        act.activation(silu[:, q, :], up[:, q, 1, :], ACT.Silu).then_inc(silu_done, 1)
                elif k == 1:
                    for q in range(QT):
                        act.wait_ge(hidden_turned, QT * b + q + 1)
                        act.activation(hiddenT[:, q, :, :], turned[:, q, :, :], ACT.Copy).then_inc(hidden_copied, 1)

            overlapped(act, ORDER, front, back)

        @block.vector
        def _(dve):
            dve.wait_ge(rows_loaded, 80)

            def front(b, par, k):
                x_rows = [sh.x_all[:, bass.ds(b * QT + q, 1), :].rearrange("p o d -> p (o d)") for q in range(QT)]
                c_rows = [ctx_rows[:, bass.ds(b * QT + q, 1), :].rearrange("p o d -> p (o d)") for q in range(QT)]
                mid = [x_mid[:, q, :] for q in range(QT)]
                if k == 0:
                    dve_moments(dve, x_rows, stats[0], moments[0], stats_done[0], moments_done[0], LN_EPS, b)
                    dve_moments(dve, c_rows, stats[2], moments[2], stats_done[2], moments_done[2], LN_EPS, b)
                elif k == 1:
                    if later(b):
                        dve.wait_ge(scaled, 2 * b)
                    dve_normalise(dve, x_rows, mid, moments[0], rstd_done[0], normed[0], b)
                    dve_normalise(dve, c_rows, [normed_rows[:, 1, q, :] for q in range(QT)], moments[2], rstd_done[2], normed[2], b)
                    dve.wait_ge(normed[0], QT * (b + 1))
                    dve_moments(dve, mid, stats[1], moments[1], stats_done[1], moments_done[1], LN_EPS, b)
                elif k == 2:
                    dve_normalise(dve, mid, [normed_rows[:, 0, q, :] for q in range(QT)], moments[1], rstd_done[1], normed[1], b)
                    dve.wait_ge(normed[1], QT * (b + 1))
                    dve.wait_ge(normed[2], QT * (b + 1))
                    if later(b):
                        dve.wait_ge(affine_done, b)
                    for j in range(2):
                        dve.tensor_tensor(scaled_rows[:, j, :, :], normed_rows[:, j, :, :],
                                          affine[:, 2 * j, :].unsqueeze(1).to_broadcast([P, QT, D]), ALU.mult).then_inc(scaled, 1)
                    dve.wait_ge(scaled, 2 * (b + 1))
                    if later(b):
                        dve.wait_ge(rows_turned, b)
                    for j in range(2):
                        last = dve.tensor_tensor(affine_rows[:, j, :, :], scaled_rows[:, j, :, :],
                                                 affine[:, 2 * j + 1, :].unsqueeze(1).to_broadcast([P, QT, D]), ALU.add)
                    last.then_inc(affine_done, 1)

            def back(b, par, k):
                if k == 0:
                    for q in range(QT):
                        dve.wait_ge(silu_done, QT * b + q + 1)
                        dve.tensor_tensor(hidden[:, q, :], silu[:, q, :], up[:, q, 0, :], ALU.mult).then_inc(hidden_done, 1)
                elif k == 2:
                    dve.wait_ge(down_done, b + 1)
                    dve.tensor_copy(sh.y_all[:, bass.ds(b * QT, QT), :], down[:, 0:QT * D].rearrange("p (q d) -> p q d", q=QT)).then_inc(y_done, 1)

            overlapped(dve, ORDER, front, back)
        ph.retire(sh)


def phase_routed_ffn(nc, sh):
    E, F = 8, 512
    C = F // P
    STEPS = 11
    with ExitStack() as ctx:
        ph = Phase(nc, ctx, "l2r")
        cent_rows = ph.sbuf("cent_rows", [E, D])
        centT = ph.sbuf("centT", [P, E])
        affine = ph.sbuf("affine", [E, 2, D])
        w1 = ph.sbuf("w1", [P, E, F])
        w2 = ph.sbuf("w2", [P, C, E, D])
        bias1 = ph.sbuf("bias1", [E, F])
        bias2 = ph.sbuf("bias2", [E, D])
        stats = [ph.sbuf(f"stats{i}", [P, QT, 6]) for i in range(2)]
        moments = [ph.sbuf(f"moments{i}", [P, QT, 4]) for i in range(2)]
        x_in = ph.sbuf("x_in", [P, 2, QT, D])
        x_inT = ph.sbuf("x_inT", [P, QT, P])
        xn = ph.sbuf("xn", [P, QT, D])
        logits = ph.sbuf("logits", [P, QT, E])
        top = ph.sbuf("top", [P, QT])
        first = ph.sbuf("first", [P, QT])
        onehot = ph.sbuf("onehot", [P, 2, QT, E])
        onehotT = ph.sbuf("onehotT", [E, 2, QT, P])
        alpha = ph.sbuf("alpha", [P, 2, QT, 3])
        expert_rows = ph.sbuf("expert_rows", [P, QT, E, D])
        expert_rowsT = ph.sbuf("expert_rowsT", [P, 2, QT, E, P])
        relu = ph.sbuf("relu", [P, QT, F])
        reluT = ph.sbuf("reluT", [P, QT, C, P])
        bias_rows = ph.sbuf("bias_rows", [P, 2, QT, D])
        y = ph.sbuf("y", [P, 2, QT, D])
        small = ph.psum("small", [P, 512])
        gathered = ph.psum("gathered", [P, QT, 2, D])
        turned = ph.psum("turned", [P, QT, 4, P])
        up = ph.psum("up", [P, 512])
        down = ph.psum("down", [P, E, D])
        bias_out = ph.psum("bias_out", [P, 512])
        stats_done = [ph.sem(f"stats_done{i}") for i in range(2)]
        moments_done = [ph.sem(f"moments_done{i}") for i in range(2)]
        rstd_done = [ph.sem(f"rstd_done{i}") for i in range(2)]
        normed = [ph.sem(f"normed{i}") for i in range(2)]
        (choice_loaded, w1_loaded, w2_loaded, cent_turned, cent_copied, step, x_turned, x_copied, logits_done, logits_copied, chosen,
         choice_turned, choice_copied, gather_done, exp_done, rows_ready, rows_turned, rows_copied, up_done,
         relu_done, relu_turned, relu_copied, down_done, selected, selected_step, y_done) = [ph.sem(n) for n in (
             "choice_loaded", "w1_loaded", "w2_loaded", "cent_turned", "cent_copied", "step", "x_turned", "x_copied", "logits_done",
             "logits_copied", "chosen", "choice_turned", "choice_copied", "gather_done", "exp_done",
             "rows_ready", "rows_turned", "rows_copied", "up_done", "relu_done", "relu_turned", "relu_copied",
             "down_done", "selected", "selected_step", "y_done")]
        block = ctx.enter_context(nc.Block())

        @block.sync
        def _(sp):
            sp.dma_start(cent_rows[:, :], sh.dram["L2_ffn_centroids"]).then_inc(choice_loaded, 16)
            sp.dma_start(affine[:, 0, :], sh.dram["L2_ffn_ln_g"]).then_inc(choice_loaded, 16)
            sp.dma_start(affine[:, 1, :], sh.dram["L2_ffn_ln_b"]).then_inc(choice_loaded, 16)
            sp.dma_start(bias2[:, :], sh.dram["L2_ffn_b2"]).then_inc(choice_loaded, 16)
            sp.dma_start(bias1[:, :], sh.dram["L2_ffn_b1"]).then_inc(w1_loaded, 16)
            sp.dma_start(w1[:, :, :], sh.dram["L2_ffn_w1"].rearrange("e d f -> d e f")).then_inc(w1_loaded, 16)
            for c in range(C):
                sp.dma_start(w2[:, c, :, :], sh.dram["L2_ffn_w2"][:, P * c:P * (c + 1), :].rearrange("e f d -> f e d")).then_inc(w2_loaded, 16)

        ORDER = "F0 B0 F1 B1 F2 B2 F3 B3 F4 B4 B5 F5 B6 F6"

        @block.gpsimd
        def _(pool):
            clear_retired(pool, sh)
            with pool.Fori(0, NB) as b:
                for i in range(2):
                    pool_rstd(pool, sh, moments[i], moments_done[i], rstd_done[i], b)

        @block.tensor
        def _(pe):
            pe.wait_ge(choice_loaded, 64)
            pe.transpose(small[:, 0:E], cent_rows[:, :], sh.ident[0:E, 0:E]).then_inc(cent_turned, 1)
            pe.wait_ge(cent_copied, 1)

            def front(b, par, k):
                if k == 1:
                    pe.wait_ge(normed[0], QT * (b + 1))
                    for q in range(QT):
                        last = pe.transpose(small[:, P * q:P * (q + 1)], x_in[:, par, q, :], sh.ident[:, :])
                    last.then_inc(x_turned, 1)
                elif k == 2:
                    pe.wait_ge(x_copied, b + 1)
                    for q in range(QT):
                        last = pe.matmul(small[:, 2 * P + E * q:2 * P + E * (q + 1)], x_inT[:, q, :], centT[:, :], start=True, stop=True)
                    last.then_inc(logits_done, 1)
                elif k == 3:
                    pe.wait_ge(logits_copied, b + 1)
                    pe.wait_ge(chosen, b + 1)
                    for q in range(QT):
                        last = pe.transpose(small[0:E, P * q:P * (q + 1)], onehot[:, par, q, :], sh.ident[:, :])
                    last.then_inc(choice_turned, 1)
                elif k == 4:
                    pe.wait_ge(choice_copied, b + 1)
                    for q in range(QT):
                        pe.matmul(gathered[:, q, :, :], onehotT[:, par, q, :], affine[:, :, :], start=True, stop=True)
                        last = pe.matmul(bias_out[:, D * q:D * (q + 1)], onehotT[:, par, q, :], bias2[:, :], start=True, stop=True)
                    last.then_inc(gather_done, 1)
                elif k >= 5:
                    q = k - 5
                    pe.wait_ge(rows_ready, QT * b + q + 1)
                    for g in range(2):
                        if g or q or later(b):
                            pe.wait_ge(rows_copied, 2 * QT * b + 2 * q + g)
                        if (q, g) == (0, 0) and later(b):
                            pe.wait_ge(relu_copied, QT * b)
                        for j in range(4):
                            last = pe.transpose(turned[:, g, j, :], expert_rows[:, q, 4 * g + j, :], sh.ident[:, :])
                        last.then_inc(rows_turned, 1)

            def back(b, par, k):
                q, part = (k // 3, k % 3) if k < 6 else (1, 2)
                if part == 0:
                    if not later(b):
                        pe.wait_ge(w1_loaded, 32)
                    pe.wait_ge(rows_copied, 2 * QT * (b + 1))
                    if q or later(b):
                        pe.wait_ge(relu_done, QT * b + q)
                    for e in range(E):
                        pe.matmul(up[:, :], expert_rowsT[:, par, q, e, :], w1[:, e, :], start=(e == 0), stop=False)
                    pe.matmul(up[:, :], onehotT[:, par, q, :], bias1[:, :], start=False, stop=True).then_inc(up_done, 1)
                elif part == 1:
                    pe.wait_ge(relu_done, QT * b + q + 1)
                    for c in range(C):
                        last = pe.transpose(turned[:, 0, c, :], relu[:, q, P * c:P * (c + 1)], sh.ident[:, :])
                    last.then_inc(relu_turned, 1)
                else:
                    if not later(b):
                        pe.wait_ge(w2_loaded, 16 * C)
                    pe.wait_ge(relu_copied, QT * b + q + 1)
                    if q or later(b):
                        pe.wait_ge(selected, QT * b + q)
                    for g in {2: (0, 1), 5: (0,), 6: (1,)}[k]:
                        for c in range(C):
                            last = pe.matmul(down[:, 4 * g:4 * g + 4, :], reluT[:, q, c, :], w2[:, c, 4 * g:4 * g + 4, :],
                                             start=(c == 0), stop=(c == C - 1))
                    if k != 5:
                        last.then_inc(down_done, 1)

            overlapped(pe, ORDER, front, back)

        @block.scalar
        def _(act):
            act.wait_ge(cent_turned, 1)
            act.activation(centT[:, :], small[:, 0:E], ACT.Copy).then_inc(cent_copied, 1)

            def front(b, par, k):
                if k == 1:
                    act.wait_ge(x_turned, b + 1)
                    act.activation(x_inT[:, :, :], small[:, 0:S].rearrange("p (q t) -> p q t", q=QT), ACT.Copy).then_inc(x_copied, 1)
                elif k == 2:
                    act.wait_ge(logits_done, b + 1)
                    act.activation(logits[:, :, :], small[:, 2 * P:2 * P + QT * E].rearrange("p (q e) -> p q e", q=QT), ACT.Copy).then_inc(logits_copied, 1)
                elif k == 3:
                    act.wait_ge(choice_turned, b + 1)
                    act.activation(onehotT[:, par, :, :], small[0:E, 0:S].rearrange("p (q t) -> p q t", q=QT), ACT.Copy).then_inc(choice_copied, 1)
                    act.activation(alpha[:, par, :, 0], top[:, :], ACT.Exp, scale=-1.0).then_inc(exp_done, 1)
                elif k >= 5:
                    q = k - 5
                    for g in range(2):
                        act.wait_ge(rows_turned, 2 * QT * b + 2 * q + g + 1)
                        act.activation(expert_rowsT[:, par, q, 4 * g:4 * g + 4, :], turned[:, g, :, :], ACT.Copy).then_inc(rows_copied, 1)

            def back(b, par, k):
                q, part = (k // 3, k % 3) if k < 6 else (1, 2)
                if part == 0:
                    act.wait_ge(up_done, QT * b + q + 1)
                    act.activation(relu[:, q, :], up[:, :], ACT.Relu).then_inc(relu_done, 1)
                elif part == 1:
                    act.wait_ge(relu_turned, QT * b + q + 1)
                    act.activation(reluT[:, q, :, :], turned[:, 0, :, :], ACT.Copy).then_inc(relu_copied, 1)

            overlapped(act, ORDER, front, back)

        @block.vector
        def _(dve):
            n = None

            def front(b, par, k):
                nonlocal n
                inner = [x_in[:, par, q, :] for q in range(QT)]
                if k == 0:
                    rows = [sh.x_all[:, bass.ds(b * QT + q, 1), :].rearrange("p o d -> p (o d)") for q in range(QT)]
                    dve_layernorm(dve, rows, inner, stats[0], moments[0], stats_done[0], moments_done[0], rstd_done[0], normed[0], LN_EPS, b)
                elif k == 1:
                    dve.wait_ge(normed[0], QT * (b + 1))
                    if later(b):
                        dve.wait_ge(rows_ready, QT * b)
                    dve_layernorm(dve, inner, [xn[:, q, :] for q in range(QT)], stats[1], moments[1], stats_done[1],
                                  moments_done[1], rstd_done[1], normed[1], LN_EPS, b)
                elif k == 2:
                    n = Counter(STEPS)
                    dve.wait_ge(logits_copied, b + 1)
                    if later(b):
                        dve.wait_ge(exp_done, b)
                    dve_choose(dve, sh, logits[:, :, :], top, first, onehot[:, par, :, :], step, n, b)
                    dve.sem_inc(chosen, 1)
                elif k == 3:
                    dve.wait_ge(exp_done, b + 1)
                    dve.tensor_scalar(alpha[:, par, :, 1], alpha[:, par, :, 0], 1.0, None, ALU.add).then_inc(step, n.up())
                    dve.wait_ge(step, n.all(b))
                    dve.reciprocal(alpha[:, par, :, 2], alpha[:, par, :, 1]).then_inc(step, n.up())
                elif k == 4:
                    dve.wait_ge(gather_done, b + 1)
                    dve.wait_ge(normed[1], QT * (b + 1))
                    dve.tensor_copy(bias_rows[:, par, :, :], bias_out[:, 0:QT * D].rearrange("p (q d) -> p q d", q=QT)).then_inc(step, n.up())
                    dve.tensor_tensor(xn[:, :, :], xn[:, :, :], gathered[:, :, 0, :], ALU.mult).then_inc(step, n.up())
                    dve.wait_ge(step, n.all(b))
                    dve.tensor_tensor(xn[:, :, :], xn[:, :, :], gathered[:, :, 1, :], ALU.add).then_inc(step, n.up())
                    dve.wait_ge(step, n.all(b))
                    n.close()
                    for q in range(QT):
                        if later(b):
                            dve.wait_ge(rows_turned, 2 * QT * (b - 1) + 2 * q + 2)
                        for e in range(E):
                            last = dve.tensor_scalar(expert_rows[:, q, e, :], xn[:, q, :], onehot[:, par, q, e:e + 1], None, ALU.mult)
                        last.then_inc(rows_ready, 1)

            def back(b, par, k):
                if k not in (2, 6):
                    return
                q = 0 if k == 2 else 1
                dve.wait_ge(down_done, QT * b + q + 1)
                for e in range(E):
                    so_far = bias_rows[:, par, q, :] if e == 0 else y[:, par, q, :]
                    dve.scalar_tensor_tensor(out=y[:, par, q, :], in0=down[:, e, :], scalar=onehot[:, par, q, e:e + 1],
                                             in1=so_far, op0=ALU.mult, op1=ALU.add).then_inc(selected_step, 1)
                    dve.wait_ge(selected_step, E * (QT * b + q) + e + 1)
                dve.sem_inc(selected, 1)
                if q < QT - 1:
                    return
                for t in range(QT):
                    dve.scalar_tensor_tensor(out=y[:, par, t, :], in0=y[:, par, t, :], scalar=alpha[:, par, t, 2:3],
                                             in1=x_in[:, par, t, :], op0=ALU.mult, op1=ALU.add).then_inc(y_done, 1)
                dve.wait_ge(y_done, (QT + 1) * b + QT)
                out_rows = sh.x_all[:, bass.ds(b * QT, QT), :]
                dve.tensor_tensor(out_rows, out_rows, y[:, par, :, :], ALU.add).then_inc(y_done, 1)
                dve.wait_ge(y_done, (QT + 1) * (b + 1))

            overlapped(dve, ORDER, front, back)
        ph.retire(sh)


def phase_head_softmax_attention(nc, sh):
    H, DH, U = 8, 16, 4
    G = 4
    W = P // G
    C = H // G
    with ExitStack() as ctx:
        ph = Phase(nc, ctx, "l3a")
        w_rows = ph.sbuf("w_rows", [P, 4, D])
        wo_rows = ph.sbuf("wo_rows", [P, H, W])
        wT = ph.sbuf("wT", [P, 3, D])
        wo = ph.sbuf("wo", [P, C, D])
        stats = ph.sbuf("stats", [P, NT, 6])
        moments = ph.sbuf("moments", [P, NT, 4])
        xn = ph.sbuf("xn", [P, NT, D])
        ctx_now = ph.sbuf("ctx_now", [P, S])
        q_head = ph.sbuf("q_head", [P, 2, H, S])
        kT = ph.sbuf("kT", [P, 2, S])
        values = ph.sbuf("values", [P, 2, QT, H, W])
        largest = ph.sbuf("largest", [P, 2, P])
        lowered = ph.sbuf("lowered", [P, 2, H, P])
        probs = ph.sbuf("probs", [P, 4, H, P])
        total = ph.sbuf("total", [P, 2, P])
        inverse = ph.sbuf("inverse", [P, 2, P])
        pairs = ph.sbuf("pairs", [P, 2, H // 2, P])
        mixedT = ph.sbuf("mixedT", [P, 2, QT, C, P])
        scores = [ph.psum(f"scores{i}", [P, H, P]) for i in range(2)]
        out_sums = [ph.psum(f"out_sums{i}", [P, 512]) for i in range(QT)]
        front_bank = ph.psum("front_bank", [P, 512])
        tail_bank = ph.psum("tail_bank", [P, 512])
        names = ["w_loaded", "padded", "w_turned", "w_copied", "stats_done", "moments_done", "rstd_done",
                 "normed", "x_turned", "x_copied", "front_filled", "front_copied", "ctx_ready", "scored", "exp_done",
                 "max_ready", "lowered_ready", "paired", "totalled", "inverted", "shared", "summed", "out_copied", "tail_filled", "tail_copied"]
        (w_loaded, padded, w_turned, w_copied, stats_done, moments_done, rstd_done, normed, x_turned, x_copied, front_filled,
         front_copied, ctx_ready, scored, exp_done, max_ready, lowered_ready, paired, totalled, inverted, shared, summed, out_copied,
         tail_filled, tail_copied) = [ph.sem(n) for n in names]
        block = ctx.enter_context(nc.Block())

        def run(eng, front, unit, finish, tail):
            def one(b, par, first, more):
                for u in range(U):
                    unit(b, par, u, first)
                    if u < 3 and more:
                        front(b + 1, 1 - par, False, u)
                    if u == 0 and not (isinstance(b, int) and b < 2):
                        tail(b - 2, par)

            for step in range(3):
                front(0, 0, True, step)
            one(0, 0, True, True)
            one(1, 1, False, True)
            with eng.Fori(2, NB - 2, 2) as b:
                one(b, 0, False, True)
                one(b + 1, 1, False, True)
            one(NB - 2, 0, False, True)
            one(NB - 1, 1, False, False)
            finish(NB - 1, 1)
            tail(NB - 2, 0)
            tail(NB - 1, 1)

        def behind(work, b, par, u, lag, first):
            if u >= lag:
                work(b, par, u - lag)
            elif not first:
                work(b - 1, 1 - par, U + u - lag)

        def nothing(*args):
            pass

        @block.sync
        def _(sp):
            for j, n in enumerate(("W_Q", "W_K", "W_V", "W_O")):
                sp.dma_start(w_rows[:, j, :], sh.dram["L3_xattn_" + n]).then_inc(w_loaded, 16)

        @block.gpsimd
        def _(pool):
            clear_retired(pool, sh)
            pool.memset(values[:, :, :, :, :], 0.0).then_inc(padded, 1)
            pool.memset(wo_rows[:, :, :], 0.0).then_inc(padded, 1)
            pool_rstd_all(pool, sh, moments, moments_done, rstd_done)
            pool.wait_ge(padded, 2)
            pool.wait_ge(w_loaded, 64)
            pool.tensor_copy(wo_rows[:, :, 0:DH], w_rows[:, 3, :].rearrange("p (h d) -> p h d", h=H)).then_inc(padded, 1)

            def share(b, par, u):
                pool.wait_ge(inverted, U * b + u + 1)
                buf = probs[:, u, :, :]
                pool.tensor_tensor(buf, buf, inverse[:, u % 2, :].unsqueeze(1).to_broadcast([P, H, P]), ALU.mult).then_inc(shared, 1)

            def unit(b, par, u, first):
                pool.wait_ge(exp_done, U * b + u + 1)
                if not (first and u < 2):
                    pool.wait_ge(totalled, U * b + u - 1)
                pool.tensor_tensor(pairs[:, u % 2, :, :], probs[:, u, 0:H // 2, :], probs[:, u, H // 2:H, :], ALU.add).then_inc(paired, 1)
                behind(share, b, par, u, 1, first)

            run(pool, nothing, unit, lambda b, par: share(b, par, U - 1), nothing)

        @block.tensor
        def _(pe):
            pe.wait_ge(w_loaded, 64)
            for j in range(3):
                last = pe.transpose(front_bank[:, P * j:P * (j + 1)], w_rows[:, j, :], sh.ident[:, :])
            last.then_inc(w_turned, 1)
            for g in range(NT // 4):
                pe.wait_ge(normed, 4 * (g + 1))
                if g >= 2:
                    pe.wait_ge(x_copied, g - 1)
                for j in range(4):
                    last = pe.transpose(out_sums[g % 2][:, P * j:P * (j + 1)], xn[:, 4 * g + j, :], sh.ident[:, :])
                last.then_inc(x_turned, 1)
            pe.wait_ge(padded, 3)
            for c in range(C):
                last = pe.transpose(tail_bank[:, P * c:P * (c + 1)],
                                    wo_rows[:, G * c:G * (c + 1), :].rearrange("p g d -> p (g d)"), sh.ident[:, :])
            last.then_inc(w_turned, 1)
            pe.wait_ge(w_copied, 2)
            pe.wait_ge(x_copied, NT // 4)

            def front(b, par, first, step):
                if step == 1:
                    pe.wait_ge(ctx_ready, b + 1)
                    if not first:
                        pe.wait_ge(front_copied, 2 * b)
                    pe.matmul(front_bank[:, 0:S], wT[:, 0, :], sh.xnT_all[:, bass.ds(b * S, S)], start=True, stop=True)
                    pe.matmul(front_bank[:, S:2 * S], wT[:, 1, :], ctx_now[:, :], start=True, stop=True).then_inc(front_filled, 1)
                elif step == 2:
                    pe.wait_ge(front_copied, 2 * b + 1)
                    for t in range(QT):
                        last = pe.matmul(front_bank[:, D * t:D * (t + 1)], ctx_now[:, P * t:P * (t + 1)], wT[:, 2, :],
                                         start=True, stop=True)
                    last.then_inc(front_filled, 1)

            def value_products(b, par, u):
                q, t = u // 2, u % 2
                pe.wait_ge(shared, U * b + u + 1)
                if t == 0 and not (isinstance(b, int) and b == 0):
                    pe.wait_ge(out_copied, QT * (b - 1) + q + 1)
                for c in range(C):
                    for j in range(G):
                        last = pe.matmul(out_sums[q][W * j:W * (j + 1), P * c:P * (c + 1)], values[:, par, t, G * c + j, :],
                                         probs[:, u, G * c + j, :], start=(t == 0 and c == 0), stop=(t == QT - 1), skip_group_check=True)
                last.then_inc(summed, 1)

            def unit(b, par, u, first):
                q, t = u // 2, u % 2
                if u == 0:
                    pe.wait_ge(front_copied, 2 * (b + 1))
                if not (first and u < 2):
                    pe.wait_ge(lowered_ready, U * b + u - 1)
                for g in range(2):
                    last = pe.matmul(scores[u % 2][:, 4 * g:4 * g + 4, :], kT[:, par, P * t:P * (t + 1)],
                                     q_head[:, par, 4 * g:4 * g + 4, P * q:P * (q + 1)], start=True, stop=True)
                last.then_inc(scored, 1)
                behind(value_products, b, par, u, 3, first)

            def finish(b, par):
                value_products(b, par, U - 3)
                value_products(b, par, U - 2)
                value_products(b, par, U - 1)

            def tail(b, par):
                pe.wait_ge(out_copied, QT * (b + 1))
                if isinstance(b, int):
                    pe.wait_ge(tail_copied, b)
                for q in range(QT):
                    for c in range(C):
                        last = pe.matmul(tail_bank[:, D * q:D * (q + 1)], mixedT[:, par, q, c, :], wo[:, c, :],
                                         start=(c == 0), stop=(c == C - 1))
                last.then_inc(tail_filled, 1)

            run(pe, front, unit, finish, tail)

        @block.scalar
        def _(act):
            act.wait_ge(w_turned, 1)
            act.activation(wT[:, :, :], front_bank[:, 0:3 * P].rearrange("p (j d) -> p j d", j=3), ACT.Copy).then_inc(w_copied, 1)
            for g in range(NT // 4):
                act.wait_ge(x_turned, g + 1)
                act.activation(sh.xnT_all[:, 4 * P * g:4 * P * (g + 1)], out_sums[g % 2][:, :], ACT.Copy).then_inc(x_copied, 1)
            act.wait_ge(w_turned, 2)
            act.activation(wo[:, :, :], tail_bank[:, 0:C * P].rearrange("p (c d) -> p c d", c=C), ACT.Copy).then_inc(w_copied, 1)
            act.wait_ge(padded, 2)

            def front(b, par, first, step):
                if step == 0:
                    if not first:
                        act.wait_ge(front_filled, 2 * b)
                    act.activation(ctx_now[:, :], sh.ctxT[:, bass.ds(b * S, S)], ACT.Copy).then_inc(ctx_ready, 1)
                    return
                act.wait_ge(front_filled, 2 * b + step)
                if step == 1:
                    for h in range(H):
                        act.activation(q_head[:, par, h, :], front_bank[:, 0:S], ACT.Copy, scale=sh.head16[:, h:h + 1])
                    act.activation(kT[:, par, :], front_bank[:, S:2 * S], ACT.Copy, scale=float(DH) ** -0.5).then_inc(front_copied, 1)
                else:
                    act.activation(values[:, par, :, :, 0:DH],
                                   front_bank[:, 0:S].rearrange("p (t h d) -> p t h d", t=QT, h=H), ACT.Copy).then_inc(front_copied, 1)

            def copy_out(b, par, u):
                if u % 2 == 0:
                    return
                act.wait_ge(summed, U * b + u + 1)
                if not (isinstance(b, int) and b < 2):
                    act.wait_ge(tail_filled, b - 1)
                act.activation(mixedT[:, par, u // 2, :, :], out_sums[u // 2][:, 0:C * P].rearrange("p (c q) -> p c q", c=C),
                               ACT.Copy).then_inc(out_copied, 1)

            def unit(b, par, u, first):
                behind(copy_out, b, par, u, 4, first)
                act.wait_ge(lowered_ready, U * b + u + 1)
                if not first:
                    act.wait_ge(summed, U * b + u - 3)
                act.activation(probs[:, u, :, :], lowered[:, u % 2, :, :], ACT.Exp).then_inc(exp_done, 1)

            def finish(b, par):
                copy_out(b, par, 1)
                copy_out(b, par, 3)

            run(act, front, unit, finish, nothing)

        @block.vector
        def _(dve):
            dve_layernorm_all(dve, sh, xn, stats, moments, stats_done, moments_done, rstd_done, normed)

            def sum_heads(b, par, u):
                dve.wait_ge(paired, U * b + u + 1)
                dve.tensor_reduce(total[:, u % 2, :], pairs[:, u % 2, :, :].rearrange("p h q -> p q h"), AX.X, ALU.add).then_inc(totalled, 1)
                dve.wait_ge(totalled, U * b + u + 1)
                if not (isinstance(b, int) and b == 0 and u < 2):
                    dve.wait_ge(shared, U * b + u - 1)
                dve.reciprocal(inverse[:, u % 2, :], total[:, u % 2, :]).then_inc(inverted, 1)

            def unit(b, par, u, first):
                dve.wait_ge(scored, U * b + u + 1)
                dve.tensor_reduce(largest[:, u % 2, :], scores[u % 2][:, :, :].rearrange("p h q -> p q h"), AX.X, ALU.max).then_inc(max_ready, 1)
                dve.wait_ge(max_ready, U * b + u + 1)
                if not (first and u < 2):
                    dve.wait_ge(exp_done, U * b + u - 1)
                dve.tensor_tensor(lowered[:, u % 2, :, :], scores[u % 2][:, :, :],
                                  largest[:, u % 2, :].unsqueeze(1).to_broadcast([P, H, P]), ALU.subtract).then_inc(lowered_ready, 1)
                behind(sum_heads, b, par, u, 1, first)

            def tail(b, par):
                dve.wait_ge(tail_filled, b + 1)
                rows = sh.x_all[:, bass.ds(b * QT, QT), :]
                dve.tensor_tensor(rows, rows, tail_bank[:, 0:S].rearrange("p (q d) -> p q d", q=QT),
                                  ALU.add).then_inc(tail_copied, 1)

            run(dve, nothing, unit, lambda b, par: sum_heads(b, par, U - 1), tail)
        ph.retire(sh)


def phase_hard_expert_ffn(nc, sh):
    E, F = 4, 512
    C = F // P
    LN3_EPS = 1e-12
    with ExitStack() as ctx:
        ph = Phase(nc, ctx, "l3f")
        router = ph.sbuf("router", [P, E])
        w1 = ph.sbuf("w1", [P, E, F])
        wo = ph.sbuf("wo", [P, C, D])
        bias1 = ph.sbuf("bias1", [E, F])
        bias_out = ph.sbuf("bias_out", [P, 3, D])
        stats = [ph.sbuf(f"stats{i}", [P, QT, 6]) for i in range(2)]
        moments = [ph.sbuf(f"moments{i}", [P, QT, 4]) for i in range(2)]
        x_in = ph.sbuf("x_in", [P, QT, D])
        x_inT = ph.sbuf("x_inT", [P, QT, P])
        logits = ph.sbuf("logits", [P, QT, E])
        top = ph.sbuf("top", [P, QT])
        first = ph.sbuf("first", [P, QT])
        onehot = ph.sbuf("onehot", [P, QT, E])
        onehotT = ph.sbuf("onehotT", [E, QT, P])
        expert_rows = ph.sbuf("expert_rows", [P, QT, E, D])
        expert_rowsT = ph.sbuf("expert_rowsT", [P, QT, E, P])
        gelu = ph.sbuf("gelu", [P, QT, F])
        geluT = ph.sbuf("geluT", [P, QT, C, P])
        y = ph.sbuf("y", [P, 2, QT, D])
        yn = ph.sbuf("yn", [P, QT, D])
        small = ph.psum("small", [P, 512])
        turned_rows = ph.psum("turned_rows", [P, QT, 4, P])
        turned = ph.psum("turned", [P, QT, 4, P])
        up = ph.psum("up", [P, QT, 512])
        down = ph.psum("down", [P, 512])
        stats_done = [ph.sem(f"stats_done{i}") for i in range(2)]
        moments_done = [ph.sem(f"moments_done{i}") for i in range(2)]
        rstd_done = [ph.sem(f"rstd_done{i}") for i in range(2)]
        normed = [ph.sem(f"normed{i}") for i in range(2)]
        (router_loaded, bias_loaded, w1_loaded, wo_loaded, step, x_turned, x_copied, logits_done, logits_copied, chosen, choice_turned, choice_copied,
         rows_ready, rows_turned, rows_copied, up_done, gelu_done, gelu_turned, gelu_copied, down_done,
         y_ready, y_scaled, residual) = [ph.sem(n) for n in (
             "router_loaded", "bias_loaded", "w1_loaded", "wo_loaded", "step", "x_turned", "x_copied", "logits_done", "logits_copied", "chosen", "choice_turned",
             "choice_copied", "rows_ready", "rows_turned", "rows_copied", "up_done", "gelu_done", "gelu_turned",
             "gelu_copied", "down_done", "y_ready", "y_scaled", "residual")]
        block = ctx.enter_context(nc.Block())

        @block.sync
        def _(sp):
            sp.dma_start(router[:, :], sh.dram["L3_ffn_W_router"]).then_inc(router_loaded, 16)
            sp.dma_start(bias1[:, :], sh.dram["L3_ffn_b1"]).then_inc(w1_loaded, 16)
            for j, n in enumerate(("bo", "ln_gamma", "ln_beta")):
                sp.dma_start(bias_out[:, j, :], sh.dram["L3_ffn_" + n].rearrange("(o d) -> o d", o=1).to_broadcast([P, D])).then_inc(bias_loaded, 16)
            sp.dma_start(w1[:, :, :], sh.dram["L3_ffn_W1"].rearrange("e d f -> d e f")).then_inc(w1_loaded, 16)
            sp.dma_start(wo[:, :, :], sh.dram["L3_ffn_Wo"].rearrange("(c p) d -> p c d", p=P)).then_inc(wo_loaded, 16)

        ORDER = "F0 B0 F1 B1 F2 B2 F3 B3 B4 F4 B5"

        @block.gpsimd
        def _(pool):
            clear_retired(pool, sh)

            def front(b, par, k):
                if k == 0:
                    pool_rstd(pool, sh, moments[0], moments_done[0], rstd_done[0], b)

            def back(b, par, k):
                if k == 5:
                    pool_rstd(pool, sh, moments[1], moments_done[1], rstd_done[1], b)

            overlapped(pool, ORDER, front, back)

        @block.tensor
        def _(pe):
            pe.wait_ge(router_loaded, 16)

            def front(b, par, k):
                if k == 1:
                    pe.wait_ge(normed[0], QT * (b + 1))
                    for q in range(QT):
                        last = pe.transpose(small[:, P * q:P * (q + 1)], x_in[:, q, :], sh.ident[:, :])
                    last.then_inc(x_turned, 1)
                elif k == 2:
                    pe.wait_ge(x_copied, b + 1)
                    for q in range(QT):
                        last = pe.matmul(small[:, 2 * P + E * q:2 * P + E * (q + 1)], x_inT[:, q, :], router[:, :], start=True, stop=True)
                    last.then_inc(logits_done, 1)
                elif k == 3:
                    pe.wait_ge(logits_copied, b + 1)
                    pe.wait_ge(chosen, b + 1)
                    for q in range(QT):
                        last = pe.transpose(small[0:E, P * q:P * (q + 1)], onehot[:, q, :], sh.ident[:, :])
                    last.then_inc(choice_turned, 1)
                elif k == 4:
                    pe.wait_ge(rows_ready, b + 1)
                    for q in range(QT):
                        for e in range(E):
                            last = pe.transpose(turned_rows[:, q, e, :], expert_rows[:, q, e, :], sh.ident[:, :])
                        last.then_inc(rows_turned, 1)

            def back(b, par, k):
                if k < QT:
                    q = k
                    if not later(b):
                        pe.wait_ge(w1_loaded, 32)
                    pe.wait_ge(choice_copied, b + 1)
                    pe.wait_ge(rows_copied, QT * b + q + 1)
                    for e in range(E):
                        pe.matmul(up[:, q, :], expert_rowsT[:, q, e, :], w1[:, e, :], start=(e == 0), stop=False)
                    pe.matmul(up[:, q, :], onehotT[:, q, :], bias1[:, :], start=False, stop=True).then_inc(up_done, 1)
                elif k < 2 * QT:
                    q = k - QT
                    pe.wait_ge(gelu_done, QT * b + q + 1)
                    for c in range(C):
                        last = pe.transpose(turned[:, q, c, :], gelu[:, q, P * c:P * (c + 1)], sh.ident[:, :])
                    last.then_inc(gelu_turned, 1)
                elif k == 4:
                    if later(b):
                        pe.wait_ge(y_ready, 3 * b - 2)
                    else:
                        pe.wait_ge(wo_loaded, 16)
                    for q in range(QT):
                        pe.wait_ge(gelu_copied, QT * b + q + 1)
                        for c in range(C):
                            last = pe.matmul(down[:, D * q:D * (q + 1)], geluT[:, q, c, :], wo[:, c, :], start=(c == 0), stop=(c == C - 1))
                    last.then_inc(down_done, 1)

            overlapped(pe, ORDER, front, back)

        @block.scalar
        def _(act):
            def front(b, par, k):
                if k == 1:
                    act.wait_ge(x_turned, b + 1)
                    act.activation(x_inT[:, :, :], small[:, 0:S].rearrange("p (q t) -> p q t", q=QT), ACT.Copy).then_inc(x_copied, 1)
                elif k == 2:
                    act.wait_ge(logits_done, b + 1)
                    act.activation(logits[:, :, :], small[:, 2 * P:2 * P + QT * E].rearrange("p (q e) -> p q e", q=QT), ACT.Copy).then_inc(logits_copied, 1)
                elif k == 3:
                    act.wait_ge(choice_turned, b + 1)
                    act.activation(onehotT[:, :, :], small[0:E, 0:S].rearrange("p (q t) -> p q t", q=QT), ACT.Copy).then_inc(choice_copied, 1)
                elif k == 4:
                    for q in range(QT):
                        act.wait_ge(rows_turned, QT * b + q + 1)
                        act.activation(expert_rowsT[:, q, :, :], turned_rows[:, q, :, :], ACT.Copy).then_inc(rows_copied, 1)

            def back(b, par, k):
                if k < QT:
                    act.wait_ge(up_done, QT * b + k + 1)
                    act.activation(gelu[:, k, :], up[:, k, :], ACT.Gelu).then_inc(gelu_done, 1)
                elif k < 2 * QT:
                    q = k - QT
                    act.wait_ge(gelu_turned, QT * b + q + 1)
                    act.activation(geluT[:, q, :, :], turned[:, q, :, :], ACT.Copy).then_inc(gelu_copied, 1)

            overlapped(act, ORDER, front, back)

        @block.vector
        def _(dve):
            choice = Counter(6)

            def front(b, par, k):
                nonlocal choice
                inner = [x_in[:, q, :] for q in range(QT)]
                if k == 0:
                    if later(b):
                        dve.wait_ge(residual, b)
                        dve.wait_ge(rows_ready, b)
                    rows = [sh.x_all[:, bass.ds(b * QT + q, 1), :].rearrange("p o d -> p (o d)") for q in range(QT)]
                    dve_layernorm(dve, rows, inner, stats[0], moments[0], stats_done[0], moments_done[0], rstd_done[0], normed[0], LN_EPS, b)
                elif k == 2:
                    choice = Counter(6)
                    dve.wait_ge(logits_copied, b + 1)
                    dve_choose(dve, sh, logits[:, :, :], top, first, onehot, step, choice, b)
                    choice.close()
                    dve.sem_inc(chosen, 1)
                elif k == 3:
                    if later(b):
                        dve.wait_ge(rows_turned, QT * b)
                    for q in range(QT):
                        for e in range(E):
                            last = dve.tensor_scalar(expert_rows[:, q, e, :], x_in[:, q, :], onehot[:, q, e:e + 1], None, ALU.mult)
                    last.then_inc(rows_ready, 1)
                    if not later(b):
                        dve.wait_ge(bias_loaded, 48)
                    dve.tensor_tensor(y[:, par, :, :], x_in[:, :, :], bias_out[:, 0, :].unsqueeze(1).to_broadcast([P, QT, D]), ALU.add).then_inc(residual, 1)

            def back(b, par, k):
                now = y[:, par, :, :]
                if k == 4:
                    dve.wait_ge(down_done, b + 1)
                    dve.wait_ge(residual, b + 1)
                    dve.tensor_tensor(now, now, down[:, 0:QT * D].rearrange("p (q d) -> p q d", q=QT), ALU.add).then_inc(y_ready, 1)
                elif k == 5:
                    dve.wait_ge(y_ready, 3 * b + 1)
                    dve_layernorm(dve, [y[:, par, q, :] for q in range(QT)], [yn[:, q, :] for q in range(QT)], stats[1], moments[1],
                                  stats_done[1], moments_done[1], rstd_done[1], normed[1], LN3_EPS, b)
                    dve.wait_ge(normed[1], QT * (b + 1))
                    dve.tensor_tensor(yn[:, :, :], yn[:, :, :], bias_out[:, 1, :].unsqueeze(1).to_broadcast([P, QT, D]), ALU.mult).then_inc(y_scaled, 1)
                    dve.wait_ge(y_scaled, b + 1)
                    dve.tensor_tensor(yn[:, :, :], yn[:, :, :], bias_out[:, 2, :].unsqueeze(1).to_broadcast([P, QT, D]), ALU.add).then_inc(y_ready, 1)
                    dve.wait_ge(y_ready, 3 * b + 2)
                    out_rows = sh.x_all[:, bass.ds(b * QT, QT), :]
                    dve.tensor_tensor(out_rows, out_rows, yn[:, :, :], ALU.add).then_inc(y_ready, 1)
                    dve.wait_ge(y_ready, 3 * (b + 1))

            overlapped(dve, ORDER, front, back)
        ph.retire(sh)


INPUTS = [
    "x",
    "ctx_1024",
    "mask_BxS_bf1",
    "mask_BxS_ik0",
    "mask_BxSxS2_ff0",
    "L0_xattn_W_q",
    "L0_xattn_W_k",
    "L0_xattn_W_v",
    "L0_xattn_W_o",
    "L0_ffn_w1",
    "L0_ffn_b1",
    "L0_ffn_w2",
    "L0_ffn_b2",
    "L1_xattn_wq",
    "L1_xattn_wk",
    "L1_xattn_wv",
    "L1_xattn_wo",
    "L1_xattn_bq",
    "L1_xattn_bk",
    "L1_xattn_bv",
    "L1_xattn_bo",
    "L1_ffn_w1",
    "L1_ffn_w3",
    "L1_ffn_w2",
    "L2_xattn_ln_g",
    "L2_xattn_ln_b",
    "L2_xattn_cln_g",
    "L2_xattn_cln_b",
    "L2_xattn_Wq",
    "L2_xattn_Wkv",
    "L2_xattn_Wout",
    "L2_xattn_W1",
    "L2_xattn_W2",
    "L2_ffn_centroids",
    "L2_ffn_ln_g",
    "L2_ffn_ln_b",
    "L2_ffn_w1",
    "L2_ffn_b1",
    "L2_ffn_w2",
    "L2_ffn_b2",
    "L3_xattn_W_Q",
    "L3_xattn_W_K",
    "L3_xattn_W_V",
    "L3_xattn_W_O",
    "L3_ffn_W_router",
    "L3_ffn_W1",
    "L3_ffn_b1",
    "L3_ffn_Wo",
    "L3_ffn_bo",
    "L3_ffn_ln_gamma",
    "L3_ffn_ln_beta",
]


def build(nc, dram, out):
    with ExitStack() as ctx:
        sh = Shared(nc, ctx, dram)
        phase_setup(nc, sh)
        phase_clipped_attention(nc, sh)
        phase_ternary_ffn(nc, sh)
        phase_softmax_attention(nc, sh, False)
        phase_expert_ffn(nc, sh)
        phase_multi_query_inputs(nc, sh)
        phase_softmax_attention(nc, sh, True)
        phase_routed_ffn(nc, sh)
        phase_head_softmax_attention(nc, sh)
        phase_hard_expert_ffn(nc, sh)
        with ExitStack() as end:
            stored = end.enter_context(nc.semaphore("stored"))
            block = end.enter_context(nc.Block())

            @block.sync
            def _(sp):
                sp.dma_start(out.rearrange("b (q p) d -> p (b q) d", p=P), sh.x_all[:, :, :]).then_inc(stored, 16)
                sp.wait_ge(stored, 16)


def kernel(**inputs):
    import numpy as np
    import concourse.bacc as bacc
    from concourse.bass_utils import run_bass_kernel_spmd

    nc = bacc.Bacc("TRN2", target_bir_lowering=False, num_devices=1)
    arrays, dram = {}, {}
    for name in INPUTS:
        a = np.ascontiguousarray(inputs[name])
        if a.dtype == np.bool_:
            a = a.view(np.uint8)
        arrays["in_" + name] = a
        dram[name] = nc.dram_tensor("in_" + name, a.shape, mybir.dt.from_np(a.dtype), kind="ExternalInput").ap()
    shape = (NB, S, D)
    out = nc.dram_tensor("out", shape, F32, kind="ExternalOutput").ap()
    build(nc, dram, out)
    return run_bass_kernel_spmd(nc, [arrays], core_ids=[0]).results[0]["out"]
```
